# Optimizing a Trainium2 kernel written in Bass

```python
import numpy as np
import jax
import jax.numpy as jnp

def _softmax(x, axis=-1):
    return jax.nn.softmax(x, axis=axis)

def _gelu(x):
    return jax.nn.gelu(x, approximate=True)

def _silu(x):
    return jax.nn.silu(x)

def _sigmoid(x):
    return jax.nn.sigmoid(x)

def _layernorm(x, axis=-1, eps=1e-05):
    m = jnp.mean(x, axis=axis, keepdims=True)
    v = jnp.var(x, axis=axis, keepdims=True)
    return (x - m) / jnp.sqrt(v + eps)

def _scatter_add(tgt, idx, src, axis=0):
    return tgt.at[idx].add(src)

def _segment_sum(src, seg, n):
    return jax.ops.segment_sum(src, seg, n)
kernel_name = 'mk_gnn_resnorm_d4_gnn_r32_5f2494'

def setup_inputs(seed: int=0):
    np.random.seed(seed)
    _w = jnp.asarray

    def _rec_inputs():
        import jax
        import jax.numpy as jnp
        _gk = jax.random.key(seed)
        x = -0.0009044 + 1 * jax.random.normal(jax.random.fold_in(_gk, 1), (3125, 32), jnp.float32)
        src = jax.random.randint(jax.random.fold_in(_gk, 2), (50000,), 0, 3125, jnp.int32)
        dst = jnp.minimum((3125 * jax.random.uniform(jax.random.fold_in(_gk, 3), (50000,)) ** 2.0).astype(jnp.int32), 99999)
        _o = jnp.argsort(dst, stable=True)
        src = src[_o]
        dst = dst[_o]
        edge_attr_16 = 0.000196303 + 1.00016 * jax.random.normal(jax.random.fold_in(_gk, 12), (50000, 16), jnp.float32)
        edge_attr_4 = 0.00086875 + 0.999764 * jax.random.normal(jax.random.fold_in(_gk, 13), (50000, 4), jnp.float32)
        edge_attr_8 = jax.random.uniform(jax.random.fold_in(_gk, 14), (50000, 8), jnp.float32, 0.0, 1)
        edge_weight = jax.random.uniform(jax.random.fold_in(_gk, 16), (50000,), jnp.float32, 0.0, 1)
        return (x, src, dst, edge_attr_16, edge_attr_4, edge_attr_8, edge_weight)
    x, src, dst, edge_attr_16, edge_attr_4, edge_attr_8, edge_weight = _rec_inputs()

    def _L0_gnn_setup():
        import jax, jax.numpy as jnp
        import numpy as np
        N_NODES = 50000
        N_EDGES = 50000
        D_NODE = 32
        D_EDGE = 16
        H = 64
        F_OUT = 32
        N_OUT = 32

        def _mlp_params(key, d_in, d_h, d_out):
            k1, k2 = jax.random.split(key)
            s1 = 1.0 / np.sqrt(d_in)
            s2 = 1.0 / np.sqrt(d_h)
            return (jax.random.uniform(k1, (d_in, d_h), jnp.float32, -s1, s1), jnp.zeros((d_h,), jnp.float32), jax.random.uniform(k2, (d_h, d_out), jnp.float32, -s2, s2), jnp.zeros((d_out,), jnp.float32))

        def _mlp(h, W1, b1, W2, b2):
            return jax.nn.relu(jax.nn.relu(h @ W1 + b1) @ W2 + b2)
        key = jax.random.key(seed)
        kx, ke, ka, kf, kb, kn = jax.random.split(key, 6)
        x = jax.random.normal(kx, (N_NODES, D_NODE), jnp.float32)
        edge_index = jax.random.randint(ke, (2, N_EDGES), 0, N_NODES, jnp.int64)
        edge_attr = jax.random.normal(ka, (N_EDGES, D_EDGE), jnp.float32)
        d_flow_in = 2 * D_NODE + D_EDGE
        W1f, b1f, W2f, b2f = _mlp_params(kf, d_flow_in, H, F_OUT)
        W1b, b1b, W2b, b2b = _mlp_params(kb, d_flow_in, H, F_OUT)
        W1n, b1n, W2n, b2n = _mlp_params(kn, 2 * F_OUT, H, N_OUT)
        return dict(x=x, edge_index=edge_index, edge_attr=edge_attr, W1f=W1f, b1f=b1f, W2f=W2f, b2f=b2f, W1b=W1b, b1b=b1b, W2b=W2b, b2b=b2b, W1n=W1n, b1n=b1n, W2n=W2n, b2n=b2n)
    _L0_gnn_all = _L0_gnn_setup()
    _L0_gnn_in = {k: v for k, v in _L0_gnn_all.items() if k in ('W1f', 'b1f', 'W2f', 'b2f', 'W1b', 'b1b', 'W2b', 'b2b', 'W1n', 'b1n', 'W2n', 'b2n')}
    del _L0_gnn_all

    def _L1_gnn_setup():
        import jax, jax.numpy as jnp
        import numpy as np
        N = 1024
        E = 16384
        MUL = 8
        NB = 8
        HR = 64
        NTP = 4 * MUL * MUL
        AVG_NEI = 16.0
        INV_SQRT3 = 1.0 / np.sqrt(3.0)
        ALPHA = 1.0 / np.sqrt(2.0 * MUL)
        key = jax.random.key(seed)
        ks = jax.random.split(key, 12)
        h = jax.random.normal(ks[0], (N, 4 * MUL), jnp.float32)
        edge_index = jax.random.randint(ks[1], (2, E), 0, N)
        edge_sh = jax.random.normal(ks[2], (E, 4), jnp.float32)
        edge_radial = jax.random.uniform(ks[3], (E, NB), jnp.float32)

        def lin(k, fi, fo):
            return (jax.random.normal(k, (fi, fo), jnp.float32) / np.sqrt(fi)).astype(jnp.float32)
        W1 = lin(ks[4], NB, HR)
        b1 = jnp.zeros((HR,), jnp.float32)
        W2 = lin(ks[5], HR, HR)
        b2 = jnp.zeros((HR,), jnp.float32)
        W3 = lin(ks[6], HR, NTP)
        b3 = jnp.zeros((NTP,), jnp.float32)
        Ws = jax.random.normal(ks[7], (MUL, MUL), jnp.float32)
        Wv = jax.random.normal(ks[8], (MUL, MUL), jnp.float32)
        return dict(h=h, edge_index=edge_index, edge_sh=edge_sh, edge_radial=edge_radial, n_atoms=N, W1=W1, b1=b1, W2=W2, b2=b2, W3=W3, b3=b3, Ws=Ws, Wv=Wv)
    _L1_gnn_all = _L1_gnn_setup()
    _L1_gnn_in = {k: v for k, v in _L1_gnn_all.items() if k in ('W1', 'b1', 'W2', 'b2', 'W3', 'b3', 'Ws', 'Wv')}
    del _L1_gnn_all

    def _L2_gnn_setup():
        import jax, jax.numpy as jnp
        import numpy as np
        ALPHA = 0.1
        K = 10
        key = jax.random.key(seed)
        k1, k2, k3 = jax.random.split(key, 3)
        N, E, D = (3125, 50000, 32)
        feat = jax.random.normal(k1, (N, D), dtype=jnp.float32)
        src = jax.random.randint(k2, (E,), 0, N)
        dst = jax.random.randint(k3, (E,), 0, N)
        return {'feat': feat, 'src': src, 'dst': dst}
    _L2_gnn_all = _L2_gnn_setup()
    _L2_gnn_in = {k: v for k, v in _L2_gnn_all.items() if k in ()}
    del _L2_gnn_all

    def _L3_gnn_setup():
        import jax, jax.numpy as jnp
        import numpy as np
        N_NODES = 3125
        N_EDGES = 50000
        EMB_DIM = 32
        NUM_LAYERS = 3
        key = jax.random.key(seed)
        k_emb, k_w, k_row, k_col = jax.random.split(key, 4)
        emb = jax.random.normal(k_emb, (N_NODES, EMB_DIM), dtype=jnp.float32)
        edge_weight = jax.random.uniform(k_w, (N_EDGES,), dtype=jnp.float32)
        row = jax.random.randint(k_row, (N_EDGES,), 0, N_NODES, dtype=jnp.int32)
        col = jax.random.randint(k_col, (N_EDGES,), 0, N_NODES, dtype=jnp.int32)
        return {'emb': emb, 'edge_weight': edge_weight, 'row': row, 'col': col, 'num_layers': NUM_LAYERS}
    _L3_gnn_all = _L3_gnn_setup()
    _L3_gnn_in = {k: v for k, v in _L3_gnn_all.items() if k in ()}
    del _L3_gnn_all
    return {'x': x, 'src': src, 'dst': dst, 'edge_attr_16': edge_attr_16, 'edge_attr_4': edge_attr_4, 'edge_attr_8': edge_attr_8, 'edge_weight': edge_weight, 'L0_gnn_W1f': _L0_gnn_in['W1f'], 'L0_gnn_b1f': _L0_gnn_in['b1f'], 'L0_gnn_W2f': _L0_gnn_in['W2f'], 'L0_gnn_b2f': _L0_gnn_in['b2f'], 'L0_gnn_W1b': _L0_gnn_in['W1b'], 'L0_gnn_b1b': _L0_gnn_in['b1b'], 'L0_gnn_W2b': _L0_gnn_in['W2b'], 'L0_gnn_b2b': _L0_gnn_in['b2b'], 'L0_gnn_W1n': _L0_gnn_in['W1n'], 'L0_gnn_b1n': _L0_gnn_in['b1n'], 'L0_gnn_W2n': _L0_gnn_in['W2n'], 'L0_gnn_b2n': _L0_gnn_in['b2n'], 'L1_gnn_W1': _L1_gnn_in['W1'], 'L1_gnn_b1': _L1_gnn_in['b1'], 'L1_gnn_W2': _L1_gnn_in['W2'], 'L1_gnn_b2': _L1_gnn_in['b2'], 'L1_gnn_W3': _L1_gnn_in['W3'], 'L1_gnn_b3': _L1_gnn_in['b3'], 'L1_gnn_Ws': _L1_gnn_in['Ws'], 'L1_gnn_Wv': _L1_gnn_in['Wv']}

def reference(x, src, dst, edge_attr_16, edge_attr_4, edge_attr_8, edge_weight, L0_gnn_W1f, L0_gnn_b1f, L0_gnn_W2f, L0_gnn_b2f, L0_gnn_W1b, L0_gnn_b1b, L0_gnn_W2b, L0_gnn_b2b, L0_gnn_W1n, L0_gnn_b1n, L0_gnn_W2n, L0_gnn_b2n, L1_gnn_W1, L1_gnn_b1, L1_gnn_W2, L1_gnn_b2, L1_gnn_W3, L1_gnn_b3, L1_gnn_Ws, L1_gnn_Wv):
    import jax
    import jax.numpy as jnp

    def _L0_gnn_ref(x, edge_index, edge_attr, W1f, b1f, W2f, b2f, W1b, b1b, W2b, b2b, W1n, b1n, W2n, b2n):
        import jax, jax.numpy as jnp
        import numpy as np
        N_NODES = 50000
        N_EDGES = 50000
        D_NODE = 32
        D_EDGE = 16
        H = 64
        F_OUT = 32
        N_OUT = 32

        def _mlp_params(key, d_in, d_h, d_out):
            k1, k2 = jax.random.split(key)
            s1 = 1.0 / np.sqrt(d_in)
            s2 = 1.0 / np.sqrt(d_h)
            return (jax.random.uniform(k1, (d_in, d_h), jnp.float32, -s1, s1), jnp.zeros((d_h,), jnp.float32), jax.random.uniform(k2, (d_h, d_out), jnp.float32, -s2, s2), jnp.zeros((d_out,), jnp.float32))

        def _mlp(h, W1, b1, W2, b2):
            return jax.nn.relu(jax.nn.relu(h @ W1 + b1) @ W2 + b2)
        past, future = (edge_index[0], edge_index[1])
        x_past = x[past]
        x_future = x[future]
        fwd_in = jnp.concatenate([x_future, x_past, edge_attr], axis=1)
        flow_fwd = _mlp(fwd_in, W1f, b1f, W2f, b2f)
        fwd_agg = jax.ops.segment_sum(flow_fwd, future, num_segments=x.shape[0])
        bwd_in = jnp.concatenate([x_past, x_future, edge_attr], axis=1)
        flow_bwd = _mlp(bwd_in, W1b, b1b, W2b, b2b)
        bwd_agg = jax.ops.segment_sum(flow_bwd, past, num_segments=x.shape[0])
        flow_total = jnp.concatenate([fwd_agg, bwd_agg], axis=1)
        return _mlp(flow_total, W1n, b1n, W2n, b2n)

    def _L1_gnn_ref(h, edge_index, edge_sh, edge_radial, n_atoms, W1, b1, W2, b2, W3, b3, Ws, Wv):
        import jax, jax.numpy as jnp
        import numpy as np
        N = 1024
        E = 16384
        MUL = 8
        NB = 8
        HR = 64
        NTP = 4 * MUL * MUL
        AVG_NEI = 16.0
        INV_SQRT3 = 1.0 / np.sqrt(3.0)
        ALPHA = 1.0 / np.sqrt(2.0 * MUL)
        src, dst = (edge_index[0], edge_index[1])
        x = jax.nn.silu(edge_radial @ W1 + b1)
        x = jax.nn.silu(x @ W2 + b2)
        tpw = x @ W3 + b3
        P = MUL * MUL
        W00 = tpw[:, 0 * P:1 * P].reshape(-1, MUL, MUL)
        W110 = tpw[:, 1 * P:2 * P].reshape(-1, MUL, MUL)
        W01 = tpw[:, 2 * P:3 * P].reshape(-1, MUL, MUL)
        W10 = tpw[:, 3 * P:4 * P].reshape(-1, MUL, MUL)
        hs = h[:, :MUL]
        hv = h[:, MUL:].reshape(-1, MUL, 3)
        hs_e = hs[src]
        hv_e = hv[src]
        sh0 = edge_sh[:, 0]
        sh1 = edge_sh[:, 1:4]
        m0 = ALPHA * (jnp.einsum('eu,euw->ew', hs_e * sh0[:, None], W00) + INV_SQRT3 * jnp.einsum('eui,ei,euw->ew', hv_e, sh1, W110))
        m1 = ALPHA * (jnp.einsum('eu,ei,euw->ewi', hs_e, sh1, W01) + jnp.einsum('eui,euw->ewi', hv_e * sh0[:, None, None], W10))
        messages = jnp.concatenate([m0, m1.reshape(-1, 3 * MUL)], axis=-1)
        agg = jax.ops.segment_sum(messages, dst, num_segments=n_atoms) / np.sqrt(AVG_NEI)
        self0 = hs @ Ws / np.sqrt(MUL)
        self1 = jnp.einsum('nui,uw->nwi', hv, Wv) / np.sqrt(MUL)
        h_self = jnp.concatenate([self0, self1.reshape(-1, 3 * MUL)], axis=-1)
        return h_self + agg

    def _L2_gnn_ref(feat, src, dst):
        import jax, jax.numpy as jnp
        import numpy as np
        ALPHA = 0.1
        K = 10
        N = feat.shape[0]
        deg = jax.ops.segment_sum(jnp.ones_like(dst, dtype=feat.dtype), dst, num_segments=N)
        norm = jnp.where(deg > 0, deg ** (-0.5), 0.0)[:, None]
        feat_0 = feat

        def step(h, _):
            h = h * norm
            h = jax.ops.segment_sum(h[src], dst, num_segments=N)
            h = h * norm
            h = (1.0 - ALPHA) * h + ALPHA * feat_0
            return (h, None)
        h, _ = jax.lax.scan(step, feat, None, length=K)
        return h

    def _L3_gnn_ref(emb, edge_weight, row, col, num_layers):
        import jax, jax.numpy as jnp
        import numpy as np
        N_NODES = 3125
        N_EDGES = 50000
        EMB_DIM = 32
        NUM_LAYERS = 3
        n = emb.shape[0]
        w = edge_weight[:, None]
        X = emb
        for _ in range(num_layers):
            msgs = w * X[col]
            X = jax.ops.segment_sum(msgs, row, num_segments=n)
        return X
    edge_index = jnp.stack([src, dst])
    x = _layernorm(x + _L0_gnn_ref(x, edge_index, edge_attr_16, L0_gnn_W1f, L0_gnn_b1f, L0_gnn_W2f, L0_gnn_b2f, L0_gnn_W1b, L0_gnn_b1b, L0_gnn_W2b, L0_gnn_b2b, L0_gnn_W1n, L0_gnn_b1n, L0_gnn_W2n, L0_gnn_b2n), axis=-1)
    x = _layernorm(x + _L1_gnn_ref(x, edge_index, edge_attr_4, edge_attr_8, 3125, L1_gnn_W1, L1_gnn_b1, L1_gnn_W2, L1_gnn_b2, L1_gnn_W3, L1_gnn_b3, L1_gnn_Ws, L1_gnn_Wv), axis=-1)
    x = _layernorm(x + _L2_gnn_ref(x, src, dst), axis=-1)
    x = _layernorm(x + _L3_gnn_ref(x, edge_weight, src, dst, 3), axis=-1)
    return x

_drawn_inputs = setup_inputs


def setup_inputs(seed=0):
    import zlib

    import numpy as np

    out = dict(_drawn_inputs(seed))
    spreads = {'L0_gnn_b1f': (0.0, 0.322),
     'L0_gnn_b2f': (0.0, 0.1),
     'L0_gnn_b1b': (0.0, 0.398),
     'L0_gnn_b2b': (0.0, 0.1),
     'L0_gnn_b1n': (0.0, 0.43),
     'L0_gnn_b2n': (0.0, 0.1),
     'L1_gnn_b1': (0.0, 0.8),
     'L1_gnn_b2': (0.0, 2.0),
     'L1_gnn_b3': (0.0, 2.0)}
    factors = {'edge_attr_16': 8.0,
     'edge_attr_4': 3.23,
     'edge_attr_8': 6.524,
     'L1_gnn_W1': 4.301,
     'L1_gnn_W2': 3.885,
     'L1_gnn_W3': 3.39}
    for name, (base, spread) in spreads.items():
        noise = np.random.default_rng([zlib.crc32(name.encode()), seed]).standard_normal(out[name].shape)
        drawn = base * np.exp(spread * noise) if base else spread * noise
        out[name] = jnp.asarray(drawn.astype(out[name].dtype))
    for name, factor in factors.items():
        out[name] = (out[name] * factor).astype(out[name].dtype)
    return out
```

```python
import concourse.bass as bass
from concourse import mybir
from contextlib import ExitStack

F32 = mybir.dt.float32
BF16 = mybir.dt.bfloat16
F16 = mybir.dt.float16
I32 = mybir.dt.int32
ALU = mybir.AluOpType
ACT = mybir.ActivationFunctionType
AX = mybir.AxisListType

P = 128
N = 3125
E = 50000
D = 32
NB = -(-N // P)
NP = NB * P
LAST = N - (NB - 1) * P
EP = 125
EC = E // EP
J = 4
Q = EC // J
S = 32
G = 4
TB = 2 * G
TILES = E // P + NB * NB
BODIES = -(-TILES // TB) + NB + 1
ROWS = BODIES * TB * P
REC = 32
C16, C8, C4, CW, CR, CSRC, CDST = 0, 16, 24, 28, 29, 30, 31
TAB = 12
TSRC, TNEW = TB, TB + 2
BIG = 1.0e9
H1 = 64


def sort_phase(nc, io, dram, sort_consts):
    used = []
    ctx = ExitStack()
    with ctx:
        def sb(name, shape, dt):
            return ctx.enter_context(nc.sbuf_tensor("s_" + name, shape, dt))

        def ps(name, shape, dt=F32):
            return ctx.enter_context(nc.psum_tensor("s_" + name, shape, dt))

        def sem(name):
            used.append(ctx.enter_context(nc.semaphore("s_" + name)))
            return used[-1]

        cst = sb("cst", [P, 6, P], F32)
        IDENT, IOTA, LOWER, SAME, EARLIER, BEFORE = range(6)
        iota_t = sb("iota_t", [P, BODIES * TB], F32)
        ident16 = sb("ident16", [P, P], F16)
        ones = sb("ones", [P, 1], F32)
        onesq = sb("onesq", [P, Q], F32)
        src_i = sb("src_i", [EP, EC], I32)
        dst_i = sb("dst_i", [EP, EC], I32)
        blk_i = sb("blk_i", [EP, 2, EC], I32)
        blk = sb("blk", [EP, 2, EC], F32)
        loc_i = sb("loc_i", [EP, 2, EC], I32)
        loc = sb("loc", [EP, 2, EC], F32)
        key = sb("key", [EP, EC], F32)
        key16 = sb("key16", [EP, EC], F16)
        keyT = sb("keyT", [Q, J, EP], F16)
        ea16 = sb("ea16", [EP, EC, 16], F32)
        ea8 = sb("ea8", [EP, EC, 8], F32)
        ea4 = sb("ea4", [EP, EC, 4], F32)
        w = sb("w", [EP, EC], F32)
        w_hi = sb("w_hi", [EP, EC], BF16)
        w_rest = sb("w_rest", [EP, EC], F32)
        oh_src = sb("oh_src", [EP, Q, J, S], F16)
        oh_dst = sb("oh_dst", [EP, Q, J, NB], F16)
        hist = sb("hist", [P, Q, NB], F32)
        cum = sb("cum", [P, Q, NB], F32)
        cum_i = hist[:, :, :].bitcast(I32)
        part_i = [cum[:, :, :].bitcast(I32), cum_i]
        lookup = sb("lookup", [P, Q, 2, J, NB], F16)
        small = sb("small", [P, 12, NB], F32)
        small_i = sb("small_i", [P, 3, NB], I32)
        col = sb("col", [P, 8], F32)
        col_i = sb("col_i", [P, 2], I32)
        starts4 = sb("starts4", [P, 7], F32)
        count_t = hist[:, :, :].rearrange("p q d -> p (q d)")[:, 0:2 * BODIES * TB].rearrange("p (a t) -> p a t", a=2)
        count_b = sb("count_b", [P, BODIES], F32)
        tabrow = cum[0:1, :, :].rearrange("p q d -> p (q d)")[:, 0:BODIES * TAB].rearrange("p (b t) -> p b t", t=TAB)
        tabrow_i = sb("tabrow_i", [1, BODIES, TAB], I32)
        bst_i = sb("bst_i", [1, S], I32)
        first = sb("first", [1, 16], F32)
        neg = sb("neg", [P, TB * REC], F32)
        rank = sb("rank", [EP, Q, J], F32)
        junk = sb("junk", [EP, J, EP], BF16)
        ohT = sb("ohT", [P, 4, EP], F16)
        prod = sb("prod", [EP, 2, 2, J * NB], F32)
        sel = sb("sel", [EP, 4, 2, J], F32)
        pos = sb("pos", [EP, 4, J], F32)
        pos_i = sb("pos_i", [EP, 5, 4 * J], I32)
        index = [sb(f"index{s}", [EP, 2 * J], I32) for s in range(2)]
        record = [sb(f"record{s}", [EP, 2 * J, REC], F32) for s in range(2)]

        p_rows = [ps(f"p_rows{i}", [P, J * EP]) for i in range(2)]
        p_t = ps("p_t", [P, 2, P], F16)
        p_h = [ps(f"p_h{i}", [P, 5, J, NB]) for i in range(2)]
        p_sm = ps("p_sm", [P, 512])

        s_idx, s_cst, s_att, s_neg = sem("s_idx"), sem("s_cst"), sem("s_att"), sem("s_neg")
        s_keyT = sem("s_keyT"); s_keyTs = sem("s_keyTs"); s_id16 = sem("s_id16"); s_key = sem("s_key")
        s_rows = sem("s_rows"); s_ranked = sem("s_ranked")
        s_oh = sem("s_oh"); s_hist = sem("s_hist"); s_histed = sem("s_histed")
        s_tot = sem("s_tot"); s_totp = sem("s_totp")
        s_ready = sem("s_ready"); s_cnt = sem("s_cnt"); s_cntp = sem("s_cntp"); s_tab = sem("s_tab")
        s_bst = sem("s_bst"); s_out = sem("s_out"); s_negset = sem("s_negset")
        s_tr = sem("s_tr"); s_trc = sem("s_trc"); s_look = sem("s_look"); s_sel = sem("s_sel")
        s_index = [sem(f"s_index{s}") for s in range(2)]
        s_record = [sem(f"s_record{s}") for s in range(2)]
        s_sent = dram["sent"]
        s_free = [sem(f"s_free{s}") for s in range(2)]
        s_v = sem("s_v"); s_loc = sem("s_loc"); s_w = sem("s_w"); s_go = sem("s_go")
        block = ctx.enter_context(nc.Block())

        @block.sync
        def _(sp):
            sp.dma_start(src_i[:, :], io["src"].rearrange("(p c) -> p c", p=EP)).then_inc(s_idx, 16)
            sp.dma_start(cst[:, :, :], sort_consts).then_inc(s_cst, 16)
            sp.dma_start(iota_t[:, :], io["iota_t"]).then_inc(s_cst, 16)
            sp.dma_start(ea16[:, :, :], io["edge_attr_16"].rearrange("(p c) f -> p c f", p=EP)).then_inc(s_att, 16)
            sp.wait_ge(s_negset, 1)
            span = ROWS * REC // P
            sp.dma_start(dram["edges"].rearrange("(p r) c -> p (r c)", p=P).rearrange("p (k m) -> p k m", m=TB * REC),
                         neg[:, :].unsqueeze(1).to_broadcast([P, span // (TB * REC), TB * REC])).then_inc(s_neg, 16)
            sp.wait_ge(s_tab, 1)
            sp.dma_start(dram["table"].unsqueeze(0), tabrow_i[:, :, :]).then_inc(s_out, 16)
            sp.dma_start(dram["starts"].unsqueeze(0), bst_i[:, :]).then_inc(s_out, 16)
            sp.wait_ge(s_out, 32)

        @block.scalar
        def _(act):
            act.dma_start(dst_i[:, :], io["dst"].rearrange("(p c) -> p c", p=EP)).then_inc(s_idx, 16)
            act.dma_start(w[:, :], io["edge_weight"].rearrange("(p c) -> p c", p=EP)).then_inc(s_att, 16)
            act.dma_start(ea8[:, :, :], io["edge_attr_8"].rearrange("(p c) f -> p c f", p=EP)).then_inc(s_att, 16)
            act.dma_start(ea4[:, :, :], io["edge_attr_4"].rearrange("(p c) f -> p c f", p=EP)).then_inc(s_att, 16)
            act.wait_ge(s_keyT, 1)
            nc.scalar.copy(keyT[:, 0:2, :], p_t[0:Q, 0:2, 0:EP]).then_inc(s_keyTs, 1)
            act.wait_ge(s_keyT, 2)
            nc.scalar.copy(keyT[:, 2:4, :], p_t[0:Q, 0:2, 0:EP]).then_inc(s_keyTs, 1)
            act.wait_ge(s_att, 64)
            act.wait_ge(s_loc, 1)
            act.wait_ge(s_w, 1)
            with act.Fori(1, Q // 4 + 1) as n:
                act.wait_ge(s_trc, n)
                for h in range(2):
                    act.wait_ge(s_tr, 2 * n - 1 + h)
                    nc.scalar.copy(ohT[:, 2 * h:2 * h + 2, :], p_t[:, :, 0:EP]).then_inc(s_ready, 1)
                c0 = (n - 1) * 4 * J
                for s in range(2):
                    act.wait_ge(s_free[s], n + s)
                    c = c0 + s * 2 * J
                    k = bass.ds(c, 2 * J)
                    nc.scalar.copy(record[s][:, :, C16:C16 + 16], ea16[:, k, :])
                    nc.scalar.copy(record[s][:, :, C8:C8 + 8], ea8[:, k, :])
                    nc.scalar.copy(record[s][:, :, C4:C4 + 4], ea4[:, k, :])
                    nc.scalar.copy(record[s][:, :, CW], w[:, k])
                    nc.scalar.copy(record[s][:, :, CR], w_rest[:, k])
                    nc.scalar.copy(record[s][:, :, CSRC:CDST + 1].rearrange("p c k -> p k c"),
                                   loc[:, :, k]).then_inc(s_record[s], 1)

        @block.gpsimd
        def _(pool):
            nc.gpsimd.memset(neg[:, :], -1.0).then_inc(s_negset, 1)
            nc.gpsimd.memset(lookup[:, :, :, :, :], 0.0).then_inc(s_negset, 1)
            for s in range(2):
                pool.sem_inc(s_free[s], 1)
            pool.dma_start(first[:, :], io["iota_t"][0:1, 0:16]).then_inc(s_sent[1], 16)
            pool.wait_ge(s_neg, 16)
            with pool.Fori(1, Q // 4 + 1) as n:
                for s in range(2):
                    pool.wait_ge(s_index[s], n)
                    pool.wait_ge(s_record[s], n)
                    pool.sem_inc(s_go, 1)
                    for c in range(2 * J):
                        pool.indirect_dma_start(dram["edges"], bass.IndirectOffsetOnAxis(ap=index[s][:, c:c + 1], axis=0),
                                                record[s][:, c, :], None).then_inc(s_sent[s], 16)
                    pool.wait_ge(s_sent[1 - s], n * (2 * J * 16) if s else (n - 1) * (2 * J * 16) + 16)
                    pool.sem_inc(s_free[1 - s], 1)
            pool.wait_ge(s_sent[1], (Q // 4) * (2 * J * 16) + 16)

        @block.tensor
        def _(pe):
            pe.wait_ge(s_key, 1)
            pe.wait_ge(s_id16, 1)
            kv = key16[:, :].rearrange("p (q j) -> p j q", j=J)
            for h in range(2):
                if h:
                    pe.wait_ge(s_keyTs, 1)
                for j in range(2):
                    t = nc.tensor.transpose(p_t[0:Q, j, 0:EP], kv[:, 2 * h + j, :], ident16[0:EP, 0:EP])
                t.then_inc(s_keyT, 1)
            pe.wait_ge(s_keyTs, 2)
            pe.wait_ge(s_oh, 1)
            with pe.Fori(1, Q // 10 + 1) as n:
                for h in range(2):
                    pe.wait_ge(s_histed, 2 * n - 1 + h)
                    for k in range(5):
                        q = (n - 1) * 10 + h * 5 + k
                        m = nc.tensor.matmul(p_h[h][:, k, :, :], oh_src[:, bass.ds(q, 1), :, :], oh_dst[:, bass.ds(q, 1), :, :],
                                             start=(k == 0), stop=(k == 4), skip_group_check=True)
                    m.then_inc(s_hist, 1)
            pe.wait_ge(s_tot, 1)
            nc.tensor.matmul(p_sm[:, 0:NB], cst[:, SAME, :], small[:, 0, :], start=True, stop=True).then_inc(s_totp, 1)
            nc.tensor.matmul(p_sm[:, 32:32 + NB], cst[:, EARLIER, :], small[:, 0, :], start=True, stop=True).then_inc(s_totp, 1)
            pe.wait_ge(s_tot, 2)
            nc.tensor.matmul(p_sm[:, 64:65], cst[:, BEFORE, :], col[:, 1:2], start=True, stop=True).then_inc(s_totp, 1)
            with pe.Fori(1, Q // 2 + 1) as n:
                for h in range(2):
                    pe.wait_ge(s_ranked, 2 * n - 1 + h)
                    k = (n - 1) * 2 + h
                    nc.tensor.matmul(p_rows[h][0:EP, :], ident16[0:Q, bass.ds(k, 1)].to_broadcast([Q, EP]), keyT[:, :, :],
                                     start=True, stop=True).then_inc(s_rows, 1)
            pe.wait_ge(s_cnt, 1)
            pe.sem_inc(s_ready, 2)
            pe.sem_inc(s_trc, 1)
            with pe.Fori(1, Q // 4 + 1) as n:
                for h in range(2):
                    pe.wait_ge(s_ready, 2 * n + h)
                    for k in range(2):
                        q = (n - 1) * 4 + 2 * h + k
                        m = nc.tensor.transpose(p_t[:, k, 0:EP], oh_src[:, bass.ds(q, 1), :, :], ident16[0:EP, 0:EP])
                    m.then_inc(s_tr, 1)
                pe.wait_ge(s_ready, 2 * n + 2)
                for h in range(2):
                    pe.wait_ge(s_sel, 2 * n - 1 + h)
                    for k in range(2):
                        q = (n - 1) * 4 + 2 * h + k
                        m = nc.tensor.matmul(p_h[h][0:EP, 0:4, :, :].rearrange("p a j d -> p (a j d)")[:, k * 2 * J * NB:(k + 1) * 2 * J * NB],
                                             ohT[:, 2 * h + k, :], lookup[:, bass.ds(q, 1), :, :, :],
                                             start=(k == 0), stop=(k == 1), skip_group_check=True)
                    m.then_inc(s_look, 1)
                pe.sem_inc(s_trc, 1)
            pe.wait_ge(s_bst, 1)
            nc.tensor.matmul(p_sm[0:1, 128:128 + BODIES], ones[0:NB, :], count_b[0:NB, :], start=True, stop=True).then_inc(s_cntp, 1)
            for k in range(3):
                a, b = k * 56, min(BODIES, (k + 1) * 56)
                bank = (p_rows[0], p_rows[1], p_h[0])[k]
                flat = bank[:, :] if k < 2 else bank[:, :, :, :].rearrange("p a j d -> p (a j d)")
                m = nc.tensor.matmul(flat[0:1, 0:(b - a) * TB], ones[:, :], count_t[:, 0, a * TB:b * TB], start=True, stop=True)
                if k < 2:
                    m.then_inc(s_cntp, 1)
            nc.tensor.matmul(p_sm[0:1, 320:320 + S], col[0:S, 4:5], cst[0:S, IDENT, 0:S], start=True, stop=True).then_inc(s_cntp, 1)

        @block.vector
        def _(dve):
            chain = [0]

            def link(ins):
                chain[0] += 1
                ins.then_inc(s_v, 1)
                dve.wait_ge(s_v, chain[0])

            V = nc.vector
            dve.wait_ge(s_idx, 32)
            for k, ids in enumerate((src_i, dst_i)):
                V.tensor_scalar(blk_i[:, k, :], ids[:, :], 7, None, ALU.arith_shift_right)
                link(V.tensor_scalar(loc_i[:, k, :], ids[:, :], P - 1, None, ALU.bitwise_and))
            V.tensor_copy(loc[:, :, :], loc_i[:, :, :]).then_inc(s_loc, 1)
            link(V.tensor_copy(blk[:, :, :], blk_i[:, :, :]))
            link(V.scalar_tensor_tensor(key[:, :], blk[:, 0, :], float(S), blk[:, 1, :], ALU.mult, ALU.add))
            V.tensor_copy(key16[:, :], key[:, :]).then_inc(s_key, 1)
            dve.wait_ge(s_cst, 32)
            V.memset(ones[:, :], 1.0)
            V.memset(onesq[:, :], 1.0)
            V.tensor_copy(ident16[:, :], cst[:, IDENT, :]).then_inc(s_id16, 1)
            for k, (o, n) in enumerate(((oh_src, S), (oh_dst, NB))):
                i = V.tensor_tensor(o[:, :, :, :].rearrange("p q j s -> p (q j) s"),
                                    cst[0:EP, IOTA, 0:n].unsqueeze(1).to_broadcast([EP, EC, n]),
                                    blk[:, k, :].unsqueeze(2).to_broadcast([EP, EC, n]), ALU.is_equal)
            i.then_inc(s_oh, 1)
            dve.wait_ge(s_att, 64)
            link(V.tensor_copy(w_hi[:, :], w[:, :]))
            V.tensor_tensor(w_rest[:, :], w[:, :], w_hi[:, :], ALU.subtract).then_inc(s_w, 1)
            dve.sem_inc(s_histed, 2)
            with dve.Fori(1, Q // 10 + 1) as n:
                for h in range(2):
                    dve.wait_ge(s_hist, 2 * n - 1 + h)
                    for j in range(J):
                        i = V.tensor_copy(hist[S * j:S * j + S, bass.ds((n - 1) * 10 + 5 * h, 5), :], p_h[h][S * j:S * j + S, :, j, :])
                    i.then_inc(s_histed, 1)
            dve.wait_ge(s_histed, 2 * (Q // 10) + 2)
            TOT, NT, PRE, ST, B0 = 0, 1, 2, 3, 4
            V.tensor_reduce(small[:, TOT, :], hist[:, :, :].rearrange("p q d -> p d q"), AX.X, ALU.add).then_inc(s_tot, 1)
            dve.wait_ge(s_totp, 2)
            link(V.tensor_scalar(small[:, 5, :], p_sm[:, 0:NB], float(P - 1), None, ALU.add))
            link(V.tensor_copy(small_i[:, 0, :], small[:, 5, :]))
            link(V.tensor_scalar(small_i[:, 1, :], small_i[:, 0, :], 7, None, ALU.arith_shift_right))
            link(V.tensor_copy(small[:, NT, :], small_i[:, 1, :]))
            link(V.tensor_reduce(col[:, 0:1], small[:, NT, :], AX.X, ALU.add))
            link(V.tensor_scalar(col[:, 2:3], col[:, 0:1], float(TB - 1), float(TB), ALU.add, ALU.max))
            link(V.tensor_copy(col_i[:, 0:1], col[:, 2:3]))
            link(V.tensor_scalar(col_i[:, 1:2], col_i[:, 0:1], 3, None, ALU.arith_shift_right))
            V.tensor_copy(col[:, 1:2], col_i[:, 1:2]).then_inc(s_tot, 1)
            link(V.tensor_tensor_scan(small[:, 6, :], onesq[:, 0:NB], small[:, NT, :], 0.0, ALU.mult, ALU.add))
            link(V.tensor_tensor(small[:, PRE, :], small[:, 6, :], small[:, NT, :], ALU.subtract))
            dve.wait_ge(s_totp, 3)
            link(V.tensor_scalar(col[:, 3:4], p_sm[:, 64:65], float(TB), None, ALU.mult))
            link(V.tensor_copy(col[:, 4:5], p_sm[:, 64:65]))
            link(V.tensor_scalar(small[:, ST, :], small[:, PRE, :], col[:, 3:4], None, ALU.add))
            link(V.scalar_tensor_tensor(small[:, B0, :], small[:, ST, :], float(P), p_sm[:, 32:32 + NB], ALU.mult, ALU.add))
            link(V.tensor_copy(cum[:, 0, :], small[:, B0, :]))
            for d in range(NB):
                i = V.tensor_tensor_scan(cum[:, 1:Q, d], onesq[:, 0:Q - 1], hist[:, 0:Q - 1, d], small[:, B0, d:d + 1], ALU.mult, ALU.add)
            link(i)
            link(V.tensor_copy(cum_i, cum[:, :, :]))
            link(V.tensor_scalar(part_i[0], cum_i, 8, None, ALU.arith_shift_right))
            link(V.tensor_scalar(part_i[1], cum_i, 255, None, ALU.bitwise_and))
            dve.wait_ge(s_negset, 2)
            for h in range(2):
                for j in range(J):
                    i = V.tensor_copy(lookup[S * j:S * j + S, :, h, j, :], part_i[h][S * j:S * j + S, :, :])
            i.then_inc(s_cnt, 1)
            dve.sem_inc(s_ranked, 2)
            with dve.Fori(1, Q // 2 + 1) as n:
                for h in range(2):
                    dve.wait_ge(s_rows, 2 * n - 1 + h)
                    dve.wait_ge(s_ranked, 2 * n + h)
                    q = (n - 1) * 2 + h
                    for j in range(J):
                        i = V.scalar_tensor_tensor(junk[:, j, :], p_rows[h][0:EP, j * EP:(j + 1) * EP], key[:, bass.ds(q * J + j, 1)],
                                                   cst[0:EP, LOWER, 0:EP], ALU.is_equal, ALU.mult,
                                                   accum_out=rank[:, bass.ds(q, 1), j])
                    i.then_inc(s_ranked, 1)
            dve.wait_ge(s_ranked, Q + 2)
            dve.sem_inc(s_sel, 2)
            k0 = chain[0]
            with dve.Fori(1, Q // 4 + 1) as n:
                step = [0]

                def linkn(ins):
                    step[0] += 1
                    ins.then_inc(s_v, 1)
                    dve.wait_ge(s_v, (n - 1) * 10 + (k0 + step[0]))

                for h in range(2):
                    dve.wait_ge(s_look, 2 * n - 1 + h)
                    o = oh_dst[:, bass.ds((n - 1) * 4 + 2 * h, 2), :, :].rearrange("p q j d -> p q (j d)")
                    linkn(V.tensor_tensor(prod[:, :, :, :], p_h[h][0:EP, 0:4, :, :].rearrange("p (q a) j d -> p q a (j d)", a=2),
                                          o.unsqueeze(2).to_broadcast([EP, 2, 2, J * NB]), ALU.mult))
                    dve.sem_inc(s_sel, 1)
                    linkn(V.tensor_reduce(sel[:, 2 * h:2 * h + 2, :, :].rearrange("p q a j -> p (q a j)"),
                                          prod[:, :, :, :].rearrange("p q a (j d) -> p (q a j) d", d=NB), AX.X, ALU.add))
                linkn(V.scalar_tensor_tensor(pos[:, :, :], sel[:, :, 0, :], 256.0, sel[:, :, 1, :], ALU.mult, ALU.add))
                linkn(V.tensor_tensor(pos_i[:, 0, :].rearrange("p (q j) -> p q j", j=J), pos[:, :, :], rank[:, bass.ds((n - 1) * 4, 4), :], ALU.add))
                linkn(V.tensor_scalar(pos_i[:, 1, :], pos_i[:, 0, :], TB * P - 1, 7, ALU.bitwise_and, ALU.logical_shift_right))
                linkn(V.tensor_scalar(pos_i[:, 2, :], pos_i[:, 0, :], -(TB * P), None, ALU.bitwise_and))
                linkn(V.tensor_tensor(pos_i[:, 3, :], pos_i[:, 1, :], pos_i[:, 2, :], ALU.bitwise_or))
                linkn(V.tensor_scalar(pos_i[:, 4, :], pos_i[:, 0, :], P - 1, 3, ALU.bitwise_and, ALU.logical_shift_left))
                for s in range(2):
                    dve.wait_ge(s_free[s], n + s)
                    k = slice(s * 2 * J, (s + 1) * 2 * J)
                    V.tensor_tensor(index[s][:, :], pos_i[:, 3, k], pos_i[:, 4, k], ALU.bitwise_or).then_inc(s_index[s], 1)
            chain[0] = k0 + 10 * (Q // 4)
            link(V.memset(starts4[:, :], BIG))
            for j in range(J):
                n = len(range(j, NB, J))
                i = V.tensor_copy(starts4[S * j:S * j + NB, 0:n], small[S * j:S * j + NB, ST, j:NB:J])
            link(i)
            link(V.tensor_scalar(count_t[:, 0, :], iota_t[:, :], starts4[:, 0:1], None, ALU.is_ge))
            for k in range(1, 7):
                link(V.scalar_tensor_tensor(count_t[:, k % 2, :], iota_t[:, :], starts4[:, k:k + 1], count_t[:, 1 - k % 2, :], ALU.is_ge, ALU.add))
            V.tensor_scalar(count_b[:, :], iota_t[:, 0:BODIES], col[:, 4:5], None, ALU.is_ge).then_inc(s_bst, 1)
            tiles = BODIES * TB
            tv = tabrow[:, :, 0:TB].rearrange("a b t -> a b t")
            link(V.memset(tabrow[:, :, :], 0.0))
            dve.wait_ge(s_cntp, 4)
            link(V.tensor_scalar(tabrow[:, :, TB:TB + 1].rearrange("a b t -> a (b t)"), p_sm[0:1, 128:128 + BODIES], -1.0, None, ALU.add))
            link(V.tensor_scalar(tabrow[:, :, TB + 1:TB + 2], tabrow[:, :, TB:TB + 1], float(NB), 1.0, ALU.mult, ALU.add))
            for k in range(3):
                a, b = k * 56, min(BODIES, (k + 1) * 56)
                bank = (p_rows[0], p_rows[1], p_h[0])[k]
                flat = bank[:, :] if k < 2 else bank[:, :, :, :].rearrange("p a j d -> p (a j d)")
                i = V.tensor_tensor(tabrow[:, a:b, 0:TB], flat[0:1, 0:(b - a) * TB].rearrange("a (b t) -> a b t", t=TB),
                                    tabrow[:, a:b, TB + 1:TB + 2].to_broadcast([1, b - a, TB]), ALU.subtract)
            link(i)
            link(V.tensor_tensor(tabrow[:, 1:BODIES, TNEW:TNEW + 1], tabrow[:, 1:BODIES, TB:TB + 1],
                                 tabrow[:, 0:BODIES - 1, TB:TB + 1], ALU.subtract))
            V.tensor_copy(bst_i[:, :], p_sm[0:1, 320:320 + S])
            V.tensor_copy(tabrow_i[:, :, :], tabrow[:, :, :]).then_inc(s_tab, 1)
    clear(nc, used)


def clear(nc, semaphores):
    numbers = [x.num for x in semaphores]
    with nc.Block() as block:
        @block.sync
        def _(sp):
            sp.sem_clear(range(min(numbers), max(numbers) + 1))


class Flag:

    def __init__(self, semaphore):
        self.semaphore = semaphore

    def after(self, engine, n):
        engine.wait_ge(self.semaphore, n + 1)

    def before(self, engine, n):
        engine.wait_ge(self.semaphore, n)

    def set_by(self, instruction):
        instruction.then_inc(self.semaphore, 1)


class Chain:

    def __init__(self, engine, sems, n):
        self.engine, self.sems, self.n, self.at = engine, sems, n, 0

    def link(self, instruction):
        semaphore = self.sems[self.at]
        self.at += 1
        instruction.then_inc(semaphore, 1)
        self.engine.wait_ge(semaphore, self.n)


def edges_of(dram):
    return dram["edges"].rearrange("(b p t) c -> b p (t c)", p=P, t=TB)


def load_nodes_phase(nc, io, keep):
    used = []
    ctx = ExitStack()
    with ctx:
        def sb(name, shape, dt):
            return ctx.enter_context(nc.sbuf_tensor("i_" + name, shape, dt))

        def sem(name):
            used.append(ctx.enter_context(nc.semaphore("i_" + name)))
            return used[-1]

        x, tab, ident = keep["x"], keep["tab"], keep["ident"]
        xT = sb("xT", [D, NP], F32)
        wsd = sb("wsd", [D, 4, H1], F32)
        rest = sb("rest", [P, 2, 4 * H1], F32)
        p_x = [ctx.enter_context(nc.psum_tensor(f"i_p_x{i}", [D, 4, P], F32)) for i in range(2)]
        p_y = [ctx.enter_context(nc.psum_tensor(f"i_p_y{i}", [P, 4 * H1], F32)) for i in range(2)]
        n_zero, n_load, n_w = sem("n_zero"), sem("n_load"), sem("n_w")
        n_t, n_tc, n_y, n_ys, n_v = sem("n_t"), sem("n_tc"), sem("n_y"), sem("n_ys"), sem("n_v")
        groups = [(b, min(4, NB - b)) for b in range(0, NB, 4)]
        block = ctx.enter_context(nc.Block())

        @block.sync
        def _(sp):
            sp.dma_start(ident[:, :], io["sort_consts"][:, 0, :]).then_inc(n_w, 16)
            wf, wb = io["L0_gnn_W1f"], io["L0_gnn_W1b"]
            for k, part in enumerate((wf[D:2 * D, :], wb[0:D, :], wf[0:D, :], wb[D:2 * D, :])):
                sp.dma_start(wsd[:, k, :], part).then_inc(n_w, 16)
            sp.wait_ge(n_zero, 1)
            sp.dma_start(x[:, 0:NB - 1, :], io["x"][0:(NB - 1) * P, :].rearrange("(b p) f -> p b f", p=P)).then_inc(n_load, 16)
            sp.dma_start(x[0:LAST, NB - 1, :], io["x"][(NB - 1) * P:N, :]).then_inc(n_load, 16)

        @block.tensor
        def _(pe):
            pe.wait_ge(n_load, 32)
            pe.wait_ge(n_w, 80)
            for g, (b0, nb) in enumerate(groups):
                if g >= 2:
                    pe.wait_ge(n_tc, g - 1)
                for k in range(nb):
                    i = nc.tensor.transpose(p_x[g % 2][:, k, :], x[:, b0 + k, :], ident[:, :])
                i.then_inc(n_t, 1)
            for b in range(NB):
                pe.wait_ge(n_tc, b // 4 + 1)
                if b >= 2:
                    pe.wait_ge(n_ys, b - 1)
                nc.tensor.matmul(p_y[b % 2][:, :], xT[:, b * P:(b + 1) * P], wsd[:, :, :], start=True, stop=True).then_inc(n_y, 1)

        @block.scalar
        def _(act):
            for g, (b0, nb) in enumerate(groups):
                act.wait_ge(n_t, g + 1)
                nc.scalar.copy(xT[:, b0 * P:(b0 + nb) * P], p_x[g % 2][:, 0:nb, :].rearrange("p k n -> p (k n)")).then_inc(n_tc, 1)

        @block.vector
        def _(dve):
            V = nc.vector
            V.memset(x[:, NB - 1, :], 0.0).then_inc(n_zero, 1)
            k = 0
            for b in range(NB):
                dve.wait_ge(n_y, b + 1)
                y, r = p_y[b % 2][:, :], rest[:, b % 2, :]
                V.tensor_copy(tab[:, b, 0, :], y).then_inc(n_v, 1)
                dve.wait_ge(n_v, k + 1)
                V.tensor_tensor(r, y, tab[:, b, 0, :], ALU.subtract).then_inc(n_ys, 1)
                dve.wait_ge(n_ys, b + 1)
                V.tensor_copy(tab[:, b, 1, :], r).then_inc(n_v, 1)
                dve.wait_ge(n_v, k + 2)
                V.tensor_tensor(tab[:, b, 2, :], r, tab[:, b, 1, :], ALU.subtract)
                k += 2
    clear(nc, used)


def layer0_edges_phase(nc, io, dram, keep):
    used = []
    ctx = ExitStack()
    with ctx:
        def sb(name, shape, dt):
            return ctx.enter_context(nc.sbuf_tensor("e_" + name, shape, dt))

        def ps(name, shape, dt=F32):
            return ctx.enter_context(nc.psum_tensor("e_" + name, shape, dt))

        def sem(name):
            used.append(ctx.enter_context(nc.semaphore("e_" + name)))
            return used[-1]

        def flags(name, n=2):
            made = [Flag(sem(f"{name}{i}")) for i in range(n)]
            primed.extend(made)
            return made

        primed = []
        tab, agg, ident = keep["tab"], keep["agg"], keep["ident"]
        two = range(2)
        table = sb("table", [1, BODIES, TAB], I32)
        starts = sb("starts", [1, S], I32)
        iota = sb("iota", [P, P], F32)
        iotab = sb("iotab", [P, P], BF16)
        identb = sb("identb", [P, P], BF16)
        w1e = sb("w1e", [16, 2, H1], F32)
        b1 = sb("b1", [P, 1], F32)
        w2 = sb("w2", [P, 2, D], F32)
        b2 = sb("b2", [1, G, 2, D], F32)
        ones = sb("ones", [1, P], F32)
        zeros = sb("zeros", [P, 2 * P], F32)
        strip = sb("strip", [P, 2, NB, 2 * P], F32)
        rec = [sb(f"rec{s}", [P, G, REC], F32) for s in two]
        wmid = [sb(f"wmid{s}", [P, G], BF16) for s in two]
        wlow = [sb(f"wlow{s}", [P, G], F32) for s in two]
        oh = [sb(f"oh{s}", [P, 2, G, P], BF16) for s in two]
        ohw = [sb(f"ohw{s}", [P, G, 3, P], BF16) for s in two]
        recT = [sb(f"recT{s}", [REC, G * P], F32) for s in two]
        ohT = [sb(f"ohT{s}", [P, 2, G, P], BF16) for s in two]
        hid = [sb(f"hid{s}", [P, G, P], F32) for s in two]
        flow = [sb(f"flow{s}", [P, G, 2 * D], F32) for s in two]
        rest = [sb(f"rest{s}", [P, G, 2 * D], F32) for s in two]
        part = [sb(f"part{s}", [P, G, 3, 2 * D + 2], BF16) for s in two]
        p_rec = ps("p_rec", [REC, G, P])
        p_oh = ps("p_oh", [P, 2, G, P], BF16)
        p_hid = ps("p_hid", [P, G * P])
        p_flow = ps("p_flow", [P, G, 2 * D])
        p_sum = ps("p_sum", [P, G + 1, 2 * D])
        p_aw = [ps(f"p_aw{i}", [P, 2, 2 * P]) for i in two]

        loaded = [sem(f"loaded{s}") for s in two]
        d_const, d_b, d_start, d_flush, d_zero = sem("d_const"), sem("d_b"), sem("d_start"), sem("d_flush"), sem("d_zero")
        strip_full = sem("strip_full")
        prime = sem("prime")
        setup = sem("setup")
        onehots, turned = flags("onehots"), flags("turned")
        recT_copied, ohT_copied = flags("recT_copied"), flags("ohT_copied")
        hid_done, hid_relued = flags("hid_done"), flags("hid_relued")
        aw_done, aw_added = flags("aw_done", 4), flags("aw_added", 4)
        flow_done, flow_relued = flags("flow_done"), flags("flow_relued")
        split, sum_done, sum_added = flags("split"), flags("sum_done"), flags("sum_added")
        weighted = flags("weighted")
        pool_chain = [sem(f"pool_chain{i}") for i in range(4)]
        dve_chain = [sem(f"dve_chain{i}") for i in range(24)]
        block = ctx.enter_context(nc.Block())
        ev = edges_of(dram)

        @block.sync
        def _(sp):
            for f in primed:
                sp.sem_inc(f.semaphore, 1)
            sp.dma_start(table[:, :, :], dram["table"].unsqueeze(0)).then_inc(d_start, 16)
            sp.dma_start(starts[:, :], dram["starts"].unsqueeze(0)).then_inc(d_start, 16)
            sp.dma_start(iota[:, :], io["sort_consts"][:, 1, :]).then_inc(d_const, 16)
            sp.wait_ge(setup, 1)
            for k, (wn, name) in enumerate(((1, "f"), (0, "b"))):
                sp.dma_start(w1e[:, k, :], io["L0_gnn_W1" + name][2 * D:2 * D + 16, :]).then_inc(d_b, 16)
                sp.dma_start(b1[k * H1:(k + 1) * H1, :], io["L0_gnn_b1" + name].unsqueeze(1)).then_inc(d_b, 16)
                sp.dma_start(w2[k * H1:(k + 1) * H1, wn, :], io["L0_gnn_W2" + name]).then_inc(d_b, 16)
                sp.dma_start(b2[:, :, wn, :], io["L0_gnn_b2" + name].unsqueeze(0).unsqueeze(0).to_broadcast([1, G, D])).then_inc(d_b, 16)
            zs = zeros[:, :].unsqueeze(1).to_broadcast([P, NB, 2 * P])
            for k in two:
                sp.dma_start(strip[:, k, :, :], zs).then_inc(d_zero, 16)
                sp.wait_ge(d_zero, 16 * (k + 1))
            sp.wait_ge(d_start, 32)
            last = sp.value_load(starts[0:1, NB:NB + 1], min_val=NB, max_val=BODIES - 1)
            with sp.Fori(1, last + 2) as n:
                for s in two:
                    onehots[s].before(sp, n)
                    turned[s].before(sp, n)
                    weighted[s].before(sp, n)
                    sp.dma_start(rec[s][:, :, :].rearrange("p t c -> p (t c)"), ev[bass.ds(n - 1, 1), :, s * G * REC:(s + 1) * G * REC].rearrange("b p c -> p (b c)")).then_inc(loaded[s], 16)
                new = sp.value_load(table[0:1, bass.ds(n - 1, 1), TNEW], min_val=0, max_val=1)
                with sp.If(new):
                    src = sp.value_load(table[0:1, bass.ds(n - 1, 1), TSRC], min_val=1, max_val=NB - 1)
                    sp.wait_ge(strip_full, src)
                    sp.dma_start(dram["strips"][bass.ds(src - 1, 1), :, :].rearrange("a p x -> p (a x)"),
                                 strip[:, bass.ds((src - 1) & 1, 1), :, :].rearrange("p a b c -> p (a b c)")).then_inc(d_flush, 16)
                    sp.wait_ge(d_flush, src * 16)
                    sp.dma_start(strip[:, bass.ds((src - 1) & 1, 1), :, :].rearrange("p a b c -> p (a b) c"), zs).then_inc(d_zero, 16)
                    sp.wait_ge(d_zero, src * 16 + 32)
                    sp.sem_inc(prime, 1)
            sp.wait_ge(strip_full, NB)
            sp.dma_start(dram["strips"][NB - 1, :, :], strip[:, (NB - 1) & 1, :, :].rearrange("p b c -> p (b c)")).then_inc(d_flush, 16)
            sp.wait_ge(d_flush, NB * 16)

        @block.gpsimd
        def _(pool):
            g = nc.gpsimd
            pool.wait_ge(d_start, 32)
            last = pool.value_load(starts[0:1, NB:NB + 1], min_val=NB, max_val=BODIES - 1)
            with pool.Fori(1, last + 1) as n:
                for s in two:
                    onehots[s].after(pool, n)
                    aw_done[2 * s + 1].before(pool, n)
                    pool.sem_inc(prime, 1)
                    g.tensor_copy(wmid[s][:, :], rec[s][:, :, CR]).then_inc(pool_chain[2 * s], 1)
                    pool.wait_ge(pool_chain[2 * s], n)
                    g.tensor_tensor(wlow[s][:, :], rec[s][:, :, CR], wmid[s][:, :], ALU.subtract).then_inc(pool_chain[2 * s + 1], 1)
                    pool.wait_ge(pool_chain[2 * s + 1], n)
                    for k, w in enumerate((rec[s][:, :, CW], rec[s][:, :, CR], wlow[s][:, :])):
                        i = g.tensor_tensor(ohw[s][:, :, k, :], oh[s][:, 0, :, :], w.unsqueeze(2).to_broadcast([P, G, P]), ALU.mult)
                    weighted[s].set_by(i)

        @block.scalar
        def _(act):
            act.wait_ge(d_start, 32)
            last = act.value_load(starts[0:1, NB:NB + 1], min_val=NB, max_val=BODIES - 1)
            act.wait_ge(d_b, 128)
            with act.Fori(1, last + 1) as n:
                for s in two:
                    turned[s].after(act, n)
                    recT_copied[s].set_by(nc.scalar.copy(recT[s][:, :], p_rec[:, :, :].rearrange("p t e -> p (t e)")))
                    ohT_copied[s].set_by(nc.scalar.copy(ohT[s][:, :, :, :], p_oh[:, :, :, :]))
                for s in two:
                    hid_done[s].after(act, n)
                    hid_relued[s].set_by(nc.scalar.activation(hid[s][:, :, :].rearrange("p t e -> p (t e)"), p_hid[:, :], ACT.Relu, bias=b1[:, :]))
                for s in two:
                    flow_done[s].after(act, n)
                    flow_relued[s].set_by(nc.scalar.activation(flow[s][:, :, :], p_flow[:, :, :], ACT.Relu))

        @block.tensor
        def _(pe):
            mm = nc.tensor.matmul
            pe.wait_ge(d_start, 32)
            last = pe.value_load(starts[0:1, NB:NB + 1], min_val=NB, max_val=BODIES - 1)
            pe.wait_ge(d_b, 128)
            pe.wait_ge(setup, 2)
            with pe.Fori(1, last + 1) as n:
                def entry(k):
                    return pe.value_load(table[0:1, bass.ds(n - 1, 1), k], min_val=0, max_val=NB - 1)

                src = entry(TSRC)
                dst = [entry(t) for t in range(TB)]

                def turn(s):
                    pe.wait_ge(loaded[s], n * 16)
                    onehots[s].after(pe, n)
                    if s:
                        recT_copied[0].after(pe, n)
                        ohT_copied[0].after(pe, n)
                    else:
                        recT_copied[1].before(pe, n)
                        ohT_copied[1].before(pe, n)
                    for t in range(G):
                        nc.tensor.transpose(p_rec[:, t, :], rec[s][:, t, :], ident[:, :])
                    for k in range(2):
                        for t in range(G):
                            i = nc.tensor.transpose(p_oh[:, k, t, :], oh[s][:, k, t, :], identb[:, :])
                    turned[s].set_by(i)

                def hidden(s):
                    if s:
                        hid_relued[0].after(pe, n)
                    else:
                        hid_relued[1].before(pe, n)
                    recT_copied[s].after(pe, n)
                    mm(p_hid[:, :], w1e[:, :, :], recT[s][0:16, :], start=True, stop=False, skip_group_check=True)
                    ohT_copied[s].after(pe, n)
                    for k in range(3):
                        mm(p_hid[:, :], tab[:, bass.ds(src, 1), k, 0:P], ohT[s][:, 0, :, :], start=False, stop=False, skip_group_check=True)
                    for t in range(G):
                        for k in range(3):
                            i = mm(p_hid[:, t * P:(t + 1) * P], tab[:, bass.ds(dst[s * G + t], 1), k, P:2 * P], ohT[s][:, 1, t, :],
                                   start=False, stop=(t == G - 1 and k == 2), skip_group_check=True)
                    hid_done[s].set_by(i)

                def dense(s):
                    weighted[s].after(pe, n)
                    for u in range(2):
                        if s:
                            aw_added[u].after(pe, n)
                        else:
                            aw_added[2 + u].before(pe, n)
                        for v in range(2):
                            t = 2 * u + v
                            mm(p_aw[u][:, v, 0:P], oh[s][:, 0, t, :], oh[s][:, 1, t, :], start=True, stop=True, skip_group_check=True)
                            for k in range(3):
                                i = mm(p_aw[u][:, v, P:2 * P], oh[s][:, 1, t, :], ohw[s][:, t, k, :], start=(k == 0), stop=(k == 2),
                                       skip_group_check=True)
                        aw_done[2 * s + u].set_by(i)

                def second(s):
                    if s:
                        flow_relued[0].after(pe, n)
                    else:
                        flow_relued[1].before(pe, n)
                    mm(p_flow[:, :, :], ones[:, :], b2[:, :, :, :], start=True, stop=False, skip_group_check=True)
                    hid_relued[s].after(pe, n)
                    for t in range(G):
                        i = mm(p_flow[:, t, :], hid[s][:, t, :], w2[:, :, :], start=False, stop=(t == G - 1), skip_group_check=True)
                    flow_done[s].set_by(i)

                def sums(s):
                    if s:
                        sum_added[0].after(pe, n)
                    else:
                        sum_added[1].before(pe, n)
                    split[s].after(pe, n)
                    for t in range(G):
                        for k in range(3):
                            mm(p_sum[:, G, 0:D], oh[s][:, 0, t, :], part[s][:, t, k, 0:D], start=(t == 0 and k == 0),
                               stop=(t == G - 1 and k == 2), skip_group_check=True)
                    for t in range(G):
                        for k in range(3):
                            i = mm(p_sum[:, t, 0:D + 1], oh[s][:, 1, t, :], part[s][:, t, k, D:2 * D + 1], start=(k == 0), stop=(k == 2),
                                   skip_group_check=True)
                    sum_done[s].set_by(i)

                turn(0); turn(1)
                hidden(0); dense(0)
                hidden(1); second(0)
                dense(1); second(1)
                sums(0); sums(1)

        @block.vector
        def _(dve):
            V = nc.vector
            V.memset(w2[:, :, :], 0.0)
            V.memset(ones[:, :], 1.0)
            V.memset(zeros[:, :], 0.0).then_inc(setup, 1)
            V.memset(agg[:, :, :], 0.0)
            for s in two:
                V.memset(part[s][:, :, :, :], 0.0).then_inc(dve_chain[s], 1)
                dve.wait_ge(dve_chain[s], 1)
                V.memset(part[s][:, :, 0, 2 * D:2 * D + 1], 1.0)
            dve.wait_ge(d_const, 16)
            V.tensor_copy(iotab[:, :], iota[:, :])
            V.tensor_copy(identb[:, :], ident[:, :]).then_inc(setup, 1)
            dve.wait_ge(setup, 2)
            for s in two:
                dve.sem_clear(dve_chain[s])
            dve.wait_ge(d_start, 32)
            def one_hots(s, n):
                dve.wait_ge(loaded[s], n * 16)
                for t in range(G):
                    for k, c in enumerate((CSRC, CDST)):
                        i = V.tensor_scalar(oh[s][:, k, t, :], iotab[:, :], rec[s][:, t, c:c + 1], None, ALU.is_equal)
                onehots[s].set_by(i)

            one_hots(0, 1)
            one_hots(1, 1)
            with dve.Fori(0, NB) as b:
                first = dve.value_load(starts[0:1, bass.ds(b, 1)], min_val=0, max_val=BODIES)
                end = dve.value_load(starts[0:1, bass.ds(b + 1, 1)], min_val=1, max_val=BODIES)
                dve.wait_ge(d_zero, (b + 1) * 16)
                half = b & 1
                with dve.Fori(first + 1, end + 1) as n:
                    chain = Chain(dve, dve_chain, n)
                    dst = [dve.value_load(table[0:1, bass.ds(n - 1, 1), t], min_val=0, max_val=NB - 1) for t in range(TB)]

                    def add_dense(s):
                        for u in range(2):
                            aw_done[2 * s + u].after(dve, n)
                            for v in range(2):
                                at = strip[:, bass.ds(half, 1), bass.ds(dst[s * G + 2 * u + v], 1), :].rearrange("p a b c -> p (a b c)")
                                if v:
                                    aw_added[2 * s + u].set_by(V.tensor_tensor(at, p_aw[u][:, v, :], at, ALU.add))
                                    aw_added[2 * s + u].after(dve, n)
                                else:
                                    chain.link(V.tensor_tensor(at, p_aw[u][:, v, :], at, ALU.add))

                    def split_flow(s):
                        flow_relued[s].after(dve, n)
                        chain.link(V.tensor_copy(part[s][:, :, 0, 0:2 * D], flow[s][:, :, :]))
                        chain.link(V.tensor_tensor(rest[s][:, :, :], flow[s][:, :, :], part[s][:, :, 0, 0:2 * D], ALU.subtract))
                        chain.link(V.tensor_copy(part[s][:, :, 1, 0:2 * D], rest[s][:, :, :]))
                        split[s].set_by(V.tensor_tensor(part[s][:, :, 2, 0:2 * D], rest[s][:, :, :], part[s][:, :, 1, 0:2 * D], ALU.subtract))

                    def add_sums(s):
                        sum_done[s].after(dve, n)
                        at = agg[:, bass.ds(b, 1), 0:D].rearrange("p a c -> p (a c)")
                        chain.link(V.tensor_tensor(at, p_sum[:, G, 0:D], at, ALU.add))
                        for t in range(G):
                            at = agg[:, bass.ds(dst[s * G + t], 1), D:2 * D + 1].rearrange("p a c -> p (a c)")
                            i = V.tensor_tensor(at, p_sum[:, t, 0:D + 1], at, ALU.add)
                            if t < G - 1:
                                chain.link(i)
                            else:
                                sum_added[s].set_by(i)
                                sum_added[s].after(dve, n)

                    add_dense(0); split_flow(0)
                    add_dense(1); split_flow(1)
                    add_sums(0); one_hots(0, n + 1)
                    add_sums(1); one_hots(1, n + 1)
                dve.sem_inc(strip_full, 1)
    clear(nc, used)


EPS = 1e-5
RT3, ALPHA_MSG, ALPHA_SELF = 3.0 ** -0.5, 16.0 ** -0.5 / 16.0 ** 0.5, 8.0 ** -0.5
MUL = 8
H2 = 64
NTP = 4 * MUL * MUL
STEPS2, ALPHA2 = 10, 0.1
STEPS3 = 3


def layernorm(dve, V, link, x, r, tmp, std, std_ready, rooted):
    wide = [P, NB, D]
    link(V.tensor_reduce(std[:, 0, :], r[:, :, :], AX.X, ALU.add))
    link(V.tensor_scalar(std[:, 0, :], std[:, 0, :], 1.0 / D, None, ALU.mult))
    link(V.tensor_tensor(r[:, :, :], r[:, :, :], std[:, 0, :].unsqueeze(2).to_broadcast(wide), ALU.subtract))
    link(V.tensor_tensor(tmp[:, :, :], r[:, :, :], r[:, :, :], ALU.mult))
    link(V.tensor_reduce(std[:, 1, :], tmp[:, :, :], AX.X, ALU.add))
    V.tensor_scalar(std[:, 1, :], std[:, 1, :], 1.0 / D, EPS, ALU.mult, ALU.add).then_inc(std_ready, 1)
    dve.wait_ge(rooted, 1)
    link(V.reciprocal(std[:, 3, :], std[:, 2, :]))
    link(V.tensor_tensor(x[:, :, :], r[:, :, :], std[:, 3, :].unsqueeze(2).to_broadcast(wide), ALU.mult))


def nodes_phase(nc, io, keep, layer):
    used = []
    ctx = ExitStack()
    with ctx:
        def sb(name, shape, dt=F32):
            return ctx.enter_context(nc.sbuf_tensor(f"n{layer}_{name}", shape, dt))

        def sem(name):
            used.append(ctx.enter_context(nc.semaphore(f"n{layer}_{name}")))
            return used[-1]

        x, agg, ident, xp = keep["x"], keep["agg"], keep["ident"], keep["xp"]
        K = 2 * D if layer == 0 else D
        turned = sb("turned", [K, NP])
        w1 = sb("w1", [K, 2 * D])
        b1 = sb("b1", [2 * D, 1])
        z = sb("z", [2 * D + 1, NP])
        w2 = sb("w2", [2 * D + 1, D])
        r = sb("r", [P, NB, D])
        tmp = sb("tmp", [P, NB, D])
        std = sb("std", [P, 4, NB])
        p_t = [ctx.enter_context(nc.psum_tensor(f"n{layer}_p_t{i}", [K, 4, P], F32)) for i in range(2)]
        p_z = [ctx.enter_context(nc.psum_tensor(f"n{layer}_p_z{i}", [2 * D, 512], F32)) for i in range(2)]
        p_o = [ctx.enter_context(nc.psum_tensor(f"n{layer}_p_o{i}", [P, 16, D], F32)) for i in range(2)]
        s_w, s_t, s_tc, s_z, s_zc, s_o, s_v = sem("w"), sem("t"), sem("tc"), sem("z"), sem("zc"), sem("o"), sem("v")
        s_std, s_root, s_zero = sem("std"), sem("root"), sem("zero")
        groups = [(b, min(4, NB - b)) for b in range(0, NB, 4)]
        halves = [(0, 16), (16, NB - 16)]
        loads = 5 if layer == 0 else 4
        block = ctx.enter_context(nc.Block())

        @block.sync
        def _(sp):
            if layer == 0:
                sp.dma_start(w1[0:D, :], io["L0_gnn_W1n"][D:2 * D, :]).then_inc(s_w, 16)
                sp.dma_start(w1[D:2 * D, :], io["L0_gnn_W1n"][0:D, :]).then_inc(s_w, 16)
                sp.dma_start(b1[:, :], io["L0_gnn_b1n"].unsqueeze(1)).then_inc(s_w, 16)
                sp.dma_start(w2[0:2 * D, :], io["L0_gnn_W2n"]).then_inc(s_w, 16)
                sp.dma_start(w2[2 * D:2 * D + 1, :], io["L0_gnn_b2n"].unsqueeze(0)).then_inc(s_w, 16)
            else:
                sp.wait_ge(s_zero, 1)
                sp.dma_start(w1[0:MUL, 0:MUL], io["L1_gnn_Ws"]).then_inc(s_w, 16)
                for i in range(3):
                    sp.dma_start(w1[MUL + i:D:3, MUL + i:D:3], io["L1_gnn_Wv"], allow_slow_non_contiguous=True).then_inc(s_w, 16)

        @block.tensor
        def _(pe):
            what = agg if layer == 0 else x
            for g, (b0, nb) in enumerate(groups):
                if g >= 2:
                    pe.wait_ge(s_tc, g - 1)
                for k in range(nb):
                    i = nc.tensor.transpose(p_t[g % 2][:, k, :], what[:, b0 + k, 0:K], ident[:, :])
                i.then_inc(s_t, 1)
            pe.wait_ge(s_w, 16 * loads)
            pe.wait_ge(s_tc, len(groups))
            if layer == 0:
                for g, (b0, nb) in enumerate(groups):
                    if g >= 2:
                        pe.wait_ge(s_zc, g - 1)
                    nc.tensor.matmul(p_z[g % 2][:, 0:nb * P], w1[:, :], turned[:, b0 * P:(b0 + nb) * P], start=True, stop=True).then_inc(s_z, 1)
                pe.wait_ge(s_zc, len(groups))
                pe.wait_ge(s_zero, 1)
            for h, (b0, nb) in enumerate(halves):
                for k in range(nb):
                    at = slice((b0 + k) * P, (b0 + k + 1) * P)
                    if layer == 0:
                        i = nc.tensor.matmul(p_o[h][:, k, :], z[:, at], w2[:, :], start=True, stop=True, skip_group_check=True)
                    else:
                        i = nc.tensor.matmul(p_o[h][:, k, :], turned[:, at], w1[:, 0:D], start=True, stop=True, skip_group_check=True)
                i.then_inc(s_o, 1)

        @block.scalar
        def _(act):
            for g, (b0, nb) in enumerate(groups):
                act.wait_ge(s_t, g + 1)
                nc.scalar.copy(turned[:, b0 * P:(b0 + nb) * P], p_t[g % 2][:, 0:nb, :].rearrange("p k n -> p (k n)")).then_inc(s_tc, 1)
            if layer == 0:
                act.wait_ge(s_w, 16 * loads)
                for g, (b0, nb) in enumerate(groups):
                    act.wait_ge(s_z, g + 1)
                    nc.scalar.activation(z[0:2 * D, b0 * P:(b0 + nb) * P], p_z[g % 2][:, 0:nb * P], ACT.Relu, bias=b1[:, :]).then_inc(s_zc, 1)
            act.wait_ge(s_std, 1)
            nc.scalar.sqrt(std[:, 2, :], std[:, 1, :]).then_inc(s_root, 1)

        @block.vector
        def _(dve):
            V = nc.vector
            at = [0]

            def link(i):
                at[0] += 1
                i.then_inc(s_v, 1)
                dve.wait_ge(s_v, at[0])

            if layer == 0:
                V.memset(z[2 * D:2 * D + 1, :], 1.0).then_inc(s_zero, 1)
            else:
                V.memset(w1[:, :], 0.0).then_inc(s_zero, 1)
            for h, (b0, nb) in enumerate(halves):
                dve.wait_ge(s_o, h + 1)
                b = slice(b0, b0 + nb)
                if layer == 0:
                    link(V.scalar_tensor_tensor(r[:, b, :], p_o[h][:, 0:nb, :], 0.0, x[:, b, :], ALU.max, ALU.add))
                else:
                    link(V.scalar_tensor_tensor(r[:, b, :], p_o[h][:, 0:nb, :], ALPHA_SELF, x[:, b, :], ALU.mult, ALU.add))
                    link(V.scalar_tensor_tensor(r[:, b, :], agg[:, b, 0:D], ALPHA_MSG, r[:, b, :], ALU.mult, ALU.add))
            layernorm(dve, V, link, x, r, tmp, std, s_std, s_root)
            if layer == 0:
                link(V.tensor_copy(xp[:, :, 0, :], x[:, :, :]))
                link(V.tensor_tensor(r[:, :, :], x[:, :, :], xp[:, :, 0, :], ALU.subtract))
                link(V.tensor_copy(xp[:, :, 1, :], r[:, :, :]))
                link(V.tensor_tensor(xp[:, :, 2, :], r[:, :, :], xp[:, :, 1, :], ALU.subtract))
    clear(nc, used)


def layer1_edges_phase(nc, io, dram, keep):
    used = []
    ctx = ExitStack()
    with ctx:
        def sb(name, shape, dt=F32):
            return ctx.enter_context(nc.sbuf_tensor("m_" + name, shape, dt))

        def ps(name, shape, dt=F32):
            return ctx.enter_context(nc.psum_tensor("m_" + name, shape, dt))

        def sem(name):
            used.append(ctx.enter_context(nc.semaphore("m_" + name)))
            return used[-1]

        def flags(name, n=2):
            made = [Flag(sem(f"{name}{i}")) for i in range(n)]
            primed.extend(made)
            return made

        primed = []
        xp, agg, ident = keep["xp"], keep["agg"], keep["ident"]
        two = range(2)
        table = sb("table", [1, BODIES, TAB], I32)
        starts = sb("starts", [1, S], I32)
        iota = sb("iota", [P, P])
        iotab = sb("iotab", [P, P], BF16)
        rt3 = sb("rt3", [P, G, 3])
        identb = sb("identb", [P, P], BF16)
        w1 = sb("w1", [C4, H2])
        b1 = sb("b1", [H2, 1])
        w2 = sb("w2", [H2, H2])
        b2 = sb("b2", [H2, 1])
        w3 = sb("w3", [H2 + 1, NTP])
        rec = [sb(f"rec{s}", [P, G, REC]) for s in two]
        oh = [sb(f"oh{s}", [P, 2, G, P], BF16) for s in two]
        recT = [sb(f"recT{s}", [C4, G * P]) for s in two]
        ohT = [sb(f"ohT{s}", [P, G, P], BF16) for s in two]
        node = [sb(f"node{s}", [P, G, D]) for s in two]
        h1 = [sb(f"h1{s}", [H2, G * P]) for s in two]
        h2 = [sb(f"h2{s}", [H2 + 1, G * P]) for s in two]
        coef = [sb(f"coef{s}", [P, G, 2 * MUL]) for s in two]
        sh3 = [sb(f"sh3{s}", [P, G, 3]) for s in two]
        dots = [sb(f"dots{s}", [P, G, MUL, 3]) for s in two]
        vec0 = [sb(f"vec0{s}", [P, G, MUL, 3]) for s in two]
        prod0 = sb("prod0", [P, G, 2 * MUL, MUL])
        prod1 = sb("prod1", [P, G, MUL, MUL])
        prod2 = sb("prod2", [P, 3, G, MUL, MUL])
        sum1 = sb("sum1", [P, G, MUL])
        sum2 = sb("sum2", [P, 3, G, MUL])
        outer = sb("outer", [P, G, MUL, 3])
        msg = [sb(f"msg{s}", [P, G, D]) for s in two]
        rest = [sb(f"rest{s}", [P, G, D]) for s in two]
        part = [sb(f"part{s}", [P, G, 3, D], BF16) for s in two]
        p_rec = ps("p_rec", [REC, G, P])
        p_oh = ps("p_oh", [P, G, P], BF16)
        p_node = ps("p_node", [P, G, D])
        p_h = [ps(f"p_h{s}", [H2, G * P]) for s in two]
        p_w = ps("p_w", [P, G, NTP])
        p_sum = ps("p_sum", [P, G, D])

        loaded = [sem(f"loaded{s}") for s in two]
        d_start, d_const, setup, prime = sem("d_start"), sem("d_const"), sem("setup"), sem("prime")
        onehots, turned = flags("onehots"), flags("turned")
        recT_copied, ohT_copied = flags("recT_copied"), flags("ohT_copied")
        node_done, node_copied, made_coef = flags("node_done"), flags("node_copied"), flags("made_coef")
        h1_done, h1_act, h2_done, h2_act = flags("h1_done"), flags("h1_act"), flags("h2_done"), flags("h2_act")
        w_done, w_read = flags("w_done"), flags("w_read")
        split, sum_done, sum_added = flags("split"), flags("sum_done"), flags("sum_added")
        dve_chain = [sem(f"dve_chain{i}") for i in range(40)]
        pool_chain = [sem(f"pool_chain{i}") for i in range(8)]
        block = ctx.enter_context(nc.Block())
        ev = edges_of(dram)

        @block.sync
        def _(sp):
            for f in primed:
                sp.sem_inc(f.semaphore, 1)
            sp.dma_start(table[:, :, :], dram["table"].unsqueeze(0)).then_inc(d_start, 16)
            sp.dma_start(starts[:, :], dram["starts"].unsqueeze(0)).then_inc(d_start, 16)
            sp.dma_start(iota[:, :], io["sort_consts"][:, 1, :]).then_inc(d_const, 16)
            sp.wait_ge(setup, 1)
            sp.dma_start(w1[C8:C8 + MUL, :], io["L1_gnn_W1"]).then_inc(d_const, 16)
            sp.dma_start(b1[:, :], io["L1_gnn_b1"].unsqueeze(1)).then_inc(d_const, 16)
            sp.dma_start(w2[:, :], io["L1_gnn_W2"]).then_inc(d_const, 16)
            sp.dma_start(b2[:, :], io["L1_gnn_b2"].unsqueeze(1)).then_inc(d_const, 16)
            sp.dma_start(w3[0:H2, :], io["L1_gnn_W3"]).then_inc(d_const, 16)
            sp.dma_start(w3[H2:H2 + 1, :], io["L1_gnn_b3"].unsqueeze(0)).then_inc(d_const, 16)
            sp.wait_ge(d_start, 32)
            last = sp.value_load(starts[0:1, NB:NB + 1], min_val=NB, max_val=BODIES - 1)
            with sp.Fori(1, last + 2) as n:
                for s in two:
                    onehots[s].before(sp, n)
                    turned[s].before(sp, n)
                    split[s].before(sp, n)
                    sp.dma_start(rec[s][:, :, :].rearrange("p t c -> p (t c)"),
                                 ev[bass.ds(n - 1, 1), :, s * G * REC:(s + 1) * G * REC].rearrange("b p c -> p (b c)")).then_inc(loaded[s], 16)

        @block.gpsimd
        def _(pool):
            g = nc.gpsimd
            pool.wait_ge(d_start, 32)
            pool.wait_ge(setup, 2)
            last = pool.value_load(starts[0:1, NB:NB + 1], min_val=NB, max_val=BODIES - 1)
            with pool.Fori(1, last + 1) as n:
                for s in two:
                    node_copied[s].after(pool, n)
                    pool.wait_ge(loaded[s], n * 16)
                    split[s].before(pool, n)
                    pool.sem_inc(prime, 1)
                    sh0, sh1 = rec[s][:, :, C4:C4 + 1], rec[s][:, :, C4 + 1:C4 + 4]
                    vec = node[s][:, :, MUL:D].rearrange("p t (u i) -> p t u i", i=3)
                    g.tensor_tensor(coef[s][:, :, 0:MUL], node[s][:, :, 0:MUL], sh0.to_broadcast([P, G, MUL]), ALU.mult)
                    g.tensor_tensor(vec0[s][:, :, :, :].rearrange("p t u i -> p t (u i)"), node[s][:, :, MUL:D],
                                    sh0.to_broadcast([P, G, 3 * MUL]), ALU.mult)
                    g.tensor_tensor(sh3[s][:, :, :], sh1, rt3[:, :, :], ALU.mult).then_inc(pool_chain[s], 1)
                    pool.wait_ge(pool_chain[s], n)
                    made_coef[s].set_by(g.tensor_tensor(dots[s][:, :, :, :], vec, sh3[s][:, :, :].unsqueeze(2).to_broadcast([P, G, MUL, 3]), ALU.mult))

        @block.scalar
        def _(act):
            act.wait_ge(d_start, 32)
            last = act.value_load(starts[0:1, NB:NB + 1], min_val=NB, max_val=BODIES - 1)
            act.wait_ge(d_const, 112)
            with act.Fori(1, last + 1) as n:
                for s in two:
                    turned[s].after(act, n)
                    recT_copied[s].set_by(nc.scalar.copy(recT[s][:, :], p_rec[0:C4, :, :].rearrange("p t e -> p (t e)")))
                    ohT_copied[s].set_by(nc.scalar.copy(ohT[s][:, :, :], p_oh[:, :, :]))
                for s in two:
                    node_done[s].after(act, n)
                    node_copied[s].set_by(nc.scalar.copy(node[s][:, :, :], p_node[:, :, :]))
                    h1_done[s].after(act, n)
                    h1_act[s].set_by(nc.scalar.activation(h1[s][:, :], p_h[s][:, :], ACT.Silu, bias=b1[:, :]))
                for s in two:
                    h2_done[s].after(act, n)
                    h2_act[s].set_by(nc.scalar.activation(h2[s][0:H2, :], p_h[s][:, :], ACT.Silu, bias=b2[:, :]))

        @block.tensor
        def _(pe):
            mm = nc.tensor.matmul
            pe.wait_ge(d_start, 32)
            last = pe.value_load(starts[0:1, NB:NB + 1], min_val=NB, max_val=BODIES - 1)
            pe.wait_ge(d_const, 112)
            pe.wait_ge(setup, 2)
            with pe.Fori(1, last + 1) as n:
                src = pe.value_load(table[0:1, bass.ds(n - 1, 1), TSRC], min_val=0, max_val=NB - 1)

                def turn(s):
                    pe.wait_ge(loaded[s], n * 16)
                    onehots[s].after(pe, n)
                    if s:
                        recT_copied[0].after(pe, n)
                        ohT_copied[0].after(pe, n)
                    else:
                        recT_copied[1].before(pe, n)
                        ohT_copied[1].before(pe, n)
                    for t in range(G):
                        nc.tensor.transpose(p_rec[:, t, :], rec[s][:, t, :], ident[:, :])
                    for t in range(G):
                        i = nc.tensor.transpose(p_oh[:, t, :], oh[s][:, 0, t, :], identb[:, :])
                    turned[s].set_by(i)

                def gather(s):
                    ohT_copied[s].after(pe, n)
                    if s:
                        node_copied[0].after(pe, n)
                    else:
                        node_copied[1].before(pe, n)
                    for t in range(G):
                        for k in range(3):
                            i = mm(p_node[:, t, :], ohT[s][:, t, :], xp[:, bass.ds(src, 1), k, :], start=(k == 0), stop=(k == 2), skip_group_check=True)
                    node_done[s].set_by(i)

                def first(s):
                    recT_copied[s].after(pe, n)
                    h2_act[s].before(pe, n)
                    h1_done[s].set_by(mm(p_h[s][:, :], w1[:, :], recT[s][:, :], start=True, stop=True))

                def second(s):
                    h1_act[s].after(pe, n)
                    pe.sem_inc(prime, 1)
                    h2_done[s].set_by(mm(p_h[s][:, :], w2[:, :], h1[s][:, :], start=True, stop=True))

                def third(s):
                    h2_act[s].after(pe, n)
                    if s:
                        w_read[0].after(pe, n)
                    else:
                        w_read[1].before(pe, n)
                    for t in range(G):
                        i = mm(p_w[:, t, :], h2[s][:, t * P:(t + 1) * P], w3[:, :], start=True, stop=True, skip_group_check=True)
                    w_done[s].set_by(i)

                def sums(s):
                    split[s].after(pe, n)
                    if s:
                        sum_added[0].after(pe, n)
                    else:
                        sum_added[1].before(pe, n)
                    for t in range(G):
                        for k in range(3):
                            i = mm(p_sum[:, t, :], oh[s][:, 1, t, :], part[s][:, t, k, :], start=(k == 0), stop=(k == 2), skip_group_check=True)
                    sum_done[s].set_by(i)

                turn(0); turn(1)
                gather(0); first(0)
                gather(1); first(1)
                second(0); second(1)
                third(0); third(1)
                sums(0); sums(1)

        @block.vector
        def _(dve):
            V = nc.vector
            V.memset(w1[:, :], 0.0).then_inc(setup, 1)
            V.memset(agg[:, :, 0:D], 0.0)
            for s in two:
                V.memset(h2[s][H2:H2 + 1, :], 1.0)
            V.memset(rt3[:, :, :], RT3)
            dve.wait_ge(d_const, 112)
            V.tensor_copy(iotab[:, :], iota[:, :])
            V.tensor_copy(identb[:, :], ident[:, :]).then_inc(setup, 1)
            dve.wait_ge(setup, 2)
            dve.wait_ge(d_start, 32)
            last = dve.value_load(starts[0:1, NB:NB + 1], min_val=NB, max_val=BODIES - 1)
            MM = MUL * MUL
            def one_hots(s, n):
                dve.wait_ge(loaded[s], n * 16)
                for t in range(G):
                    for k, c in enumerate((CSRC, CDST)):
                        i = V.tensor_scalar(oh[s][:, k, t, :], iotab[:, :], rec[s][:, t, c:c + 1], None, ALU.is_equal)
                onehots[s].set_by(i)

            one_hots(0, 1)
            one_hots(1, 1)
            with dve.Fori(1, last + 1) as n:
                chain = Chain(dve, dve_chain, n)
                link = chain.link
                dst = [dve.value_load(table[0:1, bass.ds(n - 1, 1), t], min_val=0, max_val=NB - 1) for t in range(TB)]

                def products(s):
                    made_coef[s].after(dve, n)
                    link(V.tensor_reduce(coef[s][:, :, MUL:2 * MUL], dots[s][:, :, :, :], AX.X, ALU.add))
                    w_done[s].after(dve, n)
                    link(V.tensor_tensor(prod0[:, :, :, :], p_w[:, :, 0:2 * MM].rearrange("p t (u w) -> p t u w", w=MUL),
                                         coef[s][:, :, :].unsqueeze(3).to_broadcast([P, G, 2 * MUL, MUL]), ALU.mult))
                    link(V.tensor_tensor(prod1[:, :, :, :], p_w[:, :, 2 * MM:3 * MM].rearrange("p t (u w) -> p t u w", w=MUL),
                                         node[s][:, :, 0:MUL].unsqueeze(3).to_broadcast([P, G, MUL, MUL]), ALU.mult))
                    for i in range(3):
                        last_op = V.tensor_tensor(prod2[:, i, :, :, :], p_w[:, :, 3 * MM:4 * MM].rearrange("p t (u w) -> p t u w", w=MUL),
                                                  vec0[s][:, :, :, i].unsqueeze(3).to_broadcast([P, G, MUL, MUL]), ALU.mult)
                    w_read[s].set_by(last_op)
                    w_read[s].after(dve, n)
                    link(V.tensor_reduce(msg[s][:, :, 0:MUL], prod0[:, :, :, :].rearrange("p t u w -> p t w u"), AX.X, ALU.add))
                    link(V.tensor_reduce(sum1[:, :, :], prod1[:, :, :, :].rearrange("p t u w -> p t w u"), AX.X, ALU.add))
                    link(V.tensor_reduce(sum2[:, :, :, :].rearrange("p i t w -> p (i t) w"),
                                         prod2[:, :, :, :, :].rearrange("p i t u w -> p (i t) w u"), AX.X, ALU.add))
                    link(V.tensor_tensor(outer[:, :, :, :], sum1[:, :, :].unsqueeze(3).to_broadcast([P, G, MUL, 3]),
                                         rec[s][:, :, C4 + 1:C4 + 4].unsqueeze(2).to_broadcast([P, G, MUL, 3]), ALU.mult))
                    link(V.tensor_tensor(msg[s][:, :, MUL:D].rearrange("p t (w i) -> p t w i", i=3), outer[:, :, :, :],
                                         sum2[:, :, :, :].rearrange("p i t w -> p t w i"), ALU.add))
                    link(V.tensor_copy(part[s][:, :, 0, :], msg[s][:, :, :]))
                    link(V.tensor_tensor(rest[s][:, :, :], msg[s][:, :, :], part[s][:, :, 0, :], ALU.subtract))
                    link(V.tensor_copy(part[s][:, :, 1, :], rest[s][:, :, :]))
                    split[s].set_by(V.tensor_tensor(part[s][:, :, 2, :], rest[s][:, :, :], part[s][:, :, 1, :], ALU.subtract))

                def add_sums(s):
                    sum_done[s].after(dve, n)
                    for t in range(G):
                        at = agg[:, bass.ds(dst[s * G + t], 1), 0:D].rearrange("p a c -> p (a c)")
                        i = V.tensor_tensor(at, p_sum[:, t, :], at, ALU.add)
                        if t < G - 1:
                            link(i)
                        else:
                            sum_added[s].set_by(i)
                            sum_added[s].after(dve, n)

                products(0); products(1)
                add_sums(0); one_hots(0, n + 1)
                add_sums(1); one_hots(1, n + 1)
    clear(nc, used)


def layer2_phase(nc, io, dram, keep):
    used = []
    ctx = ExitStack()
    with ctx:
        def sb(name, shape, dt=F32):
            return ctx.enter_context(nc.sbuf_tensor("q_" + name, shape, dt))

        def sem(name):
            used.append(ctx.enter_context(nc.semaphore("q_" + name)))
            return used[-1]

        def flags(name, n):
            made = [Flag(sem(f"{name}{i}")) for i in range(n)]
            primed.extend(made)
            return made

        primed = []
        x, agg, ident = keep["x"], keep["agg"], keep["ident"]
        CH = -(-NB // 4)
        width = [min(4, NB - 4 * c) for c in range(CH)]
        A = sb("A", [P, NB, NP], BF16)
        g3 = [sb(f"g3{k}", [P, NB, 3, D], BF16) for k in range(2)]
        sT = [sb(f"sT{k}", [3 * D, 4 * P]) for k in range(2)]
        s_ = sb("s_", [P, 4, D])
        gf = sb("gf", [P, 4, D])
        rest = sb("rest", [P, 4, D])
        h = sb("h", [P, NB, D])
        base = sb("base", [P, NB, D])
        norm = sb("norm", [P, 4, NB])
        std = sb("std", [P, 4, NB])
        p_s = [ctx.enter_context(nc.psum_tensor(f"q_p_s{k}", [3 * D, 512], F32)) for k in range(4)]
        p_t = [ctx.enter_context(nc.psum_tensor(f"q_p_t{k}", [P, 4, 3 * D], F32)) for k in range(2)]
        a_loaded = dram["a_loaded"]
        d_ready, rooted, s_v, started, s_std, s_root, s_credit = (sem("d_ready"), sem("rooted"), sem("v"), sem("started"),
                                                                  sem("std"), sem("root"), sem("credit"))
        U = 2
        summed, copied, turned, gathered = flags("summed", U * CH), flags("copied", U * CH), flags("turned", U * CH), flags("gathered", U * CH)
        dve_chain = [sem(f"chain{i}") for i in range(7)]
        block = ctx.enter_context(nc.Block())

        @block.gpsimd
        def _(pool):
            for b in range(NB):
                pool.dma_start(A[:, b, :].rearrange("p (d c) -> p d c", c=P),
                               dram["strips"][b, :, :].rearrange("p (d k) -> p d k", k=2 * P)[:, :, 0:P]).then_inc(a_loaded, 16)

        @block.sync
        def _(sp):
            for f in primed:
                sp.sem_inc(f.semaphore, 1)

        @block.scalar
        def _(act):
            act.wait_ge(d_ready, 1)
            nc.scalar.sqrt(norm[:, 1, :], norm[:, 0, :]).then_inc(rooted, 1)
            with act.Fori(1, STEPS2 // U + 1) as n:
                for u in range(U):
                    for c in range(CH):
                        i = u * CH + c
                        summed[i].after(act, n)
                        if i >= 2:
                            turned[i - 2].after(act, n)
                        else:
                            turned[U * CH - 2 + i].before(act, n)
                        copied[i].set_by(nc.scalar.copy(sT[i % 2][:, 0:width[c] * P], p_s[i % 4][:, 0:width[c] * P]))
            act.wait_ge(s_std, 1)
            nc.scalar.sqrt(std[:, 2, :], std[:, 1, :]).then_inc(s_root, 1)

        @block.tensor
        def _(pe):
            pe.wait_ge(started, 1)
            pe.wait_ge(a_loaded, 16 * NB)
            total = U * CH
            with pe.Fori(1, STEPS2 // U + 1) as n:
                def turn(i):
                    c = i % CH
                    copied[i].after(pe, n)
                    if i >= 2:
                        gathered[i - 2].after(pe, n)
                    else:
                        gathered[total - 2 + i].before(pe, n)
                    for k in range(width[c]):
                        m = nc.tensor.transpose(p_t[i % 2][:, k, :], sT[i % 2][:, k * P:(k + 1) * P], ident[0:3 * D, 0:3 * D])
                    turned[i].set_by(m)

                for u in range(U):
                    for c in range(CH):
                        i = u * CH + c
                        if i >= 4:
                            copied[i - 4].after(pe, n)
                        else:
                            last_use = [j for j in range(total) if j % 4 == i % 4][-1]
                            copied[last_use].before(pe, n)
                        for b in range(NB):
                            if c == 0 and b % 4 == 0:
                                if u:
                                    gathered[b // 4].after(pe, n)
                                else:
                                    gathered[CH + b // 4].before(pe, n)
                            m = nc.tensor.matmul(p_s[i % 4][:, 0:width[c] * P], g3[u][:, b, :, :], A[:, b, 4 * c * P:(4 * c + width[c]) * P],
                                                 start=(b == 0), stop=(b == NB - 1))
                        summed[i].set_by(m)
                        if c:
                            turn(i - 1)
                    turn(u * CH + CH - 1)

        @block.vector
        def _(dve):
            V = nc.vector
            at = [0]

            def link(i):
                at[0] += 1
                i.then_inc(s_v, 1)
                dve.wait_ge(s_v, at[0])

            deg = agg[:, :, 2 * D]
            wide = [P, NB, D]
            V.tensor_scalar(norm[:, 0, :], deg, 1.0, None, ALU.max).then_inc(d_ready, 1)
            link(V.tensor_scalar(norm[:, 3, :], deg, 0.0, None, ALU.is_gt))
            dve.wait_ge(rooted, 1)
            link(V.reciprocal(norm[:, 2, :], norm[:, 1, :]))
            link(V.tensor_tensor(norm[:, 1, :], norm[:, 2, :], norm[:, 3, :], ALU.mult))
            link(V.tensor_scalar(norm[:, 2, :], norm[:, 1, :], 1.0 - ALPHA2, None, ALU.mult))
            link(V.tensor_scalar(base[:, :, :], x[:, :, :], ALPHA2, None, ALU.mult))
            link(V.tensor_tensor(h[:, :, :], x[:, :, :], norm[:, 1, :].unsqueeze(2).to_broadcast(wide), ALU.mult))
            link(V.tensor_copy(g3[0][:, :, 0, :], h[:, :, :]))
            link(V.tensor_tensor(h[:, :, :], h[:, :, :], g3[0][:, :, 0, :], ALU.subtract))
            link(V.tensor_copy(g3[0][:, :, 1, :], h[:, :, :]))
            link(V.tensor_tensor(g3[0][:, :, 2, :], h[:, :, :], g3[0][:, :, 1, :], ALU.subtract))
            dve.sem_inc(started, 1)
            with dve.Fori(1, STEPS2 // U + 1) as n:
                for u in range(U):
                    to = g3[1 - u]
                    for c in range(CH):
                        i = u * CH + c
                        w = width[c]
                        b = slice(4 * c, 4 * c + w)
                        wd = [P, w, D]

                        def chained(k, ins):
                            ins.then_inc(dve_chain[k], 1)
                            dve.wait_ge(dve_chain[k], (n - 1) * total + (i + 1))

                        total = U * CH
                        turned[i].after(dve, n)
                        chained(0, V.tensor_reduce(s_[:, 0:w, :], p_t[i % 2][:, 0:w, :].rearrange("p b (k f) -> p b f k", k=3), AX.X, ALU.add))
                        chained(1, V.tensor_tensor(gf[:, 0:w, :], s_[:, 0:w, :], norm[:, 2, b].unsqueeze(2).to_broadcast(wd), ALU.mult))
                        chained(2, V.tensor_tensor(h[:, b, :], gf[:, 0:w, :], base[:, b, :], ALU.add))
                        chained(3, V.tensor_tensor(gf[:, 0:w, :], h[:, b, :], norm[:, 1, b].unsqueeze(2).to_broadcast(wd), ALU.mult))
                        chained(4, V.tensor_copy(to[:, b, 0, :], gf[:, 0:w, :]))
                        chained(5, V.tensor_tensor(rest[:, 0:w, :], gf[:, 0:w, :], to[:, b, 0, :], ALU.subtract))
                        chained(6, V.tensor_copy(to[:, b, 1, :], rest[:, 0:w, :]))
                        gathered[i].set_by(V.tensor_tensor(to[:, b, 2, :], rest[:, 0:w, :], to[:, b, 1, :], ALU.subtract))
            gathered[U * CH - 1].after(dve, STEPS2 // U)
            link(V.tensor_tensor(h[:, :, :], x[:, :, :], h[:, :, :], ALU.add))
            layernorm(dve, V, link, x, h, base, std, s_std, s_root)
    clear(nc, used)


def layer3_phase(nc, io, dram, keep, out):
    used = []
    ctx = ExitStack()
    with ctx:
        def sb(name, shape, dt=F32):
            return ctx.enter_context(nc.sbuf_tensor("r_" + name, shape, dt))

        def sem(name):
            used.append(ctx.enter_context(nc.semaphore("r_" + name)))
            return used[-1]

        def flags(name, n):
            made = [Flag(sem(f"{name}{i}")) for i in range(n)]
            primed.extend(made)
            return made

        primed = []
        x = keep["x"]
        SL, BK = 5, 4
        W = [sb(f"W{k}", [P, NB, P]) for k in range(SL)]
        X = sb("X", [P, 2, NB, D])
        tmp = sb("tmp", [P, NB, D])
        std = sb("std", [P, 4, NB])
        p_o = [ctx.enter_context(nc.psum_tensor(f"r_p_o{k}", [P, 512], F32)) for k in range(BK)]
        arrived = [sem(f"arrived{k}") for k in range(SL)]
        started, s_v, s_std, s_root, final, stored = sem("started"), sem("v"), sem("std"), sem("root"), sem("final"), sem("stored")
        summed, copied = flags("summed", NB), flags("copied", NB)
        block = ctx.enter_context(nc.Block())

        @block.sync
        def _(sp):
            for f in primed:
                sp.sem_inc(f.semaphore, 1)
            with sp.Fori(1, STEPS3 + 1) as n:
                for b in range(NB):
                    if b >= SL:
                        summed[b - SL].after(sp, n)
                    else:
                        summed[NB - SL + b].before(sp, n)
                    sp.dma_start(W[b % SL][:, :, :], dram["strips"][b, :, :].rearrange("p (d k) -> p d k", k=2 * P)[:, :, P:2 * P]
                                 ).then_inc(arrived[b % SL], 16)
            sp.wait_ge(final, 1)
            sp.dma_start(out[0:(NB - 1) * P, :].rearrange("(b p) f -> p b f", p=P), x[:, 0:NB - 1, :]).then_inc(stored, 16)
            sp.dma_start(out[(NB - 1) * P:N, :], x[0:LAST, NB - 1, :]).then_inc(stored, 16)
            sp.wait_ge(stored, 32)

        @block.tensor
        def _(pe):
            pe.wait_ge(started, 1)
            with pe.Fori(1, STEPS3 + 1) as n:
                copied[NB - 1].before(pe, n)
                for b in range(NB):
                    pe.wait_ge(arrived[b % SL], (n - 1) * (16 * NB // SL) + 16 * (b // SL + 1))
                    if b >= BK:
                        copied[b - BK].after(pe, n)
                    else:
                        copied[[j for j in range(NB) if j % BK == b][-1]].before(pe, n)
                    for d in range(NB):
                        m = nc.tensor.matmul(p_o[b % BK][:, 0:D], W[b % SL][:, d, :], X[:, bass.ds((n - 1) & 1, 1), d, :],
                                             start=(d == 0), stop=(d == NB - 1))
                    summed[b].set_by(m)

        @block.scalar
        def _(act):
            with act.Fori(1, STEPS3 + 1) as n:
                for b in range(NB):
                    summed[b].after(act, n)
                    copied[b].set_by(nc.scalar.copy(X[:, bass.ds(n & 1, 1), b, :].rearrange("p a c -> p (a c)"), p_o[b % BK][:, 0:D]))
            act.wait_ge(s_std, 1)
            nc.scalar.sqrt(std[:, 2, :], std[:, 1, :]).then_inc(s_root, 1)

        @block.vector
        def _(dve):
            V = nc.vector
            at = [0]

            def link(i):
                at[0] += 1
                i.then_inc(s_v, 1)
                dve.wait_ge(s_v, at[0])

            V.tensor_copy(X[:, 0, :, :], x[:, :, :]).then_inc(started, 1)
            copied[NB - 1].after(dve, STEPS3)
            r = X[:, STEPS3 & 1, :, :]
            link(V.tensor_tensor(r, r, x[:, :, :], ALU.add))
            layernorm(dve, V, link, x, r, tmp, std, s_std, s_root)
            dve.sem_inc(final, 1)
    clear(nc, used)


def sort_constants(np):
    r = np.arange(P)
    j, s = r // S, r % S
    same = s[:, None] == s[None, :]
    before = (s[:, None] < s[None, :]) & (j[:, None] == 0)
    mats = [r[:, None] == r[None, :], np.broadcast_to(r, (P, P)), r[:, None] > r[None, :],
            same, same & (j[:, None] < j[None, :]), before]
    return np.ascontiguousarray(np.stack(mats, 1).astype(np.float32))


_INS = ["x", "src", "dst", "edge_attr_16", "edge_attr_4", "edge_attr_8", "edge_weight",
        "L0_gnn_W1f", "L0_gnn_b1f", "L0_gnn_W2f", "L0_gnn_b2f", "L0_gnn_W1b", "L0_gnn_b1b", "L0_gnn_W2b", "L0_gnn_b2b",
        "L0_gnn_W1n", "L0_gnn_b1n", "L0_gnn_W2n", "L0_gnn_b2n",
        "L1_gnn_W1", "L1_gnn_b1", "L1_gnn_W2", "L1_gnn_b2", "L1_gnn_W3", "L1_gnn_b3", "L1_gnn_Ws", "L1_gnn_Wv"]


def build(nc, io, out):
    dram = {
        "edges": nc.dram_tensor("sorted_edges", (ROWS, REC), F32, kind="Internal").ap(),
        "table": nc.dram_tensor("body_table", (BODIES, TAB), I32, kind="Internal").ap(),
        "starts": nc.dram_tensor("block_starts", (S,), I32, kind="Internal").ap(),
        "strips": nc.dram_tensor("dense_strips", (NB, P, NB * 2 * P), F32, kind="Internal").ap(),
    }
    with ExitStack() as ctx:
        dram["sent"] = [ctx.enter_context(nc.semaphore(f"sent{k}")) for k in range(2)]
        dram["a_loaded"] = ctx.enter_context(nc.semaphore("a_loaded"))
        sort_phase(nc, io, dram, io["sort_consts"])
        with ExitStack() as inner:
            def sb(name, shape, dt=F32):
                return inner.enter_context(nc.sbuf_tensor(name, shape, dt))

            keep = {"x": sb("x", [P, NB, D]), "agg": sb("agg", [P, NB, 2 * D + 1]), "ident": sb("ident", [P, P])}
            with nc.sbuf_tensor("tab", [P, NB, 3, 4 * H1], BF16) as tab:
                keep["tab"] = tab
                load_nodes_phase(nc, io, keep)
                layer0_edges_phase(nc, io, dram, keep)
            with nc.sbuf_tensor("xp", [P, NB, 3, D], BF16) as xp:
                keep["xp"] = xp
                nodes_phase(nc, io, keep, 0)
                layer1_edges_phase(nc, io, dram, keep)
                nodes_phase(nc, io, keep, 1)
            layer2_phase(nc, io, dram, keep)
            layer3_phase(nc, io, dram, keep, out)


def kernel(**inputs):
    import numpy as np
    import concourse.bacc as bacc
    from concourse.bass_utils import run_bass_kernel_spmd

    nc = bacc.Bacc("TRN2", target_bir_lowering=False, num_devices=1)
    arrays = {name: np.ascontiguousarray(inputs[name]) for name in _INS}
    arrays["sort_consts"] = sort_constants(np)
    arrays["iota_t"] = np.ascontiguousarray(np.broadcast_to(np.arange(BODIES * TB, dtype=np.float32), (P, BODIES * TB)))
    io = {name: nc.dram_tensor(f"in_{name}", a.shape, mybir.dt.from_np(a.dtype), kind="ExternalInput").ap()
          for name, a in arrays.items()}
    out = nc.dram_tensor("out", (N, D), F32, kind="ExternalOutput").ap()
    build(nc, io, out)
    r = run_bass_kernel_spmd(nc, [{f"in_{name}": a for name, a in arrays.items()}], core_ids=[0])
    return r.results[0]["out"]
```

```python
import concourse.bass as bass
from concourse import mybir
from contextlib import ExitStack

F32 = mybir.dt.float32
BF16 = mybir.dt.bfloat16
F16 = mybir.dt.float16
I32 = mybir.dt.int32
ALU = mybir.AluOpType
ACT = mybir.ActivationFunctionType
AX = mybir.AxisListType

P = 128
N = 3125
E = 50000
D = 32
NB = -(-N // P)
NP = NB * P
LAST = N - (NB - 1) * P
EP = 125
EC = E // EP
J = 4
Q = EC // J
S = 32
G = 4
TB = 2 * G
TILES = E // P + NB * NB
U = 4 * TB // G
BODIES = (TILES + NB * (TB - 1)) // TB + U
ROWS = BODIES * TB * P
REC = 32
C16, C8, C4, CW, CR, CSRC, CDST = 0, 16, 24, 28, 29, 30, 31
TAB = 12
TSRC, TNEW = TB, TB + 2
TPACK = (TB + 1, TB + 3)
BITS = 5
BIG = 1.0e9
H1 = 64


def sort_phase(nc, io, dram, sort_consts):
    used = []
    ctx = ExitStack()
    with ctx:
        def sb(name, shape, dt):
            return ctx.enter_context(nc.sbuf_tensor("s_" + name, shape, dt))

        def ps(name, shape, dt=F32):
            return ctx.enter_context(nc.psum_tensor("s_" + name, shape, dt))

        def sem(name):
            used.append(ctx.enter_context(nc.semaphore("s_" + name)))
            return used[-1]

        cst = sb("cst", [P, 6, P], F32)
        IDENT, IOTA, LOWER, SAME, EARLIER, BEFORE = range(6)
        iota_t = sb("iota_t", [P, BODIES * TB], F32)
        ident16 = sb("ident16", [P, P], F16)
        ones = sb("ones", [P, 1], F32)
        onesq = sb("onesq", [P, Q], F32)
        src_i = sb("src_i", [EP, EC], I32)
        dst_i = sb("dst_i", [EP, EC], I32)
        blk_i = sb("blk_i", [EP, 2, EC], I32)
        blk = sb("blk", [EP, 2, EC], F32)
        loc_i = sb("loc_i", [EP, 2, EC], I32)
        loc = sb("loc", [EP, 2, EC], F32)
        key = sb("key", [EP, EC], F32)
        key16 = sb("key16", [EP, EC], F16)
        keyT = sb("keyT", [Q, J, EP], F16)
        ea16 = sb("ea16", [EP, EC, 16], F32)
        ea8 = sb("ea8", [EP, EC, 8], F32)
        ea4 = sb("ea4", [EP, EC, 4], F32)
        w = sb("w", [EP, EC], F32)
        w_hi = sb("w_hi", [EP, EC], BF16)
        w_rest = sb("w_rest", [EP, EC], F32)
        oh_src = sb("oh_src", [EP, Q, J, S], F16)
        oh_dst = sb("oh_dst", [EP, Q, J, NB], F16)
        hist = sb("hist", [P, Q, NB], F32)
        cum = sb("cum", [P, Q, NB], F32)
        cum_i = hist[:, :, :].bitcast(I32)
        part_i = [cum[:, :, :].bitcast(I32), cum_i]
        lookup = sb("lookup", [P, Q, 2, J, NB], F16)
        small = sb("small", [P, 12, NB], F32)
        small_i = sb("small_i", [P, 3, NB], I32)
        col = sb("col", [P, 8], F32)
        col_i = sb("col_i", [P, 2], I32)
        starts4 = sb("starts4", [P, 7], F32)
        count_t = hist[:, :, :].rearrange("p q d -> p (q d)")[:, 0:2 * BODIES * TB].rearrange("p (a t) -> p a t", a=2)
        count_b = sb("count_b", [P, BODIES], F32)
        tabrow = cum[0:1, :, :].rearrange("p q d -> p (q d)")[:, 0:BODIES * TAB].rearrange("p (b t) -> p b t", t=TAB)
        tabrow_i = sb("tabrow_i", [1, BODIES, TAB], I32)
        above_i = sb("above_i", [1, BODIES, 1], I32)
        bst_i = sb("bst_i", [1, S], I32)
        first = sb("first", [1, 16], F32)
        neg = sb("neg", [P, TB * REC], F32)
        rank = sb("rank", [EP, Q, J], F32)
        junk = sb("junk", [EP, J, EP], BF16)
        ohT = sb("ohT", [P, 4, EP], F16)
        prod = sb("prod", [EP, 2, 2, J * NB], F32)
        sel = sb("sel", [EP, 4, 2, J], F32)
        pos = sb("pos", [EP, 4, J], F32)
        pos_i = sb("pos_i", [EP, 5, 4 * J], I32)
        index = [sb(f"index{s}", [EP, 2 * J], I32) for s in range(2)]
        record = [sb(f"record{s}", [EP, 2 * J, REC], F32) for s in range(2)]

        p_rows = [ps(f"p_rows{i}", [P, J * EP]) for i in range(2)]
        p_t = ps("p_t", [P, 2, P], F16)
        p_h = [ps(f"p_h{i}", [P, 5, J, NB]) for i in range(2)]
        p_sm = ps("p_sm", [P, 512])

        s_idx, s_cst, s_att, s_neg = sem("s_idx"), sem("s_cst"), sem("s_att"), sem("s_neg")
        s_keyT = sem("s_keyT"); s_keyTs = sem("s_keyTs"); s_id16 = sem("s_id16"); s_key = sem("s_key")
        s_rows = sem("s_rows"); s_ranked = sem("s_ranked")
        s_oh = sem("s_oh"); s_hist = sem("s_hist"); s_histed = sem("s_histed")
        s_tot = sem("s_tot"); s_totp = sem("s_totp")
        s_ready = sem("s_ready"); s_cnt = sem("s_cnt"); s_cntp = sem("s_cntp"); s_tab = sem("s_tab")
        s_bst = sem("s_bst"); s_out = sem("s_out"); s_negset = sem("s_negset")
        s_tr = sem("s_tr"); s_trc = sem("s_trc"); s_look = sem("s_look"); s_sel = sem("s_sel")
        s_index = [sem(f"s_index{s}") for s in range(2)]
        s_record = [sem(f"s_record{s}") for s in range(2)]
        s_sent = dram["sent"]
        s_free = [sem(f"s_free{s}") for s in range(2)]
        s_v = sem("s_v"); s_loc = sem("s_loc"); s_w = sem("s_w"); s_go = sem("s_go")
        block = ctx.enter_context(nc.Block())

        @block.sync
        def _(sp):
            sp.dma_start(src_i[:, :], io["src"].rearrange("(p c) -> p c", p=EP)).then_inc(s_idx, 16)
            sp.dma_start(cst[:, :, :], sort_consts).then_inc(s_cst, 16)
            sp.dma_start(iota_t[:, :], io["iota_t"]).then_inc(s_cst, 16)
            sp.dma_start(ea16[:, :, :], io["edge_attr_16"].rearrange("(p c) f -> p c f", p=EP)).then_inc(s_att, 16)
            sp.wait_ge(s_negset, 1)
            span = ROWS * REC // P
            sp.dma_start(dram["edges"].rearrange("(p r) c -> p (r c)", p=P).rearrange("p (k m) -> p k m", m=TB * REC),
                         neg[:, :].unsqueeze(1).to_broadcast([P, span // (TB * REC), TB * REC])).then_inc(s_neg, 16)
            sp.wait_ge(s_tab, 1)
            sp.dma_start(dram["table"].unsqueeze(0), tabrow_i[:, :, :]).then_inc(s_out, 16)
            sp.dma_start(dram["starts"].unsqueeze(0), bst_i[:, :]).then_inc(s_out, 16)
            sp.wait_ge(s_out, 32)

        @block.scalar
        def _(act):
            act.dma_start(dst_i[:, :], io["dst"].rearrange("(p c) -> p c", p=EP)).then_inc(s_idx, 16)
            act.dma_start(w[:, :], io["edge_weight"].rearrange("(p c) -> p c", p=EP)).then_inc(s_att, 16)
            act.dma_start(ea8[:, :, :], io["edge_attr_8"].rearrange("(p c) f -> p c f", p=EP)).then_inc(s_att, 16)
            act.dma_start(ea4[:, :, :], io["edge_attr_4"].rearrange("(p c) f -> p c f", p=EP)).then_inc(s_att, 16)
            act.wait_ge(s_keyT, 1)
            nc.scalar.copy(keyT[:, 0:2, :], p_t[0:Q, 0:2, 0:EP]).then_inc(s_keyTs, 1)
            act.wait_ge(s_keyT, 2)
            nc.scalar.copy(keyT[:, 2:4, :], p_t[0:Q, 0:2, 0:EP]).then_inc(s_keyTs, 1)
            act.wait_ge(s_att, 64)
            act.wait_ge(s_loc, 1)
            act.wait_ge(s_w, 1)
            with act.Fori(1, Q // 4 + 1) as n:
                act.wait_ge(s_trc, n)
                for h in range(2):
                    act.wait_ge(s_tr, 2 * n - 1 + h)
                    nc.scalar.copy(ohT[:, 2 * h:2 * h + 2, :], p_t[:, :, 0:EP]).then_inc(s_ready, 1)
                c0 = (n - 1) * 4 * J
                for s in range(2):
                    act.wait_ge(s_free[s], n + s)
                    c = c0 + s * 2 * J
                    k = bass.ds(c, 2 * J)
                    nc.scalar.copy(record[s][:, :, C16:C16 + 16], ea16[:, k, :])
                    nc.scalar.copy(record[s][:, :, C8:C8 + 8], ea8[:, k, :])
                    nc.scalar.copy(record[s][:, :, C4:C4 + 4], ea4[:, k, :])
                    nc.scalar.copy(record[s][:, :, CW], w[:, k])
                    nc.scalar.copy(record[s][:, :, CR], w_rest[:, k])
                    nc.scalar.copy(record[s][:, :, CSRC:CDST + 1].rearrange("p c k -> p k c"),
                                   loc[:, :, k]).then_inc(s_record[s], 1)

        @block.gpsimd
        def _(pool):
            nc.gpsimd.memset(neg[:, :], -1.0).then_inc(s_negset, 1)
            nc.gpsimd.memset(lookup[:, :, :, :, :], 0.0).then_inc(s_negset, 1)
            for s in range(2):
                pool.sem_inc(s_free[s], 1)
            pool.dma_start(first[:, :], io["iota_t"][0:1, 0:16]).then_inc(s_sent[1], 16)
            pool.wait_ge(s_neg, 16)
            with pool.Fori(1, Q // 4 + 1) as n:
                for s in range(2):
                    pool.wait_ge(s_index[s], n)
                    pool.wait_ge(s_record[s], n)
                    pool.sem_inc(s_go, 1)
                    for c in range(2 * J):
                        pool.indirect_dma_start(dram["edges"], bass.IndirectOffsetOnAxis(ap=index[s][:, c:c + 1], axis=0),
                                                record[s][:, c, :], None).then_inc(s_sent[s], 16)
                    pool.wait_ge(s_sent[1 - s], n * (2 * J * 16) if s else (n - 1) * (2 * J * 16) + 16)
                    pool.sem_inc(s_free[1 - s], 1)
            pool.wait_ge(s_sent[1], (Q // 4) * (2 * J * 16) + 16)

        @block.tensor
        def _(pe):
            pe.wait_ge(s_key, 1)
            pe.wait_ge(s_id16, 1)
            kv = key16[:, :].rearrange("p (q j) -> p j q", j=J)
            for h in range(2):
                if h:
                    pe.wait_ge(s_keyTs, 1)
                for j in range(2):
                    t = nc.tensor.transpose(p_t[0:Q, j, 0:EP], kv[:, 2 * h + j, :], ident16[0:EP, 0:EP])
                t.then_inc(s_keyT, 1)
            pe.wait_ge(s_keyTs, 2)
            pe.wait_ge(s_oh, 1)
            with pe.Fori(1, Q // 10 + 1) as n:
                for h in range(2):
                    pe.wait_ge(s_histed, 2 * n - 1 + h)
                    for k in range(5):
                        q = (n - 1) * 10 + h * 5 + k
                        m = nc.tensor.matmul(p_h[h][:, k, :, :], oh_src[:, bass.ds(q, 1), :, :], oh_dst[:, bass.ds(q, 1), :, :],
                                             start=(k == 0), stop=(k == 4), skip_group_check=True)
                    m.then_inc(s_hist, 1)
            pe.wait_ge(s_tot, 1)
            nc.tensor.matmul(p_sm[:, 0:NB], cst[:, SAME, :], small[:, 0, :], start=True, stop=True).then_inc(s_totp, 1)
            nc.tensor.matmul(p_sm[:, 32:32 + NB], cst[:, EARLIER, :], small[:, 0, :], start=True, stop=True).then_inc(s_totp, 1)
            pe.wait_ge(s_tot, 2)
            nc.tensor.matmul(p_sm[:, 64:65], cst[:, BEFORE, :], col[:, 1:2], start=True, stop=True).then_inc(s_totp, 1)
            with pe.Fori(1, Q // 2 + 1) as n:
                for h in range(2):
                    pe.wait_ge(s_ranked, 2 * n - 1 + h)
                    k = (n - 1) * 2 + h
                    nc.tensor.matmul(p_rows[h][0:EP, :], ident16[0:Q, bass.ds(k, 1)].to_broadcast([Q, EP]), keyT[:, :, :],
                                     start=True, stop=True).then_inc(s_rows, 1)
            pe.wait_ge(s_cnt, 1)
            pe.sem_inc(s_ready, 2)
            pe.sem_inc(s_trc, 1)
            with pe.Fori(1, Q // 4 + 1) as n:
                for h in range(2):
                    pe.wait_ge(s_ready, 2 * n + h)
                    for k in range(2):
                        q = (n - 1) * 4 + 2 * h + k
                        m = nc.tensor.transpose(p_t[:, k, 0:EP], oh_src[:, bass.ds(q, 1), :, :], ident16[0:EP, 0:EP])
                    m.then_inc(s_tr, 1)
                pe.wait_ge(s_ready, 2 * n + 2)
                for h in range(2):
                    pe.wait_ge(s_sel, 2 * n - 1 + h)
                    for k in range(2):
                        q = (n - 1) * 4 + 2 * h + k
                        m = nc.tensor.matmul(p_h[h][0:EP, 0:4, :, :].rearrange("p a j d -> p (a j d)")[:, k * 2 * J * NB:(k + 1) * 2 * J * NB],
                                             ohT[:, 2 * h + k, :], lookup[:, bass.ds(q, 1), :, :, :],
                                             start=(k == 0), stop=(k == 1), skip_group_check=True)
                    m.then_inc(s_look, 1)
                pe.sem_inc(s_trc, 1)
            pe.wait_ge(s_bst, 1)
            nc.tensor.matmul(p_sm[0:1, 128:128 + BODIES], ones[0:NB, :], count_b[0:NB, :], start=True, stop=True).then_inc(s_cntp, 1)
            for k in range(3):
                a, b = k * 56, min(BODIES, (k + 1) * 56)
                bank = (p_rows[0], p_rows[1], p_h[0])[k]
                flat = bank[:, :] if k < 2 else bank[:, :, :, :].rearrange("p a j d -> p (a j d)")
                m = nc.tensor.matmul(flat[0:1, 0:(b - a) * TB], ones[:, :], count_t[:, 0, a * TB:b * TB], start=True, stop=True)
                if k < 2:
                    m.then_inc(s_cntp, 1)
            nc.tensor.matmul(p_sm[0:1, 320:320 + S], col[0:S, 4:5], cst[0:S, IDENT, 0:S], start=True, stop=True).then_inc(s_cntp, 1)

        @block.vector
        def _(dve):
            chain = [0]

            def link(ins):
                chain[0] += 1
                ins.then_inc(s_v, 1)
                dve.wait_ge(s_v, chain[0])

            V = nc.vector
            dve.wait_ge(s_idx, 32)
            for k, ids in enumerate((src_i, dst_i)):
                V.tensor_scalar(blk_i[:, k, :], ids[:, :], 7, None, ALU.arith_shift_right)
                link(V.tensor_scalar(loc_i[:, k, :], ids[:, :], P - 1, None, ALU.bitwise_and))
            V.tensor_copy(loc[:, :, :], loc_i[:, :, :]).then_inc(s_loc, 1)
            link(V.tensor_copy(blk[:, :, :], blk_i[:, :, :]))
            link(V.scalar_tensor_tensor(key[:, :], blk[:, 0, :], float(S), blk[:, 1, :], ALU.mult, ALU.add))
            V.tensor_copy(key16[:, :], key[:, :]).then_inc(s_key, 1)
            dve.wait_ge(s_cst, 32)
            V.memset(ones[:, :], 1.0)
            V.memset(onesq[:, :], 1.0)
            V.tensor_copy(ident16[:, :], cst[:, IDENT, :]).then_inc(s_id16, 1)
            for k, (o, n) in enumerate(((oh_src, S), (oh_dst, NB))):
                i = V.tensor_tensor(o[:, :, :, :].rearrange("p q j s -> p (q j) s"),
                                    cst[0:EP, IOTA, 0:n].unsqueeze(1).to_broadcast([EP, EC, n]),
                                    blk[:, k, :].unsqueeze(2).to_broadcast([EP, EC, n]), ALU.is_equal)
            i.then_inc(s_oh, 1)
            dve.wait_ge(s_att, 64)
            link(V.tensor_copy(w_hi[:, :], w[:, :]))
            V.tensor_tensor(w_rest[:, :], w[:, :], w_hi[:, :], ALU.subtract).then_inc(s_w, 1)
            dve.sem_inc(s_histed, 2)
            with dve.Fori(1, Q // 10 + 1) as n:
                for h in range(2):
                    dve.wait_ge(s_hist, 2 * n - 1 + h)
                    for j in range(J):
                        i = V.tensor_copy(hist[S * j:S * j + S, bass.ds((n - 1) * 10 + 5 * h, 5), :], p_h[h][S * j:S * j + S, :, j, :])
                    i.then_inc(s_histed, 1)
            dve.wait_ge(s_histed, 2 * (Q // 10) + 2)
            TOT, NT, PRE, ST, B0 = 0, 1, 2, 3, 4
            V.tensor_reduce(small[:, TOT, :], hist[:, :, :].rearrange("p q d -> p d q"), AX.X, ALU.add).then_inc(s_tot, 1)
            dve.wait_ge(s_totp, 2)
            link(V.tensor_scalar(small[:, 5, :], p_sm[:, 0:NB], float(P - 1), None, ALU.add))
            link(V.tensor_copy(small_i[:, 0, :], small[:, 5, :]))
            link(V.tensor_scalar(small_i[:, 1, :], small_i[:, 0, :], 7, None, ALU.arith_shift_right))
            link(V.tensor_copy(small[:, NT, :], small_i[:, 1, :]))
            link(V.tensor_reduce(col[:, 0:1], small[:, NT, :], AX.X, ALU.add))
            link(V.tensor_scalar(col[:, 2:3], col[:, 0:1], float(TB - 1), float(TB), ALU.add, ALU.max))
            link(V.tensor_copy(col_i[:, 0:1], col[:, 2:3]))
            link(V.tensor_scalar(col_i[:, 1:2], col_i[:, 0:1], 3, None, ALU.arith_shift_right))
            V.tensor_copy(col[:, 1:2], col_i[:, 1:2]).then_inc(s_tot, 1)
            link(V.tensor_tensor_scan(small[:, 6, :], onesq[:, 0:NB], small[:, NT, :], 0.0, ALU.mult, ALU.add))
            link(V.tensor_tensor(small[:, PRE, :], small[:, 6, :], small[:, NT, :], ALU.subtract))
            dve.wait_ge(s_totp, 3)
            link(V.tensor_scalar(col[:, 3:4], p_sm[:, 64:65], float(TB), None, ALU.mult))
            link(V.tensor_copy(col[:, 4:5], p_sm[:, 64:65]))
            link(V.tensor_scalar(small[:, ST, :], small[:, PRE, :], col[:, 3:4], None, ALU.add))
            link(V.scalar_tensor_tensor(small[:, B0, :], small[:, ST, :], float(P), p_sm[:, 32:32 + NB], ALU.mult, ALU.add))
            link(V.tensor_copy(cum[:, 0, :], small[:, B0, :]))
            for d in range(NB):
                i = V.tensor_tensor_scan(cum[:, 1:Q, d], onesq[:, 0:Q - 1], hist[:, 0:Q - 1, d], small[:, B0, d:d + 1], ALU.mult, ALU.add)
            link(i)
            link(V.tensor_copy(cum_i, cum[:, :, :]))
            link(V.tensor_scalar(part_i[0], cum_i, 8, None, ALU.arith_shift_right))
            link(V.tensor_scalar(part_i[1], cum_i, 255, None, ALU.bitwise_and))
            dve.wait_ge(s_negset, 2)
            for h in range(2):
                for j in range(J):
                    i = V.tensor_copy(lookup[S * j:S * j + S, :, h, j, :], part_i[h][S * j:S * j + S, :, :])
            i.then_inc(s_cnt, 1)
            dve.sem_inc(s_ranked, 2)
            with dve.Fori(1, Q // 2 + 1) as n:
                for h in range(2):
                    dve.wait_ge(s_rows, 2 * n - 1 + h)
                    dve.wait_ge(s_ranked, 2 * n + h)
                    q = (n - 1) * 2 + h
                    for j in range(J):
                        i = V.scalar_tensor_tensor(junk[:, j, :], p_rows[h][0:EP, j * EP:(j + 1) * EP], key[:, bass.ds(q * J + j, 1)],
                                                   cst[0:EP, LOWER, 0:EP], ALU.is_equal, ALU.mult,
                                                   accum_out=rank[:, bass.ds(q, 1), j])
                    i.then_inc(s_ranked, 1)
            dve.wait_ge(s_ranked, Q + 2)
            dve.sem_inc(s_sel, 2)
            k0 = chain[0]
            with dve.Fori(1, Q // 4 + 1) as n:
                step = [0]

                def linkn(ins):
                    step[0] += 1
                    ins.then_inc(s_v, 1)
                    dve.wait_ge(s_v, (n - 1) * 10 + (k0 + step[0]))

                for h in range(2):
                    dve.wait_ge(s_look, 2 * n - 1 + h)
                    o = oh_dst[:, bass.ds((n - 1) * 4 + 2 * h, 2), :, :].rearrange("p q j d -> p q (j d)")
                    linkn(V.tensor_tensor(prod[:, :, :, :], p_h[h][0:EP, 0:4, :, :].rearrange("p (q a) j d -> p q a (j d)", a=2),
                                          o.unsqueeze(2).to_broadcast([EP, 2, 2, J * NB]), ALU.mult))
                    dve.sem_inc(s_sel, 1)
                    linkn(V.tensor_reduce(sel[:, 2 * h:2 * h + 2, :, :].rearrange("p q a j -> p (q a j)"),
                                          prod[:, :, :, :].rearrange("p q a (j d) -> p (q a j) d", d=NB), AX.X, ALU.add))
                linkn(V.scalar_tensor_tensor(pos[:, :, :], sel[:, :, 0, :], 256.0, sel[:, :, 1, :], ALU.mult, ALU.add))
                linkn(V.tensor_tensor(pos_i[:, 0, :].rearrange("p (q j) -> p q j", j=J), pos[:, :, :], rank[:, bass.ds((n - 1) * 4, 4), :], ALU.add))
                linkn(V.tensor_scalar(pos_i[:, 1, :], pos_i[:, 0, :], TB * P - 1, 7, ALU.bitwise_and, ALU.logical_shift_right))
                linkn(V.tensor_scalar(pos_i[:, 2, :], pos_i[:, 0, :], -(TB * P), None, ALU.bitwise_and))
                linkn(V.tensor_tensor(pos_i[:, 3, :], pos_i[:, 1, :], pos_i[:, 2, :], ALU.bitwise_or))
                linkn(V.tensor_scalar(pos_i[:, 4, :], pos_i[:, 0, :], P - 1, 3, ALU.bitwise_and, ALU.logical_shift_left))
                for s in range(2):
                    dve.wait_ge(s_free[s], n + s)
                    k = slice(s * 2 * J, (s + 1) * 2 * J)
                    V.tensor_tensor(index[s][:, :], pos_i[:, 3, k], pos_i[:, 4, k], ALU.bitwise_or).then_inc(s_index[s], 1)
            chain[0] = k0 + 10 * (Q // 4)
            link(V.memset(starts4[:, :], BIG))
            for j in range(J):
                n = len(range(j, NB, J))
                i = V.tensor_copy(starts4[S * j:S * j + NB, 0:n], small[S * j:S * j + NB, ST, j:NB:J])
            link(i)
            link(V.tensor_scalar(count_t[:, 0, :], iota_t[:, :], starts4[:, 0:1], None, ALU.is_ge))
            for k in range(1, 7):
                link(V.scalar_tensor_tensor(count_t[:, k % 2, :], iota_t[:, :], starts4[:, k:k + 1], count_t[:, 1 - k % 2, :], ALU.is_ge, ALU.add))
            V.tensor_scalar(count_b[:, :], iota_t[:, 0:BODIES], col[:, 4:5], None, ALU.is_ge).then_inc(s_bst, 1)
            tiles = BODIES * TB
            tv = tabrow[:, :, 0:TB].rearrange("a b t -> a b t")
            link(V.memset(tabrow[:, :, :], 0.0))
            dve.wait_ge(s_cntp, 4)
            link(V.tensor_scalar(tabrow[:, :, TB:TB + 1].rearrange("a b t -> a (b t)"), p_sm[0:1, 128:128 + BODIES], -1.0, None, ALU.add))
            link(V.tensor_scalar(tabrow[:, :, TB + 1:TB + 2], tabrow[:, :, TB:TB + 1], float(NB), 1.0, ALU.mult, ALU.add))
            for k in range(3):
                a, b = k * 56, min(BODIES, (k + 1) * 56)
                bank = (p_rows[0], p_rows[1], p_h[0])[k]
                flat = bank[:, :] if k < 2 else bank[:, :, :, :].rearrange("p a j d -> p (a j d)")
                i = V.tensor_tensor(tabrow[:, a:b, 0:TB], flat[0:1, 0:(b - a) * TB].rearrange("a (b t) -> a b t", t=TB),
                                    tabrow[:, a:b, TB + 1:TB + 2].to_broadcast([1, b - a, TB]), ALU.subtract)
            link(i)
            link(V.tensor_tensor(tabrow[:, 1:BODIES, TNEW:TNEW + 1], tabrow[:, 1:BODIES, TB:TB + 1],
                                 tabrow[:, 0:BODIES - 1, TB:TB + 1], ALU.subtract))
            for h, c in enumerate(TPACK):
                at = tabrow[:, :, c:c + 1]
                link(V.scalar_tensor_tensor(at, tabrow[:, :, G * h + 3:G * h + 4], float(1 << BITS), tabrow[:, :, G * h + 2:G * h + 3], ALU.mult, ALU.add))
                for t in (1, 0):
                    link(V.scalar_tensor_tensor(at, at, float(1 << BITS), tabrow[:, :, G * h + t:G * h + t + 1], ALU.mult, ALU.add))
            V.tensor_copy(bst_i[:, :], p_sm[0:1, 320:320 + S])
            link(V.tensor_copy(tabrow_i[:, :, :], tabrow[:, :, :]))
            link(V.tensor_scalar(above_i[:, :, :], tabrow_i[:, :, TSRC:TSRC + 1], G * BITS, None, ALU.logical_shift_left))
            for c in TPACK:
                i = V.tensor_tensor(tabrow_i[:, :, c:c + 1], tabrow_i[:, :, c:c + 1], above_i[:, :, :], ALU.bitwise_or)
            i.then_inc(s_tab, 1)
    clear(nc, used)


def clear(nc, semaphores):
    numbers = [x.num for x in semaphores]
    with nc.Block() as block:
        @block.sync
        def _(sp):
            sp.sem_clear(range(min(numbers), max(numbers) + 1))


class Flag:

    def __init__(self, semaphore):
        self.semaphore = semaphore

    def after(self, engine, n):
        engine.wait_ge(self.semaphore, n + 1)

    def before(self, engine, n):
        engine.wait_ge(self.semaphore, n)

    def set_by(self, instruction):
        instruction.then_inc(self.semaphore, 1)


def group(n, k):
    return n + k // U * U, k % U


class Counter:

    def __init__(self, semaphore):
        self.semaphore = semaphore

    def after(self, engine, n, s):
        engine.wait_ge(self.semaphore, n + (s + U))

    def before(self, engine, n, s, depth):
        engine.wait_ge(self.semaphore, n + (s + U - depth))

    def set_by(self, instruction):
        instruction.then_inc(self.semaphore, 1)


class Chain:

    def __init__(self, engine, sems, n, s):
        self.engine, self.sems, self.value, self.at = engine, sems, n + s, 0

    def link(self, instruction):
        semaphore = self.sems[self.at]
        self.at += 1
        instruction.then_inc(semaphore, 1)
        self.engine.wait_ge(semaphore, self.value)


def round_end(last):
    return ((last + 3) >> 2) * U + 1


def body_of(nc, n, s):
    if isinstance(n, int):
        return (n >> 1) + s // 2
    return nc.s_assert_within((n >> 1) + s // 2, 0, BODIES - 1,
                              skip_runtime_bounds_check_because="BODIES counts the round behind the last body too")


def blocks_of(nc, engine, table, n, s):
    c = TPACK[s % 2]
    packed = engine.value_load(table[0:1, bass.ds(body_of(nc, n, s), 1), c], min_val=0, max_val=(1 << (G + 1) * BITS) - 1)

    def block(value):
        return nc.s_assert_within(value, 0, NB - 1, skip_runtime_bounds_check_because="the sort wrote block numbers there")

    return block(packed >> (G * BITS)), [block((packed >> (BITS * t)) & ((1 << BITS) - 1)) for t in range(G)]


def in_turn(make, depth):
    made = [make(k) for k in range(depth)]
    return [made[s % depth] for s in range(U)]


def edges_of(dram):
    return dram["edges"].rearrange("(b p t) c -> b p (t c)", p=P, t=TB)


def load_nodes_phase(nc, io, keep):
    used = []
    ctx = ExitStack()
    with ctx:
        def sb(name, shape, dt):
            return ctx.enter_context(nc.sbuf_tensor("i_" + name, shape, dt))

        def sem(name):
            used.append(ctx.enter_context(nc.semaphore("i_" + name)))
            return used[-1]

        x, tab, ident = keep["x"], keep["tab"], keep["ident"]
        xT = sb("xT", [D, NP], F32)
        wsd = sb("wsd", [D, 4, H1], F32)
        rest = sb("rest", [P, 2, 4 * H1], F32)
        p_x = [ctx.enter_context(nc.psum_tensor(f"i_p_x{i}", [D, 4, P], F32)) for i in range(2)]
        p_y = [ctx.enter_context(nc.psum_tensor(f"i_p_y{i}", [P, 4 * H1], F32)) for i in range(2)]
        n_zero, n_load, n_w = sem("n_zero"), sem("n_load"), sem("n_w")
        n_t, n_tc, n_y, n_ys, n_v = sem("n_t"), sem("n_tc"), sem("n_y"), sem("n_ys"), sem("n_v")
        groups = [(b, min(4, NB - b)) for b in range(0, NB, 4)]
        block = ctx.enter_context(nc.Block())

        @block.sync
        def _(sp):
            sp.dma_start(ident[:, :], io["sort_consts"][:, 0, :]).then_inc(n_w, 16)
            wf, wb = io["L0_gnn_W1f"], io["L0_gnn_W1b"]
            for k, part in enumerate((wf[D:2 * D, :], wb[0:D, :], wf[0:D, :], wb[D:2 * D, :])):
                sp.dma_start(wsd[:, k, :], part).then_inc(n_w, 16)
            sp.wait_ge(n_zero, 1)
            sp.dma_start(x[:, 0:NB - 1, :], io["x"][0:(NB - 1) * P, :].rearrange("(b p) f -> p b f", p=P)).then_inc(n_load, 16)
            sp.dma_start(x[0:LAST, NB - 1, :], io["x"][(NB - 1) * P:N, :]).then_inc(n_load, 16)

        @block.tensor
        def _(pe):
            pe.wait_ge(n_load, 32)
            pe.wait_ge(n_w, 80)
            for g, (b0, nb) in enumerate(groups):
                if g >= 2:
                    pe.wait_ge(n_tc, g - 1)
                for k in range(nb):
                    i = nc.tensor.transpose(p_x[g % 2][:, k, :], x[:, b0 + k, :], ident[:, :])
                i.then_inc(n_t, 1)
            for b in range(NB):
                pe.wait_ge(n_tc, b // 4 + 1)
                if b >= 2:
                    pe.wait_ge(n_ys, b - 1)
                nc.tensor.matmul(p_y[b % 2][:, :], xT[:, b * P:(b + 1) * P], wsd[:, :, :], start=True, stop=True).then_inc(n_y, 1)

        @block.scalar
        def _(act):
            for g, (b0, nb) in enumerate(groups):
                act.wait_ge(n_t, g + 1)
                nc.scalar.copy(xT[:, b0 * P:(b0 + nb) * P], p_x[g % 2][:, 0:nb, :].rearrange("p k n -> p (k n)")).then_inc(n_tc, 1)

        @block.vector
        def _(dve):
            V = nc.vector
            V.memset(x[:, NB - 1, :], 0.0).then_inc(n_zero, 1)
            k = 0
            for b in range(NB):
                dve.wait_ge(n_y, b + 1)
                y, r = p_y[b % 2][:, :], rest[:, b % 2, :]
                V.tensor_copy(tab[:, b, 0, :], y).then_inc(n_v, 1)
                dve.wait_ge(n_v, k + 1)
                V.tensor_tensor(r, y, tab[:, b, 0, :], ALU.subtract).then_inc(n_ys, 1)
                dve.wait_ge(n_ys, b + 1)
                V.tensor_copy(tab[:, b, 1, :], r).then_inc(n_v, 1)
                dve.wait_ge(n_v, k + 2)
                V.tensor_tensor(tab[:, b, 2, :], r, tab[:, b, 1, :], ALU.subtract)
                k += 2
    clear(nc, used)


MEETS = (0, 1, 2, 0, 1, 0)


def cut_weights(dve, V, chain, whole, parts, at=0):
    steps = (lambda: V.tensor_copy(parts[:, 0, :], whole), lambda: V.tensor_tensor(whole, whole, parts[:, 0, :], ALU.subtract),
             lambda: V.tensor_copy(parts[:, 1, :], whole), lambda: V.tensor_tensor(parts[:, 2, :], whole, parts[:, 1, :], ALU.subtract))
    for k, step in enumerate(steps):
        step().then_inc(chain, 1)
        dve.wait_ge(chain, at + k + 1)


def layer0_edges_phase(nc, io, dram, keep):
    used = []
    ctx = ExitStack()
    with ctx:
        def sb(name, shape, dt):
            return ctx.enter_context(nc.sbuf_tensor("e_" + name, shape, dt))

        def ps(name, shape, dt=F32):
            return ctx.enter_context(nc.psum_tensor("e_" + name, shape, dt))

        def sem(name):
            used.append(ctx.enter_context(nc.semaphore("e_" + name)))
            return used[-1]

        def counter(name):
            primed.append(Counter(sem(name)))
            return primed[-1]

        primed = []
        tab, agg, ident = keep["tab"], keep["agg"], keep["ident"]
        slots = range(U)
        table = sb("table", [1, BODIES, TAB], I32)
        turns = sb("turns", [1, BODIES + 1, TAB], I32)
        starts = sb("starts", [1, S], I32)
        iota = sb("iota", [P, P], F32)
        iotab = sb("iotab", [P, P], BF16)
        identb = sb("identb", [P, P], BF16)
        w1e = sb("w1e", [6 * 16, 2, H1], F32)
        w1_parts = sb("w1_parts", [6 * 16, 3, 2 * H1], BF16)
        w1s = sb("w1s", [6 * 16, 2 * H1], BF16)
        b1 = sb("b1", [P, 1], F32)
        w2 = sb("w2", [P, 2, D], F32)
        b2 = sb("b2", [1, G, 2, D], F32)
        ones = sb("ones", [1, P], F32)
        zeros = sb("zeros", [P, 2 * P], F32)
        strip = sb("strip", [P, 3, NB, 2 * P], F32)
        spare = sb("spare", [1, 16], F32)
        rec = in_turn(lambda s: sb(f"rec{s}", [P, G, REC], F32), U)
        wmid = in_turn(lambda s: sb(f"wmid{s}", [P, G], BF16), 4)
        wlow = in_turn(lambda s: sb(f"wlow{s}", [P, G], F32), 4)
        oh = in_turn(lambda s: sb(f"oh{s}", [P, 2, G, P], BF16), U)
        ohw = in_turn(lambda s: sb(f"ohw{s}", [P, G, 3, P], BF16), 4)
        attr = in_turn(lambda s: sb(f"attr{s}", [P, G, 6, 16], BF16), 4)
        arest = in_turn(lambda s: sb(f"arest{s}", [P, G, 16], F32), 4)
        recT = in_turn(lambda s: sb(f"recT{s}", [6 * 16, G * P], BF16), 2)
        ohT = in_turn(lambda s: sb(f"ohT{s}", [P, 2, G, P], BF16), 2)
        hid = in_turn(lambda s: sb(f"hid{s}", [P, G, P], F32), 2)
        flow = in_turn(lambda s: sb(f"flow{s}", [P, G, 2 * D], F32), 2)
        rest = in_turn(lambda s: sb(f"rest{s}", [P, G, 2 * D], F32), 2)
        part = in_turn(lambda s: sb(f"part{s}", [P, G, 3, 2 * D + 2], BF16), 4)
        p_rec = ps("p_rec", [6 * 16, G, P], BF16)
        p_oh = ps("p_oh", [P, 2, G, P], BF16)
        p_hid = ps("p_hid", [P, G * P])
        p_flow = ps("p_flow", [P, G, 2 * D])
        p_sum = ps("p_sum", [P, G + 1, 2 * D])
        p_aw = [ps(f"p_aw{i}", [P, 2, 2 * P]) for i in range(2)]

        loaded = [sem(f"loaded{s}") for s in slots]
        w_chain = sem("w_chain")
        d_const, d_w, d_b, d_start, d_flush, d_zero = sem("d_const"), sem("d_w"), sem("d_b"), sem("d_start"), sem("d_flush"), sem("d_zero")
        prime = sem("prime")
        setup = sem("setup")
        onehots, turned = counter("onehots"), counter("turned")
        recT_copied, ohT_copied = counter("recT_copied"), counter("ohT_copied")
        hid_done, hid_relued = counter("hid_done"), counter("hid_relued")
        aw_done, aw_added = ([counter(f"{name}{u}") for u in range(2)] for name in ("aw_done", "aw_added"))
        flow_cut, hi_cut = counter("flow_cut"), counter("hi_cut")
        flow_done = counter("flow_done")
        split, sum_done, sum_added = counter("split"), counter("sum_done"), counter("sum_added")
        weighted = counter("weighted")
        attr_hi, attr_rest, attr_mid, attr_cut = counter("attr_hi"), counter("attr_rest"), counter("attr_mid"), counter("attr_cut")
        rest_cut, mid_cut = counter("rest_cut"), counter("mid_cut")
        pool_chain = [sem(f"pool_chain{i}") for i in range(2)]
        dve_chain = [sem(f"dve_chain{i}") for i in range(6)]
        block = ctx.enter_context(nc.Block())
        ev = edges_of(dram)

        @block.sync
        def _(sp):
            for f in primed:
                sp.sem_inc(f.semaphore, U)
            sp.dma_start(table[:, :, :], dram["table"].unsqueeze(0)).then_inc(d_start, 16)
            sp.dma_start(turns[:, 1:BODIES + 1, :], dram["table"].unsqueeze(0)).then_inc(d_start, 16)
            sp.dma_start(turns[:, 0:1, :], dram["table"][0:1, :].unsqueeze(0)).then_inc(d_start, 16)
            sp.dma_start(starts[:, :], dram["starts"].unsqueeze(0)).then_inc(d_start, 16)
            sp.dma_start(iota[:, :], io["sort_consts"][:, 1, :]).then_inc(d_const, 16)
            sp.dma_start(spare[:, :], io["sort_consts"][0:1, 1, 0:16]).then_inc(d_flush, 16)
            sp.wait_ge(setup, 1)
            for k, (wn, name) in enumerate(((1, "f"), (0, "b"))):
                for i in range(6):
                    sp.dma_start(w1e[16 * i:16 * i + 16, k, :], io["L0_gnn_W1" + name][2 * D:2 * D + 16, :]).then_inc(d_b, 16)
                sp.dma_start(b1[k * H1:(k + 1) * H1, :], io["L0_gnn_b1" + name].unsqueeze(1)).then_inc(d_b, 16)
                sp.dma_start(w2[k * H1:(k + 1) * H1, wn, :], io["L0_gnn_W2" + name]).then_inc(d_b, 16)
                sp.dma_start(b2[:, :, wn, :], io["L0_gnn_b2" + name].unsqueeze(0).unsqueeze(0).to_broadcast([1, G, D])).then_inc(d_b, 16)
            sp.wait_ge(w_chain, 4)
            for i, k in enumerate(MEETS):
                sp.dma_start(w1s[16 * i:16 * i + 16, :], w1_parts[16 * i:16 * i + 16, k, :]).then_inc(d_w, 16)
            zs = zeros[:, :].unsqueeze(1).to_broadcast([P, NB, 2 * P])
            for k in range(2):
                sp.dma_start(strip[:, k, :, :], zs).then_inc(d_zero, 16)
                sp.wait_ge(d_zero, 16 * (k + 1))
            sp.wait_ge(d_start, 64)
            last = sp.value_load(starts[0:1, NB:NB + 1], min_val=NB, max_val=BODIES - U)

            def one_strip(k):
                return strip[:, bass.ds(k % 3, 1), :, :]

            with sp.Fori(1, round_end(last) + U, U) as n:
                for s in slots:
                    onehots.before(sp, n, s, U)
                    weighted.before(sp, n, s, U)
                    attr_rest.before(sp, n, s, U)
                    body = body_of(nc, n, s)
                    sp.dma_start(rec[s][:, :, :].rearrange("p t c -> p (t c)"),
                                 ev[bass.ds(body, 1), :, (s % 2) * G * REC:(s % 2 + 1) * G * REC].rearrange("b p c -> p (b c)")).then_inc(loaded[s], 16)
                    if s % 2 == 0:
                        continue
                    new = sp.value_load(turns[0:1, bass.ds(body, 1), TNEW], min_val=0, max_val=1)
                    with sp.If(new):
                        src = sp.value_load(turns[0:1, bass.ds(body, 1), TSRC], min_val=1, max_val=NB - 1)
                        aw_added[1].before(sp, n, s - 3, 1)
                        sp.sem_inc(prime, 1)
                        sp.wait_ge(d_flush, src * 16)
                        sp.sem_inc(prime, 1)
                        sp.dma_start(dram["strips"][bass.ds(src - 1, 1), :, :].rearrange("a p x -> p (a x)"),
                                     one_strip(src - 1).rearrange("p a b c -> p (a b c)")).then_inc(d_flush, 16)
                        sp.wait_ge(d_zero, src * 16 + 16)
                        sp.sem_inc(prime, 1)
                        sp.dma_start(one_strip(src + 1).rearrange("p a b c -> p (a b) c"), zs).then_inc(d_zero, 16)
            for s in slots:
                sp.wait_ge(loaded[s], round_end(last) * 2 + 14)
                sp.sem_inc(prime, 1)
            aw_added[1].after(sp, round_end(last), 1)
            sp.sem_inc(prime, 1)
            sp.wait_ge(d_flush, NB * 16)
            sp.dma_start(dram["strips"][NB - 1, :, :], strip[:, (NB - 1) % 3, :, :].rearrange("p b c -> p (b c)")).then_inc(d_flush, 16)
            sp.wait_ge(d_flush, NB * 16 + 16)
            sp.wait_ge(d_zero, NB * 16 + 16)

        @block.gpsimd
        def _(pool):
            g = nc.gpsimd
            pool.wait_ge(d_start, 64)
            last = pool.value_load(starts[0:1, NB:NB + 1], min_val=NB, max_val=BODIES - U)

            def weigh(n, s):
                onehots.after(pool, n, s)
                aw_done[1].before(pool, n, s, 4)
                pool.sem_inc(prime, 1)
                g.tensor_copy(wmid[s][:, :], rec[s][:, :, CR]).then_inc(pool_chain[0], 1)
                pool.wait_ge(pool_chain[0], n + s)
                g.tensor_tensor(wlow[s][:, :], rec[s][:, :, CR], wmid[s][:, :], ALU.subtract).then_inc(pool_chain[1], 1)
                pool.wait_ge(pool_chain[1], n + s)
                for k, w in enumerate((rec[s][:, :, CW], rec[s][:, :, CR], wlow[s][:, :])):
                    i = g.tensor_tensor(ohw[s][:, :, k, :], oh[s][:, 0, :, :], w.unsqueeze(2).to_broadcast([P, G, P]), ALU.mult)
                weighted.set_by(i)

            def attributes_rest(n, s):
                attr_hi.after(pool, n, s)
                pool.sem_inc(prime, 1)
                attr_rest.set_by(g.tensor_tensor(arest[s][:, :, :], rec[s][:, :, C16:C16 + 16], attr[s][:, :, 0, :], ALU.subtract))

            def attributes_low(n, s):
                attr_mid.after(pool, n, s)
                pool.sem_inc(prime, 1)
                attr_cut.set_by(g.tensor_tensor(attr[s][:, :, 5, :], arest[s][:, :, :], attr[s][:, :, 3, :], ALU.subtract))

            def flow_rest(n, s):
                hi_cut.after(pool, n, s)
                pool.sem_inc(prime, 1)
                rest_cut.set_by(g.tensor_tensor(rest[s][:, :, :], flow[s][:, :, :], part[s][:, :, 0, 0:2 * D], ALU.subtract))

            def flow_low(n, s):
                mid_cut.after(pool, n, s)
                pool.sem_inc(prime, 1)
                split.set_by(g.tensor_tensor(part[s][:, :, 2, 0:2 * D], rest[s][:, :, :], part[s][:, :, 1, 0:2 * D], ALU.subtract))

            pool.wait_ge(setup, 2)
            for s in range(4):
                attributes_rest(1, s); attributes_low(1, s)
            weigh(1, 0); weigh(1, 1); weigh(1, 2); flow_rest(1, 0); flow_low(1, 0)
            with pool.Fori(1, round_end(last), U) as n:
                for j in slots:
                    attributes_rest(*group(n, j + 4))
                    flow_rest(*group(n, j + 1))
                    attributes_low(*group(n, j + 4))
                    flow_low(*group(n, j + 1))
                    weigh(*group(n, j + 3))

        @block.scalar
        def _(act):
            act.wait_ge(d_start, 64)
            last = act.value_load(starts[0:1, NB:NB + 1], min_val=NB, max_val=BODIES - U)
            act.wait_ge(d_b, 288)

            def copies(n, s):
                turned.after(act, n, s)
                hid_done.before(act, n, s, 2)
                recT_copied.set_by(nc.scalar.copy(recT[s][:, :], p_rec[:, :, :].rearrange("p t e -> p (t e)")))
                ohT_copied.set_by(nc.scalar.copy(ohT[s][:, :, :, :], p_oh[:, :, :, :]))

            def attributes(n, s):
                act.wait_ge(loaded[s], n * 2 + 14)
                turned.before(act, n, s, 4)
                act.sem_inc(prime, 1)
                wide = [P, G, 3, 16]
                attr_hi.set_by(nc.scalar.copy(attr[s][:, :, 0:3, :], rec[s][:, :, C16:C16 + 16].unsqueeze(2).to_broadcast(wide)))
                attr_rest.after(act, n, s)
                attr_mid.set_by(nc.scalar.copy(attr[s][:, :, 3:5, :], arest[s][:, :, :].unsqueeze(2).to_broadcast([P, G, 2, 16])))

            def middle(n, s):
                rest_cut.after(act, n, s)
                mid_cut.set_by(nc.scalar.copy(part[s][:, :, 1, 0:2 * D], rest[s][:, :, :]))

            def relu1(n, s):
                hid_done.after(act, n, s)
                flow_done.before(act, n, s, 2)
                hid_relued.set_by(nc.scalar.activation(hid[s][:, :, :].rearrange("p t e -> p (t e)"), p_hid[:, :], ACT.Relu, bias=b1[:, :]))

            def relu2(n, s):
                flow_done.after(act, n, s)
                rest_cut.before(act, n, s, 2)
                sum_done.before(act, n, s, 4)
                flow_cut.set_by(nc.scalar.activation(flow[s][:, :, :], p_flow[:, :, :], ACT.Relu))
                hi_cut.set_by(nc.scalar.activation(part[s][:, :, 0, 0:2 * D], p_flow[:, :, :], ACT.Relu))

            act.wait_ge(setup, 2)
            for s in range(4):
                attributes(1, s)
            copies(1, 0)
            copies(1, 1); relu1(1, 0)
            copies(1, 2); relu1(1, 1); relu2(1, 0); middle(1, 0)
            with act.Fori(1, round_end(last), U) as n:
                for j in slots:
                    relu1(*group(n, j + 2))
                    attributes(*group(n, j + 4))
                    relu2(*group(n, j + 1))
                    middle(*group(n, j + 1))
                    copies(*group(n, j + 3))

        @block.tensor
        def _(pe):
            mm = nc.tensor.matmul
            pe.wait_ge(d_start, 64)
            last = pe.value_load(starts[0:1, NB:NB + 1], min_val=NB, max_val=BODIES - U)
            pe.wait_ge(d_b, 288)
            pe.wait_ge(d_w, 96)
            pe.wait_ge(setup, 2)

            def turn(n, s):
                attr_cut.after(pe, n, s)
                recT_copied.before(pe, n, s, 1)
                for t in range(G):
                    nc.tensor.transpose(p_rec[:, t, :], attr[s][:, t, :, :].rearrange("p k f -> p (k f)"), identb[:, :])
                onehots.after(pe, n, s)
                ohT_copied.before(pe, n, s, 1)
                for k in range(2):
                    for t in range(G):
                        i = nc.tensor.transpose(p_oh[:, k, t, :], oh[s][:, k, t, :], identb[:, :])
                turned.set_by(i)

            def hidden(n, s):
                src, dsts = blocks_of(nc, pe, table, n, s)
                hid_relued.before(pe, n, s, 1)
                recT_copied.after(pe, n, s)
                mm(p_hid[:, :], w1s[:, :], recT[s][:, :], start=True, stop=False, skip_group_check=True)
                ohT_copied.after(pe, n, s)
                for k in range(3):
                    mm(p_hid[:, :], tab[:, bass.ds(src, 1), k, 0:P], ohT[s][:, 0, :, :], start=False, stop=False, skip_group_check=True)
                for t in range(G):
                    for k in range(3):
                        i = mm(p_hid[:, t * P:(t + 1) * P], tab[:, bass.ds(dsts[t], 1), k, P:2 * P], ohT[s][:, 1, t, :],
                               start=False, stop=(t == G - 1 and k == 2), skip_group_check=True)
                hid_done.set_by(i)

            def dense(n, s):
                weighted.after(pe, n, s)
                for u in range(2):
                    aw_added[u].before(pe, n, s, 1)
                    for v in range(2):
                        t = 2 * u + v
                        mm(p_aw[u][:, v, 0:P], oh[s][:, 0, t, :], oh[s][:, 1, t, :], start=True, stop=True, skip_group_check=True)
                        for k in range(3):
                            i = mm(p_aw[u][:, v, P:2 * P], oh[s][:, 1, t, :], ohw[s][:, t, k, :], start=(k == 0), stop=(k == 2),
                                   skip_group_check=True)
                    aw_done[u].set_by(i)

            def second(n, s):
                hi_cut.before(pe, n, s, 1)
                mm(p_flow[:, :, :], ones[:, :], b2[:, :, :, :], start=True, stop=False, skip_group_check=True)
                hid_relued.after(pe, n, s)
                for t in range(G):
                    i = mm(p_flow[:, t, :], hid[s][:, t, :], w2[:, :, :], start=False, stop=(t == G - 1), skip_group_check=True)
                flow_done.set_by(i)

            def sums(n, s):
                sum_added.before(pe, n, s, 1)
                split.after(pe, n, s)
                for t in range(G):
                    for k in range(3):
                        mm(p_sum[:, G, 0:D], oh[s][:, 0, t, :], part[s][:, t, k, 0:D], start=(t == 0 and k == 0),
                           stop=(t == G - 1 and k == 2), skip_group_check=True)
                for t in range(G):
                    for k in range(3):
                        i = mm(p_sum[:, t, 0:D + 1], oh[s][:, 1, t, :], part[s][:, t, k, D:2 * D + 1], start=(k == 0), stop=(k == 2),
                               skip_group_check=True)
                sum_done.set_by(i)

            turn(1, 0)
            turn(1, 1); hidden(1, 0); dense(1, 0)
            turn(1, 2); hidden(1, 1); dense(1, 1); second(1, 0)
            with pe.Fori(1, round_end(last), U) as n:
                for j in slots:
                    hidden(*group(n, j + 2))
                    second(*group(n, j + 1))
                    sums(*group(n, j))
                    dense(*group(n, j + 2))
                    turn(*group(n, j + 3))

        @block.vector
        def _(dve):
            V = nc.vector
            V.memset(w2[:, :, :], 0.0)
            V.memset(ones[:, :], 1.0)
            V.memset(zeros[:, :], 0.0).then_inc(setup, 1)
            V.memset(agg[:, :, :], 0.0)
            for s in range(4):
                V.memset(part[s][:, :, :, :], 0.0).then_inc(dve_chain[s], 1)
                dve.wait_ge(dve_chain[s], 1)
                dve.sem_clear(dve_chain[s])
                V.memset(part[s][:, :, 0, 2 * D:2 * D + 1], 1.0)
            dve.wait_ge(d_const, 16)
            V.tensor_copy(iotab[:, :], iota[:, :])
            V.tensor_copy(identb[:, :], ident[:, :]).then_inc(setup, 1)
            dve.wait_ge(d_b, 288)
            cut_weights(dve, V, w_chain, w1e[:, :, :].rearrange("p k h -> p (k h)"), w1_parts)
            dve.wait_ge(setup, 2)
            dve.wait_ge(d_start, 64)
            last = dve.value_load(starts[0:1, NB:NB + 1], min_val=NB, max_val=BODIES - U)

            def one_hots(n, s):
                dve.wait_ge(loaded[s], n * 2 + 14)
                sum_done.before(dve, n, s, U)
                for t in range(G):
                    for k, c in enumerate((CSRC, CDST)):
                        i = V.tensor_scalar(oh[s][:, k, t, :], iotab[:, :], rec[s][:, t, c:c + 1], None, ALU.is_equal)
                onehots.set_by(i)

            def add_dense(n, s):
                src, dsts = blocks_of(nc, dve, table, n, s)
                turn = src % 3
                dve.wait_ge(d_zero, (src + 1) * 16)
                for u in range(2):
                    aw_done[u].after(dve, n, s)
                    for v in range(2):
                        at = strip[:, bass.ds(turn, 1), bass.ds(dsts[2 * u + v], 1), :].rearrange("p a b c -> p (a b c)")
                        i = V.tensor_tensor(at, p_aw[u][:, v, :], at, ALU.add)
                        if v:
                            aw_added[u].set_by(i)
                            aw_added[u].after(dve, n, s)
                        else:
                            i.then_inc(dve_chain[u], 1)
                            dve.wait_ge(dve_chain[u], n + s)

            def add_sums(n, s):
                dve.sem_inc(prime, 1)
                src, dsts = blocks_of(nc, dve, table, n, s)
                sum_done.after(dve, n, s)
                at = agg[:, bass.ds(src, 1), 0:D].rearrange("p a c -> p (a c)")
                V.tensor_tensor(at, p_sum[:, G, 0:D], at, ALU.add).then_inc(dve_chain[2], 1)
                for t in range(G):
                    at = agg[:, bass.ds(dsts[t], 1), D:2 * D + 1].rearrange("p a c -> p (a c)")
                    i = V.tensor_tensor(at, p_sum[:, t, 0:D + 1], at, ALU.add)
                    if t < G - 1:
                        i.then_inc(dve_chain[3 + t], 1)
                        dve.wait_ge(dve_chain[3 + t], n + s)
                    else:
                        sum_added.set_by(i)
                        sum_added.after(dve, n, s)

            for s in range(4):
                one_hots(1, s)
            add_dense(1, 0)
            dve.sem_inc(prime, 1)
            add_dense(1, 1)
            with dve.Fori(1, round_end(last), U) as n:
                for j in slots:
                    add_sums(*group(n, j))
                    one_hots(*group(n, j + 4))
                    add_dense(*group(n, j + 2))
    clear(nc, used)


EPS = 1e-5
RT3, ALPHA_MSG, ALPHA_SELF = 3.0 ** -0.5, 16.0 ** -0.5 / 16.0 ** 0.5, 8.0 ** -0.5
MUL = 8
H2 = 64
NTP = 4 * MUL * MUL
STEPS2, ALPHA2 = 10, 0.1
STEPS3 = 3


def layernorm(dve, V, link, x, r, tmp, std, std_ready, rooted):
    wide = [P, NB, D]
    link(V.tensor_reduce(std[:, 0, :], r[:, :, :], AX.X, ALU.add))
    link(V.tensor_scalar(std[:, 0, :], std[:, 0, :], 1.0 / D, None, ALU.mult))
    link(V.tensor_tensor(r[:, :, :], r[:, :, :], std[:, 0, :].unsqueeze(2).to_broadcast(wide), ALU.subtract))
    link(V.tensor_tensor(tmp[:, :, :], r[:, :, :], r[:, :, :], ALU.mult))
    link(V.tensor_reduce(std[:, 1, :], tmp[:, :, :], AX.X, ALU.add))
    V.tensor_scalar(std[:, 1, :], std[:, 1, :], 1.0 / D, EPS, ALU.mult, ALU.add).then_inc(std_ready, 1)
    dve.wait_ge(rooted, 1)
    link(V.reciprocal(std[:, 3, :], std[:, 2, :]))
    link(V.tensor_tensor(x[:, :, :], r[:, :, :], std[:, 3, :].unsqueeze(2).to_broadcast(wide), ALU.mult))


def nodes_phase(nc, io, keep, layer):
    used = []
    ctx = ExitStack()
    with ctx:
        def sb(name, shape, dt=F32):
            return ctx.enter_context(nc.sbuf_tensor(f"n{layer}_{name}", shape, dt))

        def sem(name):
            used.append(ctx.enter_context(nc.semaphore(f"n{layer}_{name}")))
            return used[-1]

        x, agg, ident, xp = keep["x"], keep["agg"], keep["ident"], keep["xp"]
        K = 2 * D if layer == 0 else D
        turned = sb("turned", [K, NP])
        w1 = sb("w1", [K, 2 * D])
        b1 = sb("b1", [2 * D, 1])
        z = sb("z", [2 * D + 1, NP])
        w2 = sb("w2", [2 * D + 1, D])
        r = sb("r", [P, NB, D])
        tmp = sb("tmp", [P, NB, D])
        std = sb("std", [P, 4, NB])
        p_t = [ctx.enter_context(nc.psum_tensor(f"n{layer}_p_t{i}", [K, 4, P], F32)) for i in range(2)]
        p_z = [ctx.enter_context(nc.psum_tensor(f"n{layer}_p_z{i}", [2 * D, 512], F32)) for i in range(2)]
        p_o = [ctx.enter_context(nc.psum_tensor(f"n{layer}_p_o{i}", [P, 16, D], F32)) for i in range(2)]
        s_w, s_t, s_tc, s_z, s_zc, s_o, s_v = sem("w"), sem("t"), sem("tc"), sem("z"), sem("zc"), sem("o"), sem("v")
        s_std, s_root, s_zero = sem("std"), sem("root"), sem("zero")
        groups = [(b, min(4, NB - b)) for b in range(0, NB, 4)]
        halves = [(0, 16), (16, NB - 16)]
        loads = 5 if layer == 0 else 4
        block = ctx.enter_context(nc.Block())

        @block.sync
        def _(sp):
            if layer == 0:
                sp.dma_start(w1[0:D, :], io["L0_gnn_W1n"][D:2 * D, :]).then_inc(s_w, 16)
                sp.dma_start(w1[D:2 * D, :], io["L0_gnn_W1n"][0:D, :]).then_inc(s_w, 16)
                sp.dma_start(b1[:, :], io["L0_gnn_b1n"].unsqueeze(1)).then_inc(s_w, 16)
                sp.dma_start(w2[0:2 * D, :], io["L0_gnn_W2n"]).then_inc(s_w, 16)
                sp.dma_start(w2[2 * D:2 * D + 1, :], io["L0_gnn_b2n"].unsqueeze(0)).then_inc(s_w, 16)
            else:
                sp.wait_ge(s_zero, 1)
                sp.dma_start(w1[0:MUL, 0:MUL], io["L1_gnn_Ws"]).then_inc(s_w, 16)
                for i in range(3):
                    sp.dma_start(w1[MUL + i:D:3, MUL + i:D:3], io["L1_gnn_Wv"], allow_slow_non_contiguous=True).then_inc(s_w, 16)

        @block.tensor
        def _(pe):
            what = agg if layer == 0 else x
            for g, (b0, nb) in enumerate(groups):
                if g >= 2:
                    pe.wait_ge(s_tc, g - 1)
                for k in range(nb):
                    i = nc.tensor.transpose(p_t[g % 2][:, k, :], what[:, b0 + k, 0:K], ident[:, :])
                i.then_inc(s_t, 1)
            pe.wait_ge(s_w, 16 * loads)
            pe.wait_ge(s_tc, len(groups))
            if layer == 0:
                for g, (b0, nb) in enumerate(groups):
                    if g >= 2:
                        pe.wait_ge(s_zc, g - 1)
                    nc.tensor.matmul(p_z[g % 2][:, 0:nb * P], w1[:, :], turned[:, b0 * P:(b0 + nb) * P], start=True, stop=True).then_inc(s_z, 1)
                pe.wait_ge(s_zc, len(groups))
                pe.wait_ge(s_zero, 1)
            for h, (b0, nb) in enumerate(halves):
                for k in range(nb):
                    at = slice((b0 + k) * P, (b0 + k + 1) * P)
                    if layer == 0:
                        i = nc.tensor.matmul(p_o[h][:, k, :], z[:, at], w2[:, :], start=True, stop=True, skip_group_check=True)
                    else:
                        i = nc.tensor.matmul(p_o[h][:, k, :], turned[:, at], w1[:, 0:D], start=True, stop=True, skip_group_check=True)
                i.then_inc(s_o, 1)

        @block.scalar
        def _(act):
            for g, (b0, nb) in enumerate(groups):
                act.wait_ge(s_t, g + 1)
                nc.scalar.copy(turned[:, b0 * P:(b0 + nb) * P], p_t[g % 2][:, 0:nb, :].rearrange("p k n -> p (k n)")).then_inc(s_tc, 1)
            if layer == 0:
                act.wait_ge(s_w, 16 * loads)
                for g, (b0, nb) in enumerate(groups):
                    act.wait_ge(s_z, g + 1)
                    nc.scalar.activation(z[0:2 * D, b0 * P:(b0 + nb) * P], p_z[g % 2][:, 0:nb * P], ACT.Relu, bias=b1[:, :]).then_inc(s_zc, 1)
            act.wait_ge(s_std, 1)
            nc.scalar.sqrt(std[:, 2, :], std[:, 1, :]).then_inc(s_root, 1)

        @block.vector
        def _(dve):
            V = nc.vector
            at = [0]

            def link(i):
                at[0] += 1
                i.then_inc(s_v, 1)
                dve.wait_ge(s_v, at[0])

            if layer == 0:
                V.memset(z[2 * D:2 * D + 1, :], 1.0).then_inc(s_zero, 1)
            else:
                V.memset(w1[:, :], 0.0).then_inc(s_zero, 1)
            for h, (b0, nb) in enumerate(halves):
                dve.wait_ge(s_o, h + 1)
                b = slice(b0, b0 + nb)
                if layer == 0:
                    link(V.scalar_tensor_tensor(r[:, b, :], p_o[h][:, 0:nb, :], 0.0, x[:, b, :], ALU.max, ALU.add))
                else:
                    link(V.scalar_tensor_tensor(r[:, b, :], p_o[h][:, 0:nb, :], ALPHA_SELF, x[:, b, :], ALU.mult, ALU.add))
                    link(V.scalar_tensor_tensor(r[:, b, :], agg[:, b, 0:D], ALPHA_MSG, r[:, b, :], ALU.mult, ALU.add))
            layernorm(dve, V, link, x, r, tmp, std, s_std, s_root)
            if layer == 0:
                link(V.tensor_copy(xp[:, :, 0, :], x[:, :, :]))
                link(V.tensor_tensor(r[:, :, :], x[:, :, :], xp[:, :, 0, :], ALU.subtract))
                link(V.tensor_copy(xp[:, :, 1, :], r[:, :, :]))
                link(V.tensor_tensor(xp[:, :, 2, :], r[:, :, :], xp[:, :, 1, :], ALU.subtract))
    clear(nc, used)


def layer1_edges_phase(nc, io, dram, keep):
    used = []
    ctx = ExitStack()
    with ctx:
        def sb(name, shape, dt=F32):
            return ctx.enter_context(nc.sbuf_tensor("m_" + name, shape, dt))

        def ps(name, shape, dt=F32):
            return ctx.enter_context(nc.psum_tensor("m_" + name, shape, dt))

        def sem(name):
            used.append(ctx.enter_context(nc.semaphore("m_" + name)))
            return used[-1]

        def counter(name):
            primed.append(Counter(sem(name)))
            return primed[-1]

        primed = []
        xp, agg, ident = keep["xp"], keep["agg"], keep["ident"]
        slots = range(U)
        table = sb("table", [1, BODIES, TAB], I32)
        starts = sb("starts", [1, S], I32)
        iota = sb("iota", [P, P])
        iotab = sb("iotab", [P, P], BF16)
        rt3 = sb("rt3", [P, G, 3])
        identb = sb("identb", [P, P], BF16)
        w1 = sb("w1", [6 * MUL, 2, H2])
        b1 = sb("b1", [2 * H2, 1])
        w2 = sb("w2", [H2, 2, H2])
        b2 = sb("b2", [2 * H2, 1])
        w3 = sb("w3", [H2, NTP])
        b3 = sb("b3", [3, NTP])
        w1_parts = sb("w1_parts", [6 * MUL, 3, 2 * H2], BF16)
        w2_parts = sb("w2_parts", [H2, 3, 2 * H2], BF16)
        w3_parts = sb("w3_parts", [H2, 3, NTP], BF16)
        b3_parts = sb("b3_parts", [3, 3, NTP], BF16)
        w1s = sb("w1s", [6 * MUL, 2 * H2], BF16)
        w2s = sb("w2s", [2 * H2, 2 * H2], BF16)
        w3s = sb("w3s", [2 * H2, NTP], BF16)
        b3s = sb("b3s", [3, NTP], BF16)
        ones3 = sb("ones3", [3, P], BF16)
        rec = in_turn(lambda s: sb(f"rec{s}", [P, G, REC]), U)
        oh = in_turn(lambda s: sb(f"oh{s}", [P, 2, G, P], BF16), U)
        attr = in_turn(lambda s: sb(f"attr{s}", [P, G, 6, MUL], BF16), 2)
        arest = in_turn(lambda s: sb(f"arest{s}", [P, G, MUL]), 2)
        recT = in_turn(lambda s: sb(f"recT{s}", [6 * MUL, G * P], BF16), 2)
        ohT = in_turn(lambda s: sb(f"ohT{s}", [P, G, P], BF16), 2)
        node = in_turn(lambda s: sb(f"node{s}", [P, G, D]), 4)
        h = [in_turn(lambda s: sb(f"h{k}_{s}", [2 * H2, G * P]), 2) for k in range(2)]
        hrest = [in_turn(lambda s: sb(f"hrest{k}_{s}", [2 * H2, G * P]), 2) for k in range(2)]
        hpart = [in_turn(lambda s: sb(f"hpart{k}_{s}", [2 * H2, 3, G * P], BF16), 2) for k in range(2)]
        coef = in_turn(lambda s: sb(f"coef{s}", [P, G, 2 * MUL]), 4)
        sh3 = in_turn(lambda s: sb(f"sh3{s}", [P, G, 3]), 4)
        dots = in_turn(lambda s: sb(f"dots{s}", [P, G, MUL, 3]), 4)
        vec0 = in_turn(lambda s: sb(f"vec0{s}", [P, G, MUL, 3]), 4)
        prod0 = sb("prod0", [P, G, 2 * MUL, MUL])
        prod1 = sb("prod1", [P, G, MUL, MUL])
        prod2 = sb("prod2", [P, 3, G, MUL, MUL])
        sum1 = sb("sum1", [P, G, MUL])
        sum2 = sb("sum2", [P, 3, G, MUL])
        outer = sb("outer", [P, G, MUL, 3])
        msg = in_turn(lambda s: sb(f"msg{s}", [P, G, D]), 2)
        rest = in_turn(lambda s: sb(f"rest{s}", [P, G, D]), 2)
        part = in_turn(lambda s: sb(f"part{s}", [P, G, 3, D], BF16), 2)
        p_rec = ps("p_rec", [6 * MUL, G, P], BF16)
        p_oh = ps("p_oh", [P, G, P], BF16)
        p_node = ps("p_node", [P, G, D])
        p_h = [ps(f"p_h{k}", [2 * H2, G * P]) for k in range(2)]
        p_w = ps("p_w", [P, G, NTP])
        p_sum = ps("p_sum", [P, G, D])

        loaded = [sem(f"loaded{s}") for s in slots]
        d_start, d_const, setup, prime = sem("d_start"), sem("d_const"), sem("setup"), sem("prime")
        onehots, turned = counter("onehots"), counter("turned")
        recT_copied, ohT_copied = counter("recT_copied"), counter("ohT_copied")
        node_done, node_copied, made_coef = counter("node_done"), counter("node_copied"), counter("made_coef")
        attr_hi, attr_rest, attr_mid, attr_cut = counter("attr_hi"), counter("attr_rest"), counter("attr_mid"), counter("attr_cut")
        h_done, h_hi, h_rest, h_mid, h_cut = ([counter(f"{name}{k}") for k in range(2)] for name in ("h_done", "h_hi", "h_rest", "h_mid", "h_cut"))
        w_done, w_read = counter("w_done"), counter("w_read")
        split, sum_done, sum_added = counter("split"), counter("sum_done"), counter("sum_added")
        dve_chain = [sem(f"dve_chain{i}") for i in range(12)]
        pool_chain = sem("pool_chain")
        w_chain, d_w = sem("w_chain"), sem("d_w")
        D_CONST = 16 * 21
        block = ctx.enter_context(nc.Block())
        ev = edges_of(dram)

        @block.sync
        def _(sp):
            for f in primed:
                sp.sem_inc(f.semaphore, U)
            sp.dma_start(table[:, :, :], dram["table"].unsqueeze(0)).then_inc(d_start, 16)
            sp.dma_start(starts[:, :], dram["starts"].unsqueeze(0)).then_inc(d_start, 16)
            sp.dma_start(iota[:, :], io["sort_consts"][:, 1, :]).then_inc(d_const, 16)
            for k in range(2):
                for i in range(6):
                    sp.dma_start(w1[MUL * i:MUL * i + MUL, k, :], io["L1_gnn_W1"]).then_inc(d_const, 16)
                sp.dma_start(b1[H2 * k:H2 * k + H2, :], io["L1_gnn_b1"].unsqueeze(1)).then_inc(d_const, 16)
                sp.dma_start(w2[:, k, :], io["L1_gnn_W2"]).then_inc(d_const, 16)
                sp.dma_start(b2[H2 * k:H2 * k + H2, :], io["L1_gnn_b2"].unsqueeze(1)).then_inc(d_const, 16)
            sp.dma_start(w3[:, :], io["L1_gnn_W3"]).then_inc(d_const, 16)
            sp.dma_start(b3[:, :], io["L1_gnn_b3"].unsqueeze(0).to_broadcast([3, NTP])).then_inc(d_const, 16)
            sp.wait_ge(w_chain, 16)
            for i, k in enumerate(MEETS):
                sp.dma_start(w1s[MUL * i:MUL * i + MUL, :], w1_parts[MUL * i:MUL * i + MUL, k, :]).then_inc(d_w, 16)
            for k in range(2):
                sp.dma_start(w2s[H2 * k:H2 * k + H2, :], w2_parts[:, k, :]).then_inc(d_w, 16)
                sp.dma_start(w3s[H2 * k:H2 * k + H2, :], w3_parts[:, k, :]).then_inc(d_w, 16)
            for k in range(3):
                sp.dma_start(b3s[k:k + 1, :], b3_parts[k:k + 1, k, :]).then_inc(d_w, 16)
            sp.wait_ge(d_start, 32)
            last = sp.value_load(starts[0:1, NB:NB + 1], min_val=NB, max_val=BODIES - U)
            with sp.Fori(1, round_end(last) + U, U) as n:
                for s in slots:
                    onehots.before(sp, n, s, U)
                    attr_rest.before(sp, n, s, U)
                    split.before(sp, n, s, U)
                    sp.dma_start(rec[s][:, :, :].rearrange("p t c -> p (t c)"),
                                 ev[bass.ds(body_of(nc, n, s), 1), :, (s % 2) * G * REC:(s % 2 + 1) * G * REC].rearrange("b p c -> p (b c)")
                                 ).then_inc(loaded[s], 16)
            for s in slots:
                sp.wait_ge(loaded[s], round_end(last) * 2 + 14)
                sp.sem_inc(prime, 1)

        @block.gpsimd
        def _(pool):
            g = nc.gpsimd
            pool.wait_ge(d_start, 32)
            pool.wait_ge(setup, 2)
            last = pool.value_load(starts[0:1, NB:NB + 1], min_val=NB, max_val=BODIES - U)

            def coefficients(n, s):
                node_copied.after(pool, n, s)
                pool.wait_ge(loaded[s], n * 2 + 14)
                w_read.before(pool, n, s, 4)
                pool.sem_inc(prime, 1)
                sh0, sh1 = rec[s][:, :, C4:C4 + 1], rec[s][:, :, C4 + 1:C4 + 4]
                vec = node[s][:, :, MUL:D].rearrange("p t (u i) -> p t u i", i=3)
                g.tensor_tensor(coef[s][:, :, 0:MUL], node[s][:, :, 0:MUL], sh0.to_broadcast([P, G, MUL]), ALU.mult)
                g.tensor_tensor(vec0[s][:, :, :, :].rearrange("p t u i -> p t (u i)"), node[s][:, :, MUL:D],
                                sh0.to_broadcast([P, G, 3 * MUL]), ALU.mult)
                g.tensor_tensor(sh3[s][:, :, :], sh1, rt3[:, :, :], ALU.mult).then_inc(pool_chain, 1)
                pool.wait_ge(pool_chain, n + s)
                made_coef.set_by(g.tensor_tensor(dots[s][:, :, :, :], vec, sh3[s][:, :, :].unsqueeze(2).to_broadcast([P, G, MUL, 3]), ALU.mult))

            def attributes_rest(n, s):
                attr_hi.after(pool, n, s)
                pool.sem_inc(prime, 1)
                attr_rest.set_by(g.tensor_tensor(arest[s][:, :, :], rec[s][:, :, C8:C8 + MUL], attr[s][:, :, 0, :], ALU.subtract))

            def attributes_low(n, s):
                attr_mid.after(pool, n, s)
                pool.sem_inc(prime, 1)
                attr_cut.set_by(g.tensor_tensor(attr[s][:, :, 5, :], arest[s][:, :, :], attr[s][:, :, 3, :], ALU.subtract))

            def hidden_rest(k, n, s):
                h_hi[k].after(pool, n, s)
                pool.sem_inc(prime, 1)
                h_rest[k].set_by(g.tensor_tensor(hrest[k][s][:, :], h[k][s][:, :], hpart[k][s][:, 0, :], ALU.subtract))

            def hidden_low(k, n, s):
                h_mid[k].after(pool, n, s)
                pool.sem_inc(prime, 1)
                h_cut[k].set_by(g.tensor_tensor(hpart[k][s][0:H2, 2, :], hrest[k][s][0:H2, :], hpart[k][s][0:H2, 1, :], ALU.subtract))

            for s in range(2):
                attributes_rest(1, s); attributes_low(1, s)
            for s in range(3):
                attributes_rest(1, s + 2); attributes_low(1, s + 2)
                hidden_rest(0, 1, s); hidden_low(0, 1, s)
                coefficients(1, s)
            for s in range(2):
                hidden_rest(1, 1, s); hidden_low(1, 1, s)
            with pool.Fori(1, round_end(last), U) as n:
                for j in slots:
                    attributes_rest(*group(n, j + 5))
                    hidden_rest(0, *group(n, j + 3))
                    attributes_low(*group(n, j + 5))
                    hidden_rest(1, *group(n, j + 2))
                    hidden_low(0, *group(n, j + 3))
                    hidden_low(1, *group(n, j + 2))
                    coefficients(*group(n, j + 3))

        @block.scalar
        def _(act):
            act.wait_ge(d_start, 32)
            last = act.value_load(starts[0:1, NB:NB + 1], min_val=NB, max_val=BODIES - U)
            act.wait_ge(d_const, D_CONST)

            def copies(n, s):
                turned.after(act, n, s)
                h_done[0].before(act, n, s, 2)
                node_done.before(act, n, s, 2)
                recT_copied.set_by(nc.scalar.copy(recT[s][:, :], p_rec[:, :, :].rearrange("p t e -> p (t e)")))
                ohT_copied.set_by(nc.scalar.copy(ohT[s][:, :, :], p_oh[:, :, :]))

            def attributes(n, s):
                act.wait_ge(loaded[s], n * 2 + 14)
                turned.before(act, n, s, 2)
                act.sem_inc(prime, 1)
                attr_hi.set_by(nc.scalar.copy(attr[s][:, :, 0:3, :], rec[s][:, :, C8:C8 + MUL].unsqueeze(2).to_broadcast([P, G, 3, MUL])))

            def attributes_mid(n, s):
                attr_rest.after(act, n, s)
                attr_mid.set_by(nc.scalar.copy(attr[s][:, :, 3:5, :], arest[s][:, :, :].unsqueeze(2).to_broadcast([P, G, 2, MUL])))

            def node_copy(n, s):
                node_done.after(act, n, s)
                w_read.before(act, n, s, 4)
                node_copied.set_by(nc.scalar.copy(node[s][:, :, :], p_node[:, :, :]))

            def silu(k, n, s):
                h_done[k].after(act, n, s)
                h_rest[k].before(act, n, s, 2)
                (h_done[1], w_done)[k].before(act, n, s, 2)
                nc.scalar.activation(h[k][s][:, :], p_h[k][:, :], ACT.Silu, bias=(b1, b2)[k][:, :])
                h_hi[k].set_by(nc.scalar.activation(hpart[k][s][:, 0, :], p_h[k][:, :], ACT.Silu, bias=(b1, b2)[k][:, :]))

            def silu_mid(k, n, s):
                h_rest[k].after(act, n, s)
                h_mid[k].set_by(nc.scalar.copy(hpart[k][s][:, 1, :], hrest[k][s][:, :]))

            act.wait_ge(setup, 2)
            for s in range(2):
                attributes(1, s); attributes_mid(1, s)
            for s in range(3):
                copies(1, s)
                attributes(1, s + 2); attributes_mid(1, s + 2)
                silu(0, 1, s); silu_mid(0, 1, s)
                node_copy(1, s)
            copies(1, 3)
            for s in range(2):
                silu(1, 1, s); silu_mid(1, 1, s)
            with act.Fori(1, round_end(last), U) as n:
                for j in slots:
                    attributes(*group(n, j + 5))
                    silu(0, *group(n, j + 3))
                    silu(1, *group(n, j + 2))
                    attributes_mid(*group(n, j + 5))
                    silu_mid(0, *group(n, j + 3))
                    node_copy(*group(n, j + 3))
                    silu_mid(1, *group(n, j + 2))
                    copies(*group(n, j + 4))

        @block.tensor
        def _(pe):
            mm = nc.tensor.matmul
            pe.wait_ge(d_start, 32)
            last = pe.value_load(starts[0:1, NB:NB + 1], min_val=NB, max_val=BODIES - U)
            pe.wait_ge(d_const, D_CONST)
            pe.wait_ge(d_w, 16 * 13)
            pe.wait_ge(setup, 2)

            def turn(n, s):
                attr_cut.after(pe, n, s)
                recT_copied.before(pe, n, s, 1)
                pe.sem_inc(prime, 1)
                for t in range(G):
                    nc.tensor.transpose(p_rec[:, t, :], attr[s][:, t, :, :].rearrange("p k f -> p (k f)"), identb[:, :])
                onehots.after(pe, n, s)
                ohT_copied.before(pe, n, s, 1)
                for t in range(G):
                    i = nc.tensor.transpose(p_oh[:, t, :], oh[s][:, 0, t, :], identb[:, :])
                turned.set_by(i)

            def gather(n, s):
                src, _ = blocks_of(nc, pe, table, n, s)
                ohT_copied.after(pe, n, s)
                node_copied.before(pe, n, s, 1)
                for t in range(G):
                    for k in range(3):
                        i = mm(p_node[:, t, :], ohT[s][:, t, :], xp[:, bass.ds(src, 1), k, :], start=(k == 0), stop=(k == 2), skip_group_check=True)
                node_done.set_by(i)

            def first(n, s):
                recT_copied.after(pe, n, s)
                h_hi[0].before(pe, n, s, 1)
                pe.sem_inc(prime, 1)
                h_done[0].set_by(mm(p_h[0][:, :], w1s[:, :], recT[s][:, :], start=True, stop=True))

            def second(n, s):
                h_cut[0].after(pe, n, s)
                h_hi[1].before(pe, n, s, 1)
                pe.sem_inc(prime, 1)
                part = hpart[0][s]
                mm(p_h[1][:, :], w2s[:, :], part[:, 0, :], start=True, stop=False)
                mm(p_h[1][:, :], w2s[:, :], part[:, 1, :], start=False, stop=False)
                mm(p_h[1][:, :], w2_parts[:, 2, :], part[0:H2, 0, :], start=False, stop=False)
                h_done[1].set_by(mm(p_h[1][:, :], w2_parts[:, 0, :], part[0:H2, 2, :], start=False, stop=True))

            def third(n, s):
                h_cut[1].after(pe, n, s)
                w_read.before(pe, n, s, 1)
                part = hpart[1][s]
                pe.sem_inc(prime, 1)
                for t in range(0, G, 2):
                    mm(p_w[:, t:t + 2, :], ones3[:, :], b3s[:, :].unsqueeze(1).to_broadcast([3, 2, NTP]), start=True, stop=False, skip_group_check=True)
                for t in range(G):
                    e = slice(t * P, (t + 1) * P)
                    for k, (a, b) in enumerate(((part[:, 0, e], w3s[:, :]), (part[:, 1, e], w3s[:, :]),
                                 (part[0:H2, 0, e], w3_parts[:, 2, :]), (part[0:H2, 2, e], w3_parts[:, 0, :]))):
                        i = mm(p_w[:, t, :], a, b, start=False, stop=(t % 2 == 1 and k == 3), skip_group_check=True)
                w_done.set_by(i)

            def sums(n, s):
                split.after(pe, n, s)
                sum_added.before(pe, n, s, 1)
                for t in range(G):
                    for k in range(3):
                        i = mm(p_sum[:, t, :], oh[s][:, 1, t, :], part[s][:, t, k, :], start=(k == 0), stop=(k == 2), skip_group_check=True)
                sum_done.set_by(i)

            for s in range(3):
                turn(1, s)
                first(1, s); gather(1, s)
            turn(1, 3)
            for s in range(2):
                second(1, s)
            third(1, 0)
            with pe.Fori(1, round_end(last), U) as n:
                for j in slots:
                    first(*group(n, j + 3))
                    second(*group(n, j + 2))
                    third(*group(n, j + 1))
                    sums(*group(n, j))
                    gather(*group(n, j + 3))
                    turn(*group(n, j + 4))

        @block.vector
        def _(dve):
            V = nc.vector
            V.memset(ones3[:, :], 1.0).then_inc(setup, 1)
            V.memset(agg[:, :, 0:D], 0.0)
            V.memset(rt3[:, :, :], RT3)
            dve.wait_ge(d_const, D_CONST)
            V.tensor_copy(iotab[:, :], iota[:, :])
            V.tensor_copy(identb[:, :], ident[:, :]).then_inc(setup, 1)
            for at, (whole, parts) in enumerate(((w1[:, :, :].rearrange("p k h -> p (k h)"), w1_parts), (w2[:, :, :].rearrange("p k h -> p (k h)"), w2_parts),
                                                 (w3[:, :], w3_parts), (b3[:, :], b3_parts))):
                cut_weights(dve, V, w_chain, whole, parts, 4 * at)
            dve.wait_ge(setup, 2)
            dve.wait_ge(d_start, 32)
            last = dve.value_load(starts[0:1, NB:NB + 1], min_val=NB, max_val=BODIES - U)
            MM = MUL * MUL

            def one_hots(n, s):
                dve.wait_ge(loaded[s], n * 2 + 14)
                sum_done.before(dve, n, s, U)
                for t in range(G):
                    for k, c in enumerate((CSRC, CDST)):
                        i = V.tensor_scalar(oh[s][:, k, t, :], iotab[:, :], rec[s][:, t, c:c + 1], None, ALU.is_equal)
                onehots.set_by(i)

            def products(n, s):
                link = Chain(dve, dve_chain, n, s).link
                made_coef.after(dve, n, s)
                link(V.tensor_reduce(coef[s][:, :, MUL:2 * MUL], dots[s][:, :, :, :], AX.X, ALU.add))
                w_done.after(dve, n, s)
                V.tensor_tensor(prod0[:, :, :, :], p_w[:, :, 0:2 * MM].rearrange("p t (u w) -> p t u w", w=MUL),
                                coef[s][:, :, :].unsqueeze(3).to_broadcast([P, G, 2 * MUL, MUL]), ALU.mult)
                V.tensor_tensor(prod1[:, :, :, :], p_w[:, :, 2 * MM:3 * MM].rearrange("p t (u w) -> p t u w", w=MUL),
                                node[s][:, :, 0:MUL].unsqueeze(3).to_broadcast([P, G, MUL, MUL]), ALU.mult)
                for i in range(3):
                    last_op = V.tensor_tensor(prod2[:, i, :, :, :], p_w[:, :, 3 * MM:4 * MM].rearrange("p t (u w) -> p t u w", w=MUL),
                                              vec0[s][:, :, :, i].unsqueeze(3).to_broadcast([P, G, MUL, MUL]), ALU.mult)
                w_read.set_by(last_op)

            def messages(n, s):
                link = Chain(dve, dve_chain[1:], n, s).link
                w_read.after(dve, n, s)
                sum_done.before(dve, n, s, 2)
                V.tensor_reduce(msg[s][:, :, 0:MUL], prod0[:, :, :, :].rearrange("p t u w -> p t w u"), AX.X, ALU.add)
                link(V.tensor_reduce(sum1[:, :, :], prod1[:, :, :, :].rearrange("p t u w -> p t w u"), AX.X, ALU.add))
                V.tensor_tensor(outer[:, :, :, :], sum1[:, :, :].unsqueeze(3).to_broadcast([P, G, MUL, 3]),
                                rec[s][:, :, C4 + 1:C4 + 4].unsqueeze(2).to_broadcast([P, G, MUL, 3]), ALU.mult)
                link(V.tensor_reduce(sum2[:, :, :, :].rearrange("p i t w -> p (i t) w"),
                                     prod2[:, :, :, :, :].rearrange("p i t u w -> p (i t) w u"), AX.X, ALU.add))
                link(V.tensor_tensor(msg[s][:, :, MUL:D].rearrange("p t (w i) -> p t w i", i=3), outer[:, :, :, :],
                                     sum2[:, :, :, :].rearrange("p i t w -> p t w i"), ALU.add))
                link(V.tensor_copy(part[s][:, :, 0, :], msg[s][:, :, :]))
                link(V.tensor_tensor(rest[s][:, :, :], msg[s][:, :, :], part[s][:, :, 0, :], ALU.subtract))
                link(V.tensor_copy(part[s][:, :, 1, :], rest[s][:, :, :]))
                split.set_by(V.tensor_tensor(part[s][:, :, 2, :], rest[s][:, :, :], part[s][:, :, 1, :], ALU.subtract))

            def add_sums(n, s):
                _, dsts = blocks_of(nc, dve, table, n, s)
                sum_done.after(dve, n, s)
                for t in range(G):
                    at = agg[:, bass.ds(dsts[t], 1), 0:D].rearrange("p a c -> p (a c)")
                    i = V.tensor_tensor(at, p_sum[:, t, :], at, ALU.add)
                    if t < G - 1:
                        i.then_inc(dve_chain[9 + t], 1)
                        dve.wait_ge(dve_chain[9 + t], n + s)
                    else:
                        sum_added.set_by(i)
                        sum_added.after(dve, n, s)

            for s in range(5):
                one_hots(1, s)
            products(1, 0); messages(1, 0)
            with dve.Fori(1, round_end(last), U) as n:
                for j in slots:
                    products(*group(n, j + 1))
                    add_sums(*group(n, j))
                    one_hots(*group(n, j + 5))
                    messages(*group(n, j + 1))
    clear(nc, used)


def layer2_phase(nc, io, dram, keep):
    used = []
    ctx = ExitStack()
    with ctx:
        def sb(name, shape, dt=F32):
            return ctx.enter_context(nc.sbuf_tensor("q_" + name, shape, dt))

        def sem(name):
            used.append(ctx.enter_context(nc.semaphore("q_" + name)))
            return used[-1]

        def flags(name, n):
            made = [Flag(sem(f"{name}{i}")) for i in range(n)]
            primed.extend(made)
            return made

        primed = []
        x, agg, ident = keep["x"], keep["agg"], keep["ident"]
        CH = -(-NB // 4)
        width = [min(4, NB - 4 * c) for c in range(CH)]
        A = sb("A", [P, NB, NP], BF16)
        g3 = [sb(f"g3{k}", [P, NB, 3, D], BF16) for k in range(2)]
        sT = [sb(f"sT{k}", [3 * D, 4 * P]) for k in range(2)]
        s_ = sb("s_", [P, 4, D])
        gf = sb("gf", [P, 4, D])
        rest = sb("rest", [P, 4, D])
        h = sb("h", [P, NB, D])
        base = sb("base", [P, NB, D])
        norm = sb("norm", [P, 4, NB])
        std = sb("std", [P, 4, NB])
        p_s = [ctx.enter_context(nc.psum_tensor(f"q_p_s{k}", [3 * D, 512], F32)) for k in range(4)]
        p_t = [ctx.enter_context(nc.psum_tensor(f"q_p_t{k}", [P, 4, 3 * D], F32)) for k in range(2)]
        a_loaded = dram["a_loaded"]
        d_ready, rooted, s_v, started, s_std, s_root, s_credit = (sem("d_ready"), sem("rooted"), sem("v"), sem("started"),
                                                                  sem("std"), sem("root"), sem("credit"))
        U = 2
        summed, copied, turned, gathered = flags("summed", U * CH), flags("copied", U * CH), flags("turned", U * CH), flags("gathered", U * CH)
        dve_chain = [sem(f"chain{i}") for i in range(7)]
        block = ctx.enter_context(nc.Block())

        @block.gpsimd
        def _(pool):
            for b in range(NB):
                pool.dma_start(A[:, b, :].rearrange("p (d c) -> p d c", c=P),
                               dram["strips"][b, :, :].rearrange("p (d k) -> p d k", k=2 * P)[:, :, 0:P]).then_inc(a_loaded, 16)

        @block.sync
        def _(sp):
            for f in primed:
                sp.sem_inc(f.semaphore, 1)

        @block.scalar
        def _(act):
            act.wait_ge(d_ready, 1)
            nc.scalar.sqrt(norm[:, 1, :], norm[:, 0, :]).then_inc(rooted, 1)
            with act.Fori(1, STEPS2 // U + 1) as n:
                for u in range(U):
                    for c in range(CH):
                        i = u * CH + c
                        summed[i].after(act, n)
                        if i >= 2:
                            turned[i - 2].after(act, n)
                        else:
                            turned[U * CH - 2 + i].before(act, n)
                        copied[i].set_by(nc.scalar.copy(sT[i % 2][:, 0:width[c] * P], p_s[i % 4][:, 0:width[c] * P]))
            act.wait_ge(s_std, 1)
            nc.scalar.sqrt(std[:, 2, :], std[:, 1, :]).then_inc(s_root, 1)

        @block.tensor
        def _(pe):
            pe.wait_ge(started, 1)
            pe.wait_ge(a_loaded, 16 * NB)
            total = U * CH
            with pe.Fori(1, STEPS2 // U + 1) as n:
                def turn(i):
                    c = i % CH
                    copied[i].after(pe, n)
                    if i >= 2:
                        gathered[i - 2].after(pe, n)
                    else:
                        gathered[total - 2 + i].before(pe, n)
                    for k in range(width[c]):
                        m = nc.tensor.transpose(p_t[i % 2][:, k, :], sT[i % 2][:, k * P:(k + 1) * P], ident[0:3 * D, 0:3 * D])
                    turned[i].set_by(m)

                for u in range(U):
                    for c in range(CH):
                        i = u * CH + c
                        if i >= 4:
                            copied[i - 4].after(pe, n)
                        else:
                            last_use = [j for j in range(total) if j % 4 == i % 4][-1]
                            copied[last_use].before(pe, n)
                        for b in range(NB):
                            if c == 0 and b % 4 == 0:
                                if u:
                                    gathered[b // 4].after(pe, n)
                                else:
                                    gathered[CH + b // 4].before(pe, n)
                            m = nc.tensor.matmul(p_s[i % 4][:, 0:width[c] * P], g3[u][:, b, :, :], A[:, b, 4 * c * P:(4 * c + width[c]) * P],
                                                 start=(b == 0), stop=(b == NB - 1))
                        summed[i].set_by(m)
                        if c:
                            turn(i - 1)
                    turn(u * CH + CH - 1)

        @block.vector
        def _(dve):
            V = nc.vector
            at = [0]

            def link(i):
                at[0] += 1
                i.then_inc(s_v, 1)
                dve.wait_ge(s_v, at[0])

            deg = agg[:, :, 2 * D]
            wide = [P, NB, D]
            V.tensor_scalar(norm[:, 0, :], deg, 1.0, None, ALU.max).then_inc(d_ready, 1)
            link(V.tensor_scalar(norm[:, 3, :], deg, 0.0, None, ALU.is_gt))
            dve.wait_ge(rooted, 1)
            link(V.reciprocal(norm[:, 2, :], norm[:, 1, :]))
            link(V.tensor_tensor(norm[:, 1, :], norm[:, 2, :], norm[:, 3, :], ALU.mult))
            link(V.tensor_scalar(norm[:, 2, :], norm[:, 1, :], 1.0 - ALPHA2, None, ALU.mult))
            link(V.tensor_scalar(base[:, :, :], x[:, :, :], ALPHA2, None, ALU.mult))
            link(V.tensor_tensor(h[:, :, :], x[:, :, :], norm[:, 1, :].unsqueeze(2).to_broadcast(wide), ALU.mult))
            link(V.tensor_copy(g3[0][:, :, 0, :], h[:, :, :]))
            link(V.tensor_tensor(h[:, :, :], h[:, :, :], g3[0][:, :, 0, :], ALU.subtract))
            link(V.tensor_copy(g3[0][:, :, 1, :], h[:, :, :]))
            link(V.tensor_tensor(g3[0][:, :, 2, :], h[:, :, :], g3[0][:, :, 1, :], ALU.subtract))
            dve.sem_inc(started, 1)
            with dve.Fori(1, STEPS2 // U + 1) as n:
                for u in range(U):
                    to = g3[1 - u]
                    for c in range(CH):
                        i = u * CH + c
                        w = width[c]
                        b = slice(4 * c, 4 * c + w)
                        wd = [P, w, D]

                        def chained(k, ins):
                            ins.then_inc(dve_chain[k], 1)
                            dve.wait_ge(dve_chain[k], (n - 1) * total + (i + 1))

                        total = U * CH
                        turned[i].after(dve, n)
                        chained(0, V.tensor_reduce(s_[:, 0:w, :], p_t[i % 2][:, 0:w, :].rearrange("p b (k f) -> p b f k", k=3), AX.X, ALU.add))
                        chained(1, V.tensor_tensor(gf[:, 0:w, :], s_[:, 0:w, :], norm[:, 2, b].unsqueeze(2).to_broadcast(wd), ALU.mult))
                        chained(2, V.tensor_tensor(h[:, b, :], gf[:, 0:w, :], base[:, b, :], ALU.add))
                        chained(3, V.tensor_tensor(gf[:, 0:w, :], h[:, b, :], norm[:, 1, b].unsqueeze(2).to_broadcast(wd), ALU.mult))
                        chained(4, V.tensor_copy(to[:, b, 0, :], gf[:, 0:w, :]))
                        chained(5, V.tensor_tensor(rest[:, 0:w, :], gf[:, 0:w, :], to[:, b, 0, :], ALU.subtract))
                        chained(6, V.tensor_copy(to[:, b, 1, :], rest[:, 0:w, :]))
                        gathered[i].set_by(V.tensor_tensor(to[:, b, 2, :], rest[:, 0:w, :], to[:, b, 1, :], ALU.subtract))
            gathered[U * CH - 1].after(dve, STEPS2 // U)
            link(V.tensor_tensor(h[:, :, :], x[:, :, :], h[:, :, :], ALU.add))
            layernorm(dve, V, link, x, h, base, std, s_std, s_root)
    clear(nc, used)


def layer3_phase(nc, io, dram, keep, out):
    used = []
    ctx = ExitStack()
    with ctx:
        def sb(name, shape, dt=F32):
            return ctx.enter_context(nc.sbuf_tensor("r_" + name, shape, dt))

        def sem(name):
            used.append(ctx.enter_context(nc.semaphore("r_" + name)))
            return used[-1]

        def flags(name, n):
            made = [Flag(sem(f"{name}{i}")) for i in range(n)]
            primed.extend(made)
            return made

        primed = []
        x = keep["x"]
        SL, BK = 5, 4
        W = [sb(f"W{k}", [P, NB, P]) for k in range(SL)]
        X = sb("X", [P, 2, NB, D])
        tmp = sb("tmp", [P, NB, D])
        std = sb("std", [P, 4, NB])
        p_o = [ctx.enter_context(nc.psum_tensor(f"r_p_o{k}", [P, 512], F32)) for k in range(BK)]
        arrived = [sem(f"arrived{k}") for k in range(SL)]
        started, s_v, s_std, s_root, final, stored = sem("started"), sem("v"), sem("std"), sem("root"), sem("final"), sem("stored")
        summed, copied = flags("summed", NB), flags("copied", NB)
        block = ctx.enter_context(nc.Block())

        @block.sync
        def _(sp):
            for f in primed:
                sp.sem_inc(f.semaphore, 1)
            with sp.Fori(1, STEPS3 + 1) as n:
                for b in range(NB):
                    if b >= SL:
                        summed[b - SL].after(sp, n)
                    else:
                        summed[NB - SL + b].before(sp, n)
                    sp.dma_start(W[b % SL][:, :, :], dram["strips"][b, :, :].rearrange("p (d k) -> p d k", k=2 * P)[:, :, P:2 * P]
                                 ).then_inc(arrived[b % SL], 16)
            sp.wait_ge(final, 1)
            sp.dma_start(out[0:(NB - 1) * P, :].rearrange("(b p) f -> p b f", p=P), x[:, 0:NB - 1, :]).then_inc(stored, 16)
            sp.dma_start(out[(NB - 1) * P:N, :], x[0:LAST, NB - 1, :]).then_inc(stored, 16)
            sp.wait_ge(stored, 32)

        @block.tensor
        def _(pe):
            pe.wait_ge(started, 1)
            with pe.Fori(1, STEPS3 + 1) as n:
                copied[NB - 1].before(pe, n)
                for b in range(NB):
                    pe.wait_ge(arrived[b % SL], (n - 1) * (16 * NB // SL) + 16 * (b // SL + 1))
                    if b >= BK:
                        copied[b - BK].after(pe, n)
                    else:
                        copied[[j for j in range(NB) if j % BK == b][-1]].before(pe, n)
                    for d in range(NB):
                        m = nc.tensor.matmul(p_o[b % BK][:, 0:D], W[b % SL][:, d, :], X[:, bass.ds((n - 1) & 1, 1), d, :],
                                             start=(d == 0), stop=(d == NB - 1))
                    summed[b].set_by(m)

        @block.scalar
        def _(act):
            with act.Fori(1, STEPS3 + 1) as n:
                for b in range(NB):
                    summed[b].after(act, n)
                    copied[b].set_by(nc.scalar.copy(X[:, bass.ds(n & 1, 1), b, :].rearrange("p a c -> p (a c)"), p_o[b % BK][:, 0:D]))
            act.wait_ge(s_std, 1)
            nc.scalar.sqrt(std[:, 2, :], std[:, 1, :]).then_inc(s_root, 1)

        @block.vector
        def _(dve):
            V = nc.vector
            at = [0]

            def link(i):
                at[0] += 1
                i.then_inc(s_v, 1)
                dve.wait_ge(s_v, at[0])

            V.tensor_copy(X[:, 0, :, :], x[:, :, :]).then_inc(started, 1)
            copied[NB - 1].after(dve, STEPS3)
            r = X[:, STEPS3 & 1, :, :]
            link(V.tensor_tensor(r, r, x[:, :, :], ALU.add))
            layernorm(dve, V, link, x, r, tmp, std, s_std, s_root)
            dve.sem_inc(final, 1)
    clear(nc, used)


def sort_constants(np):
    r = np.arange(P)
    j, s = r // S, r % S
    same = s[:, None] == s[None, :]
    before = (s[:, None] < s[None, :]) & (j[:, None] == 0)
    mats = [r[:, None] == r[None, :], np.broadcast_to(r, (P, P)), r[:, None] > r[None, :],
            same, same & (j[:, None] < j[None, :]), before]
    return np.ascontiguousarray(np.stack(mats, 1).astype(np.float32))


_INS = ["x", "src", "dst", "edge_attr_16", "edge_attr_4", "edge_attr_8", "edge_weight",
        "L0_gnn_W1f", "L0_gnn_b1f", "L0_gnn_W2f", "L0_gnn_b2f", "L0_gnn_W1b", "L0_gnn_b1b", "L0_gnn_W2b", "L0_gnn_b2b",
        "L0_gnn_W1n", "L0_gnn_b1n", "L0_gnn_W2n", "L0_gnn_b2n",
        "L1_gnn_W1", "L1_gnn_b1", "L1_gnn_W2", "L1_gnn_b2", "L1_gnn_W3", "L1_gnn_b3", "L1_gnn_Ws", "L1_gnn_Wv"]


def build(nc, io, out):
    dram = {
        "edges": nc.dram_tensor("sorted_edges", (ROWS, REC), F32, kind="Internal").ap(),
        "table": nc.dram_tensor("body_table", (BODIES, TAB), I32, kind="Internal").ap(),
        "starts": nc.dram_tensor("block_starts", (S,), I32, kind="Internal").ap(),
        "strips": nc.dram_tensor("dense_strips", (NB, P, NB * 2 * P), F32, kind="Internal").ap(),
    }
    with ExitStack() as ctx:
        dram["sent"] = [ctx.enter_context(nc.semaphore(f"sent{k}")) for k in range(2)]
        dram["a_loaded"] = ctx.enter_context(nc.semaphore("a_loaded"))
        sort_phase(nc, io, dram, io["sort_consts"])
        with ExitStack() as inner:
            def sb(name, shape, dt=F32):
                return inner.enter_context(nc.sbuf_tensor(name, shape, dt))

            keep = {"x": sb("x", [P, NB, D]), "agg": sb("agg", [P, NB, 2 * D + 1]), "ident": sb("ident", [P, P])}
            with nc.sbuf_tensor("tab", [P, NB, 3, 4 * H1], BF16) as tab:
                keep["tab"] = tab
                load_nodes_phase(nc, io, keep)
                layer0_edges_phase(nc, io, dram, keep)
            with nc.sbuf_tensor("xp", [P, NB, 3, D], BF16) as xp:
                keep["xp"] = xp
                nodes_phase(nc, io, keep, 0)
                layer1_edges_phase(nc, io, dram, keep)
                nodes_phase(nc, io, keep, 1)
            layer2_phase(nc, io, dram, keep)
            layer3_phase(nc, io, dram, keep, out)


def kernel(**inputs):
    import numpy as np
    import concourse.bacc as bacc
    from concourse.bass_utils import run_bass_kernel_spmd

    nc = bacc.Bacc("TRN2", target_bir_lowering=False, num_devices=1)
    arrays = {name: np.ascontiguousarray(inputs[name]) for name in _INS}
    arrays["sort_consts"] = sort_constants(np)
    arrays["iota_t"] = np.ascontiguousarray(np.broadcast_to(np.arange(BODIES * TB, dtype=np.float32), (P, BODIES * TB)))
    io = {name: nc.dram_tensor(f"in_{name}", a.shape, mybir.dt.from_np(a.dtype), kind="ExternalInput").ap()
          for name, a in arrays.items()}
    out = nc.dram_tensor("out", (N, D), F32, kind="ExternalOutput").ap()
    build(nc, io, out)
    r = run_bass_kernel_spmd(nc, [{f"in_{name}": a for name, a in arrays.items()}], core_ids=[0])
    return r.results[0]["out"]
```

```python
import concourse.bass as bass
from concourse import mybir
from contextlib import ExitStack

F32 = mybir.dt.float32
BF16 = mybir.dt.bfloat16
F16 = mybir.dt.float16
I32 = mybir.dt.int32
ALU = mybir.AluOpType
ACT = mybir.ActivationFunctionType
AX = mybir.AxisListType

P = 128
N = 3125
E = 50000
D = 32
NB = -(-N // P)
NP = NB * P
LAST = N - (NB - 1) * P
EP = 125
EC = E // EP
J = 4
Q = EC // J
S = 32
G = 4
TB = 2 * G
TILES = E // P + NB * NB
U = 4 * TB // G
BODIES = (TILES + NB * (TB - 1)) // TB + U
ROWS = BODIES * TB * P
REC = 32
C16, C8, C4, CW, CR, CSRC, CDST = 0, 16, 24, 28, 29, 30, 31
TAB = 12
TSRC, TNEW = TB, TB + 2
TPACK = (TB + 1, TB + 3)
BITS = 5
BIG = 1.0e9
H1 = 64
OUT_DEGREE, IN_DEGREE = 0, 2 * D + 1


def sort_phase(nc, io, dram, sort_consts):
    used = []
    ctx = ExitStack()
    with ctx:
        def sb(name, shape, dt):
            return ctx.enter_context(nc.sbuf_tensor("s_" + name, shape, dt))

        def ps(name, shape, dt=F32):
            return ctx.enter_context(nc.psum_tensor("s_" + name, shape, dt))

        def sem(name):
            used.append(ctx.enter_context(nc.semaphore("s_" + name)))
            return used[-1]

        cst = sb("cst", [P, 6, P], F32)
        IDENT, IOTA, LOWER, SAME, EARLIER, BEFORE = range(6)
        iota_t = sb("iota_t", [P, BODIES * TB], F32)
        ident16 = sb("ident16", [P, P], F16)
        ones = sb("ones", [P, 1], F32)
        onesq = sb("onesq", [P, Q], F32)
        src_i = sb("src_i", [EP, EC], I32)
        dst_i = sb("dst_i", [EP, EC], I32)
        blk_i = sb("blk_i", [EP, 2, EC], I32)
        blk = sb("blk", [EP, 2, EC], F32)
        loc_i = sb("loc_i", [EP, 2, EC], I32)
        loc = sb("loc", [EP, 2, EC], F32)
        key = sb("key", [EP, EC], F32)
        key16 = sb("key16", [EP, EC], F16)
        keyT = sb("keyT", [Q, J, EP], F16)
        ea16 = sb("ea16", [EP, EC, 16], F32)
        ea8 = sb("ea8", [EP, EC, 8], F32)
        ea4 = sb("ea4", [EP, EC, 4], F32)
        w = sb("w", [EP, EC], F32)
        w_hi = sb("w_hi", [EP, EC], BF16)
        w_rest = sb("w_rest", [EP, EC], F32)
        oh_src = sb("oh_src", [EP, Q, J, S], F16)
        oh_dst = sb("oh_dst", [EP, Q, J, NB], F16)
        hist = sb("hist", [P, Q, NB], F32)
        cum = sb("cum", [P, Q, NB], F32)
        cum_i = hist[:, :, :].bitcast(I32)
        part_i = [cum[:, :, :].bitcast(I32), cum_i]
        lookup = sb("lookup", [P, Q, 2, J, NB], F16)
        small = sb("small", [P, 12, NB], F32)
        small_i = sb("small_i", [P, 3, NB], I32)
        col = sb("col", [P, 8], F32)
        col_i = sb("col_i", [P, 2], I32)
        starts4 = sb("starts4", [P, 7], F32)
        count_t = hist[:, :, :].rearrange("p q d -> p (q d)")[:, 0:2 * BODIES * TB].rearrange("p (a t) -> p a t", a=2)
        count_b = sb("count_b", [P, BODIES], F32)
        tabrow = cum[0:1, :, :].rearrange("p q d -> p (q d)")[:, 0:BODIES * TAB].rearrange("p (b t) -> p b t", t=TAB)
        tabrow_i = sb("tabrow_i", [1, BODIES, TAB], I32)
        above_i = sb("above_i", [1, BODIES, 1], I32)
        bst_i = sb("bst_i", [1, S], I32)
        first = sb("first", [1, 16], F32)
        neg = sb("neg", [P, TB * REC], F32)
        rank = sb("rank", [EP, Q, J], F32)
        junk = sb("junk", [EP, J, EP], BF16)
        ohT = sb("ohT", [P, 4, EP], F16)
        prod = sb("prod", [EP, 2, 2, J * NB], F32)
        sel = sb("sel", [EP, 4, 2, J], F32)
        pos = sb("pos", [EP, 4, J], F32)
        pos_i = sb("pos_i", [EP, 5, 4 * J], I32)
        index = [sb(f"index{s}", [EP, 2 * J], I32) for s in range(2)]
        record = [sb(f"record{s}", [EP, 2 * J, REC], F32) for s in range(2)]

        p_rows = [ps(f"p_rows{i}", [P, J * EP]) for i in range(2)]
        p_t = ps("p_t", [P, 2, P], F16)
        p_h = [ps(f"p_h{i}", [P, 5, J, NB]) for i in range(2)]
        p_sm = ps("p_sm", [P, 512])

        s_idx, s_cst, s_att, s_neg = sem("s_idx"), sem("s_cst"), sem("s_att"), sem("s_neg")
        s_keyT = sem("s_keyT"); s_keyTs = sem("s_keyTs"); s_id16 = sem("s_id16"); s_key = sem("s_key")
        s_rows = sem("s_rows"); s_ranked = sem("s_ranked")
        s_oh = sem("s_oh"); s_hist = sem("s_hist"); s_histed = sem("s_histed")
        s_tot = sem("s_tot"); s_totp = sem("s_totp")
        s_ready = sem("s_ready"); s_cnt = sem("s_cnt"); s_cntp = sem("s_cntp"); s_tab = sem("s_tab")
        s_bst = sem("s_bst"); s_out = sem("s_out"); s_negset = sem("s_negset")
        s_tr = sem("s_tr"); s_trc = sem("s_trc"); s_look = sem("s_look"); s_sel = sem("s_sel")
        s_index = [sem(f"s_index{s}") for s in range(2)]
        s_record = [sem(f"s_record{s}") for s in range(2)]
        s_sent = dram["sent"]
        s_free = [sem(f"s_free{s}") for s in range(2)]
        s_v = sem("s_v"); s_loc = sem("s_loc"); s_w = sem("s_w"); s_go = sem("s_go")
        block = ctx.enter_context(nc.Block())

        @block.sync
        def _(sp):
            sp.dma_start(src_i[:, :], io["src"].rearrange("(p c) -> p c", p=EP)).then_inc(s_idx, 16)
            sp.dma_start(cst[:, :, :], sort_consts).then_inc(s_cst, 16)
            sp.dma_start(iota_t[:, :], io["iota_t"]).then_inc(s_cst, 16)
            sp.dma_start(ea16[:, :, :], io["edge_attr_16"].rearrange("(p c) f -> p c f", p=EP)).then_inc(s_att, 16)
            sp.wait_ge(s_negset, 1)
            span = ROWS * REC // P
            sp.dma_start(dram["edges"].rearrange("(p r) c -> p (r c)", p=P).rearrange("p (k m) -> p k m", m=TB * REC),
                         neg[:, :].unsqueeze(1).to_broadcast([P, span // (TB * REC), TB * REC])).then_inc(s_neg, 16)
            sp.wait_ge(s_tab, 1)
            sp.dma_start(dram["table"].unsqueeze(0), tabrow_i[:, :, :]).then_inc(s_out, 16)
            sp.dma_start(dram["starts"].unsqueeze(0), bst_i[:, :]).then_inc(s_out, 16)
            sp.wait_ge(s_out, 32)

        @block.scalar
        def _(act):
            act.dma_start(dst_i[:, :], io["dst"].rearrange("(p c) -> p c", p=EP)).then_inc(s_idx, 16)
            act.dma_start(w[:, :], io["edge_weight"].rearrange("(p c) -> p c", p=EP)).then_inc(s_att, 16)
            act.dma_start(ea8[:, :, :], io["edge_attr_8"].rearrange("(p c) f -> p c f", p=EP)).then_inc(s_att, 16)
            act.dma_start(ea4[:, :, :], io["edge_attr_4"].rearrange("(p c) f -> p c f", p=EP)).then_inc(s_att, 16)
            act.wait_ge(s_keyT, 1)
            nc.scalar.copy(keyT[:, 0:2, :], p_t[0:Q, 0:2, 0:EP]).then_inc(s_keyTs, 1)
            act.wait_ge(s_keyT, 2)
            nc.scalar.copy(keyT[:, 2:4, :], p_t[0:Q, 0:2, 0:EP]).then_inc(s_keyTs, 1)
            act.wait_ge(s_att, 64)
            act.wait_ge(s_loc, 1)
            act.wait_ge(s_w, 1)
            with act.Fori(1, Q // 4 + 1) as n:
                act.wait_ge(s_trc, n)
                for h in range(2):
                    act.wait_ge(s_tr, 2 * n - 1 + h)
                    nc.scalar.copy(ohT[:, 2 * h:2 * h + 2, :], p_t[:, :, 0:EP]).then_inc(s_ready, 1)
                c0 = (n - 1) * 4 * J
                for s in range(2):
                    act.wait_ge(s_free[s], n + s)
                    c = c0 + s * 2 * J
                    k = bass.ds(c, 2 * J)
                    nc.scalar.copy(record[s][:, :, C16:C16 + 16], ea16[:, k, :])
                    nc.scalar.copy(record[s][:, :, C8:C8 + 8], ea8[:, k, :])
                    nc.scalar.copy(record[s][:, :, C4:C4 + 4], ea4[:, k, :])
                    nc.scalar.copy(record[s][:, :, CW], w[:, k])
                    nc.scalar.copy(record[s][:, :, CR], w_rest[:, k])
                    nc.scalar.copy(record[s][:, :, CSRC:CDST + 1].rearrange("p c k -> p k c"),
                                   loc[:, :, k]).then_inc(s_record[s], 1)

        @block.gpsimd
        def _(pool):
            nc.gpsimd.memset(neg[:, :], -1.0).then_inc(s_negset, 1)
            nc.gpsimd.memset(lookup[:, :, :, :, :], 0.0).then_inc(s_negset, 1)
            for s in range(2):
                pool.sem_inc(s_free[s], 1)
            pool.dma_start(first[:, :], io["iota_t"][0:1, 0:16]).then_inc(s_sent[1], 16)
            pool.wait_ge(s_neg, 16)
            with pool.Fori(1, Q // 4 + 1) as n:
                for s in range(2):
                    pool.wait_ge(s_index[s], n)
                    pool.wait_ge(s_record[s], n)
                    pool.sem_inc(s_go, 1)
                    for c in range(2 * J):
                        pool.indirect_dma_start(dram["edges"], bass.IndirectOffsetOnAxis(ap=index[s][:, c:c + 1], axis=0),
                                                record[s][:, c, :], None).then_inc(s_sent[s], 16)
                    pool.wait_ge(s_sent[1 - s], n * (2 * J * 16) if s else (n - 1) * (2 * J * 16) + 16)
                    pool.sem_inc(s_free[1 - s], 1)
            pool.wait_ge(s_sent[1], (Q // 4) * (2 * J * 16) + 16)

        @block.tensor
        def _(pe):
            pe.wait_ge(s_key, 1)
            pe.wait_ge(s_id16, 1)
            kv = key16[:, :].rearrange("p (q j) -> p j q", j=J)
            for h in range(2):
                if h:
                    pe.wait_ge(s_keyTs, 1)
                for j in range(2):
                    t = nc.tensor.transpose(p_t[0:Q, j, 0:EP], kv[:, 2 * h + j, :], ident16[0:EP, 0:EP])
                t.then_inc(s_keyT, 1)
            pe.wait_ge(s_keyTs, 2)
            pe.wait_ge(s_oh, 1)
            with pe.Fori(1, Q // 10 + 1) as n:
                for h in range(2):
                    pe.wait_ge(s_histed, 2 * n - 1 + h)
                    for k in range(5):
                        q = (n - 1) * 10 + h * 5 + k
                        m = nc.tensor.matmul(p_h[h][:, k, :, :], oh_src[:, bass.ds(q, 1), :, :], oh_dst[:, bass.ds(q, 1), :, :],
                                             start=(k == 0), stop=(k == 4), skip_group_check=True)
                    m.then_inc(s_hist, 1)
            pe.wait_ge(s_tot, 1)
            nc.tensor.matmul(p_sm[:, 0:NB], cst[:, SAME, :], small[:, 0, :], start=True, stop=True).then_inc(s_totp, 1)
            nc.tensor.matmul(p_sm[:, 32:32 + NB], cst[:, EARLIER, :], small[:, 0, :], start=True, stop=True).then_inc(s_totp, 1)
            pe.wait_ge(s_tot, 2)
            nc.tensor.matmul(p_sm[:, 64:65], cst[:, BEFORE, :], col[:, 1:2], start=True, stop=True).then_inc(s_totp, 1)
            with pe.Fori(1, Q // 2 + 1) as n:
                for h in range(2):
                    pe.wait_ge(s_ranked, 2 * n - 1 + h)
                    k = (n - 1) * 2 + h
                    nc.tensor.matmul(p_rows[h][0:EP, :], ident16[0:Q, bass.ds(k, 1)].to_broadcast([Q, EP]), keyT[:, :, :],
                                     start=True, stop=True).then_inc(s_rows, 1)
            pe.wait_ge(s_cnt, 1)
            pe.sem_inc(s_ready, 2)
            pe.sem_inc(s_trc, 1)
            with pe.Fori(1, Q // 4 + 1) as n:
                for h in range(2):
                    pe.wait_ge(s_ready, 2 * n + h)
                    for k in range(2):
                        q = (n - 1) * 4 + 2 * h + k
                        m = nc.tensor.transpose(p_t[:, k, 0:EP], oh_src[:, bass.ds(q, 1), :, :], ident16[0:EP, 0:EP])
                    m.then_inc(s_tr, 1)
                pe.wait_ge(s_ready, 2 * n + 2)
                for h in range(2):
                    pe.wait_ge(s_sel, 2 * n - 1 + h)
                    for k in range(2):
                        q = (n - 1) * 4 + 2 * h + k
                        m = nc.tensor.matmul(p_h[h][0:EP, 0:4, :, :].rearrange("p a j d -> p (a j d)")[:, k * 2 * J * NB:(k + 1) * 2 * J * NB],
                                             ohT[:, 2 * h + k, :], lookup[:, bass.ds(q, 1), :, :, :],
                                             start=(k == 0), stop=(k == 1), skip_group_check=True)
                    m.then_inc(s_look, 1)
                pe.sem_inc(s_trc, 1)
            pe.wait_ge(s_bst, 1)
            nc.tensor.matmul(p_sm[0:1, 128:128 + BODIES], ones[0:NB, :], count_b[0:NB, :], start=True, stop=True).then_inc(s_cntp, 1)
            for k in range(3):
                a, b = k * 56, min(BODIES, (k + 1) * 56)
                bank = (p_rows[0], p_rows[1], p_h[0])[k]
                flat = bank[:, :] if k < 2 else bank[:, :, :, :].rearrange("p a j d -> p (a j d)")
                m = nc.tensor.matmul(flat[0:1, 0:(b - a) * TB], ones[:, :], count_t[:, 0, a * TB:b * TB], start=True, stop=True)
                if k < 2:
                    m.then_inc(s_cntp, 1)
            nc.tensor.matmul(p_sm[0:1, 320:320 + S], col[0:S, 4:5], cst[0:S, IDENT, 0:S], start=True, stop=True).then_inc(s_cntp, 1)

        @block.vector
        def _(dve):
            chain = [0]

            def link(ins):
                chain[0] += 1
                ins.then_inc(s_v, 1)
                dve.wait_ge(s_v, chain[0])

            V = nc.vector
            dve.wait_ge(s_idx, 32)
            for k, ids in enumerate((src_i, dst_i)):
                V.tensor_scalar(blk_i[:, k, :], ids[:, :], 7, None, ALU.arith_shift_right)
                link(V.tensor_scalar(loc_i[:, k, :], ids[:, :], P - 1, None, ALU.bitwise_and))
            V.tensor_copy(loc[:, :, :], loc_i[:, :, :]).then_inc(s_loc, 1)
            link(V.tensor_copy(blk[:, :, :], blk_i[:, :, :]))
            link(V.scalar_tensor_tensor(key[:, :], blk[:, 0, :], float(S), blk[:, 1, :], ALU.mult, ALU.add))
            V.tensor_copy(key16[:, :], key[:, :]).then_inc(s_key, 1)
            dve.wait_ge(s_cst, 32)
            V.memset(ones[:, :], 1.0)
            V.memset(onesq[:, :], 1.0)
            V.tensor_copy(ident16[:, :], cst[:, IDENT, :]).then_inc(s_id16, 1)
            for k, (o, n) in enumerate(((oh_src, S), (oh_dst, NB))):
                i = V.tensor_tensor(o[:, :, :, :].rearrange("p q j s -> p (q j) s"),
                                    cst[0:EP, IOTA, 0:n].unsqueeze(1).to_broadcast([EP, EC, n]),
                                    blk[:, k, :].unsqueeze(2).to_broadcast([EP, EC, n]), ALU.is_equal)
            i.then_inc(s_oh, 1)
            dve.wait_ge(s_att, 64)
            link(V.tensor_copy(w_hi[:, :], w[:, :]))
            V.tensor_tensor(w_rest[:, :], w[:, :], w_hi[:, :], ALU.subtract).then_inc(s_w, 1)
            dve.sem_inc(s_histed, 2)
            with dve.Fori(1, Q // 10 + 1) as n:
                for h in range(2):
                    dve.wait_ge(s_hist, 2 * n - 1 + h)
                    for j in range(J):
                        i = V.tensor_copy(hist[S * j:S * j + S, bass.ds((n - 1) * 10 + 5 * h, 5), :], p_h[h][S * j:S * j + S, :, j, :])
                    i.then_inc(s_histed, 1)
            dve.wait_ge(s_histed, 2 * (Q // 10) + 2)
            TOT, NT, PRE, ST, B0 = 0, 1, 2, 3, 4
            V.tensor_reduce(small[:, TOT, :], hist[:, :, :].rearrange("p q d -> p d q"), AX.X, ALU.add).then_inc(s_tot, 1)
            dve.wait_ge(s_totp, 2)
            link(V.tensor_scalar(small[:, 5, :], p_sm[:, 0:NB], float(P - 1), None, ALU.add))
            link(V.tensor_copy(small_i[:, 0, :], small[:, 5, :]))
            link(V.tensor_scalar(small_i[:, 1, :], small_i[:, 0, :], 7, None, ALU.arith_shift_right))
            link(V.tensor_copy(small[:, NT, :], small_i[:, 1, :]))
            link(V.tensor_reduce(col[:, 0:1], small[:, NT, :], AX.X, ALU.add))
            link(V.tensor_scalar(col[:, 2:3], col[:, 0:1], float(TB - 1), float(TB), ALU.add, ALU.max))
            link(V.tensor_copy(col_i[:, 0:1], col[:, 2:3]))
            link(V.tensor_scalar(col_i[:, 1:2], col_i[:, 0:1], 3, None, ALU.arith_shift_right))
            V.tensor_copy(col[:, 1:2], col_i[:, 1:2]).then_inc(s_tot, 1)
            link(V.tensor_tensor_scan(small[:, 6, :], onesq[:, 0:NB], small[:, NT, :], 0.0, ALU.mult, ALU.add))
            link(V.tensor_tensor(small[:, PRE, :], small[:, 6, :], small[:, NT, :], ALU.subtract))
            dve.wait_ge(s_totp, 3)
            link(V.tensor_scalar(col[:, 3:4], p_sm[:, 64:65], float(TB), None, ALU.mult))
            link(V.tensor_copy(col[:, 4:5], p_sm[:, 64:65]))
            link(V.tensor_scalar(small[:, ST, :], small[:, PRE, :], col[:, 3:4], None, ALU.add))
            link(V.scalar_tensor_tensor(small[:, B0, :], small[:, ST, :], float(P), p_sm[:, 32:32 + NB], ALU.mult, ALU.add))
            link(V.tensor_copy(cum[:, 0, :], small[:, B0, :]))
            for d in range(NB):
                i = V.tensor_tensor_scan(cum[:, 1:Q, d], onesq[:, 0:Q - 1], hist[:, 0:Q - 1, d], small[:, B0, d:d + 1], ALU.mult, ALU.add)
            link(i)
            link(V.tensor_copy(cum_i, cum[:, :, :]))
            link(V.tensor_scalar(part_i[0], cum_i, 8, None, ALU.arith_shift_right))
            link(V.tensor_scalar(part_i[1], cum_i, 255, None, ALU.bitwise_and))
            dve.wait_ge(s_negset, 2)
            for h in range(2):
                for j in range(J):
                    i = V.tensor_copy(lookup[S * j:S * j + S, :, h, j, :], part_i[h][S * j:S * j + S, :, :])
            i.then_inc(s_cnt, 1)
            dve.sem_inc(s_ranked, 2)
            with dve.Fori(1, Q // 2 + 1) as n:
                for h in range(2):
                    dve.wait_ge(s_rows, 2 * n - 1 + h)
                    dve.wait_ge(s_ranked, 2 * n + h)
                    q = (n - 1) * 2 + h
                    for j in range(J):
                        i = V.scalar_tensor_tensor(junk[:, j, :], p_rows[h][0:EP, j * EP:(j + 1) * EP], key[:, bass.ds(q * J + j, 1)],
                                                   cst[0:EP, LOWER, 0:EP], ALU.is_equal, ALU.mult,
                                                   accum_out=rank[:, bass.ds(q, 1), j])
                    i.then_inc(s_ranked, 1)
            dve.wait_ge(s_ranked, Q + 2)
            dve.sem_inc(s_sel, 2)
            k0 = chain[0]
            with dve.Fori(1, Q // 4 + 1) as n:
                step = [0]

                def linkn(ins):
                    step[0] += 1
                    ins.then_inc(s_v, 1)
                    dve.wait_ge(s_v, (n - 1) * 10 + (k0 + step[0]))

                for h in range(2):
                    dve.wait_ge(s_look, 2 * n - 1 + h)
                    o = oh_dst[:, bass.ds((n - 1) * 4 + 2 * h, 2), :, :].rearrange("p q j d -> p q (j d)")
                    linkn(V.tensor_tensor(prod[:, :, :, :], p_h[h][0:EP, 0:4, :, :].rearrange("p (q a) j d -> p q a (j d)", a=2),
                                          o.unsqueeze(2).to_broadcast([EP, 2, 2, J * NB]), ALU.mult))
                    dve.sem_inc(s_sel, 1)
                    linkn(V.tensor_reduce(sel[:, 2 * h:2 * h + 2, :, :].rearrange("p q a j -> p (q a j)"),
                                          prod[:, :, :, :].rearrange("p q a (j d) -> p (q a j) d", d=NB), AX.X, ALU.add))
                linkn(V.scalar_tensor_tensor(pos[:, :, :], sel[:, :, 0, :], 256.0, sel[:, :, 1, :], ALU.mult, ALU.add))
                linkn(V.tensor_tensor(pos_i[:, 0, :].rearrange("p (q j) -> p q j", j=J), pos[:, :, :], rank[:, bass.ds((n - 1) * 4, 4), :], ALU.add))
                linkn(V.tensor_scalar(pos_i[:, 1, :], pos_i[:, 0, :], TB * P - 1, 7, ALU.bitwise_and, ALU.logical_shift_right))
                linkn(V.tensor_scalar(pos_i[:, 2, :], pos_i[:, 0, :], -(TB * P), None, ALU.bitwise_and))
                linkn(V.tensor_tensor(pos_i[:, 3, :], pos_i[:, 1, :], pos_i[:, 2, :], ALU.bitwise_or))
                linkn(V.tensor_scalar(pos_i[:, 4, :], pos_i[:, 0, :], P - 1, 3, ALU.bitwise_and, ALU.logical_shift_left))
                for s in range(2):
                    dve.wait_ge(s_free[s], n + s)
                    k = slice(s * 2 * J, (s + 1) * 2 * J)
                    V.tensor_tensor(index[s][:, :], pos_i[:, 3, k], pos_i[:, 4, k], ALU.bitwise_or).then_inc(s_index[s], 1)
            chain[0] = k0 + 10 * (Q // 4)
            link(V.memset(starts4[:, :], BIG))
            for j in range(J):
                n = len(range(j, NB, J))
                i = V.tensor_copy(starts4[S * j:S * j + NB, 0:n], small[S * j:S * j + NB, ST, j:NB:J])
            link(i)
            link(V.tensor_scalar(count_t[:, 0, :], iota_t[:, :], starts4[:, 0:1], None, ALU.is_ge))
            for k in range(1, 7):
                link(V.scalar_tensor_tensor(count_t[:, k % 2, :], iota_t[:, :], starts4[:, k:k + 1], count_t[:, 1 - k % 2, :], ALU.is_ge, ALU.add))
            V.tensor_scalar(count_b[:, :], iota_t[:, 0:BODIES], col[:, 4:5], None, ALU.is_ge).then_inc(s_bst, 1)
            tiles = BODIES * TB
            tv = tabrow[:, :, 0:TB].rearrange("a b t -> a b t")
            link(V.memset(tabrow[:, :, :], 0.0))
            dve.wait_ge(s_cntp, 4)
            link(V.tensor_scalar(tabrow[:, :, TB:TB + 1].rearrange("a b t -> a (b t)"), p_sm[0:1, 128:128 + BODIES], -1.0, None, ALU.add))
            link(V.tensor_scalar(tabrow[:, :, TB + 1:TB + 2], tabrow[:, :, TB:TB + 1], float(NB), 1.0, ALU.mult, ALU.add))
            for k in range(3):
                a, b = k * 56, min(BODIES, (k + 1) * 56)
                bank = (p_rows[0], p_rows[1], p_h[0])[k]
                flat = bank[:, :] if k < 2 else bank[:, :, :, :].rearrange("p a j d -> p (a j d)")
                i = V.tensor_tensor(tabrow[:, a:b, 0:TB], flat[0:1, 0:(b - a) * TB].rearrange("a (b t) -> a b t", t=TB),
                                    tabrow[:, a:b, TB + 1:TB + 2].to_broadcast([1, b - a, TB]), ALU.subtract)
            link(i)
            link(V.tensor_tensor(tabrow[:, 1:BODIES, TNEW:TNEW + 1], tabrow[:, 1:BODIES, TB:TB + 1],
                                 tabrow[:, 0:BODIES - 1, TB:TB + 1], ALU.subtract))
            for h, c in enumerate(TPACK):
                at = tabrow[:, :, c:c + 1]
                link(V.scalar_tensor_tensor(at, tabrow[:, :, G * h + 3:G * h + 4], float(1 << BITS), tabrow[:, :, G * h + 2:G * h + 3], ALU.mult, ALU.add))
                for t in (1, 0):
                    link(V.scalar_tensor_tensor(at, at, float(1 << BITS), tabrow[:, :, G * h + t:G * h + t + 1], ALU.mult, ALU.add))
            V.tensor_copy(bst_i[:, :], p_sm[0:1, 320:320 + S])
            link(V.tensor_copy(tabrow_i[:, :, :], tabrow[:, :, :]))
            link(V.tensor_scalar(above_i[:, :, :], tabrow_i[:, :, TSRC:TSRC + 1], G * BITS, None, ALU.logical_shift_left))
            for c in TPACK:
                i = V.tensor_tensor(tabrow_i[:, :, c:c + 1], tabrow_i[:, :, c:c + 1], above_i[:, :, :], ALU.bitwise_or)
            i.then_inc(s_tab, 1)
    clear(nc, used)


def clear(nc, semaphores):
    numbers = [x.num for x in semaphores]
    with nc.Block() as block:
        @block.sync
        def _(sp):
            sp.sem_clear(range(min(numbers), max(numbers) + 1))


class Flag:

    def __init__(self, semaphore):
        self.semaphore = semaphore

    def after(self, engine, n):
        engine.wait_ge(self.semaphore, n + 1)

    def before(self, engine, n):
        engine.wait_ge(self.semaphore, n)

    def set_by(self, instruction):
        instruction.then_inc(self.semaphore, 1)


def group(n, k):
    return n + k // U * U, k % U


class Counter:

    def __init__(self, semaphore):
        self.semaphore = semaphore

    def after(self, engine, n, s):
        engine.wait_ge(self.semaphore, n + (s + U))

    def before(self, engine, n, s, depth):
        engine.wait_ge(self.semaphore, n + (s + U - depth))

    def set_by(self, instruction):
        instruction.then_inc(self.semaphore, 1)


class Chain:

    def __init__(self, engine, sems, n, s):
        self.engine, self.sems, self.value, self.at = engine, sems, n + s, 0

    def link(self, instruction):
        semaphore = self.sems[self.at]
        self.at += 1
        instruction.then_inc(semaphore, 1)
        self.engine.wait_ge(semaphore, self.value)


def round_end(last):
    return ((last + 3) >> 2) * U + 1


def body_of(nc, n, s):
    if isinstance(n, int):
        return (n >> 1) + s // 2
    return nc.s_assert_within((n >> 1) + s // 2, 0, BODIES - 1,
                              skip_runtime_bounds_check_because="BODIES counts the round behind the last body too")


def blocks_of(nc, engine, table, n, s, source=True, targets=True):
    c = TPACK[s % 2]
    packed = engine.value_load(table[0:1, bass.ds(body_of(nc, n, s), 1), c], min_val=0, max_val=(1 << (G + 1) * BITS) - 1)

    def block(value):
        return nc.snap(value, engines=[engine.engine], min_val=0, max_val=NB - 1)

    return (block(packed >> (G * BITS)) if source else None,
            [block((packed >> (BITS * t)) & ((1 << BITS) - 1)) for t in range(G)] if targets else None)


def staged(n, j, *stages):
    for stage, ahead in stages:
        if j + ahead >= 0:
            stage(*group(n, j + ahead))


def in_turn(make, depth):
    made = [make(k) for k in range(depth)]
    return [made[s % depth] for s in range(U)]


def edges_of(dram):
    return dram["edges"].rearrange("(b p t) c -> b p (t c)", p=P, t=TB)


def load_nodes_phase(nc, io, keep):
    used = []
    ctx = ExitStack()
    with ctx:
        def sb(name, shape, dt):
            return ctx.enter_context(nc.sbuf_tensor("i_" + name, shape, dt))

        def sem(name):
            used.append(ctx.enter_context(nc.semaphore("i_" + name)))
            return used[-1]

        x, tab, ident = keep["x"], keep["tab"], keep["ident"]
        xT = sb("xT", [D, NP], F32)
        wsd = sb("wsd", [D, 4, H1], F32)
        rest = sb("rest", [P, 2, 4 * H1], F32)
        p_x = [ctx.enter_context(nc.psum_tensor(f"i_p_x{i}", [D, 4, P], F32)) for i in range(2)]
        p_y = [ctx.enter_context(nc.psum_tensor(f"i_p_y{i}", [P, 4 * H1], F32)) for i in range(2)]
        n_zero, n_load, n_w = sem("n_zero"), sem("n_load"), sem("n_w")
        n_t, n_tc, n_y, n_ys, n_v = sem("n_t"), sem("n_tc"), sem("n_y"), sem("n_ys"), sem("n_v")
        groups = [(b, min(4, NB - b)) for b in range(0, NB, 4)]
        block = ctx.enter_context(nc.Block())

        @block.sync
        def _(sp):
            sp.dma_start(ident[:, :], io["sort_consts"][:, 0, :]).then_inc(n_w, 16)
            wf, wb = io["L0_gnn_W1f"], io["L0_gnn_W1b"]
            for k, part in enumerate((wf[D:2 * D, :], wb[0:D, :], wf[0:D, :], wb[D:2 * D, :])):
                sp.dma_start(wsd[:, k, :], part).then_inc(n_w, 16)
            sp.wait_ge(n_zero, 1)
            sp.dma_start(x[:, 0:NB - 1, :], io["x"][0:(NB - 1) * P, :].rearrange("(b p) f -> p b f", p=P)).then_inc(n_load, 16)
            sp.dma_start(x[0:LAST, NB - 1, :], io["x"][(NB - 1) * P:N, :]).then_inc(n_load, 16)

        @block.tensor
        def _(pe):
            pe.wait_ge(n_load, 32)
            pe.wait_ge(n_w, 80)
            for g, (b0, nb) in enumerate(groups):
                if g >= 2:
                    pe.wait_ge(n_tc, g - 1)
                for k in range(nb):
                    i = nc.tensor.transpose(p_x[g % 2][:, k, :], x[:, b0 + k, :], ident[:, :])
                i.then_inc(n_t, 1)
            for b in range(NB):
                pe.wait_ge(n_tc, b // 4 + 1)
                if b >= 2:
                    pe.wait_ge(n_ys, b - 1)
                nc.tensor.matmul(p_y[b % 2][:, :], xT[:, b * P:(b + 1) * P], wsd[:, :, :], start=True, stop=True).then_inc(n_y, 1)

        @block.scalar
        def _(act):
            for g, (b0, nb) in enumerate(groups):
                act.wait_ge(n_t, g + 1)
                nc.scalar.copy(xT[:, b0 * P:(b0 + nb) * P], p_x[g % 2][:, 0:nb, :].rearrange("p k n -> p (k n)")).then_inc(n_tc, 1)

        @block.vector
        def _(dve):
            V = nc.vector
            V.memset(x[:, NB - 1, :], 0.0).then_inc(n_zero, 1)
            k = 0
            for b in range(NB):
                dve.wait_ge(n_y, b + 1)
                y, r = p_y[b % 2][:, :], rest[:, b % 2, :]
                V.tensor_copy(tab[:, b, 0, :], y).then_inc(n_v, 1)
                dve.wait_ge(n_v, k + 1)
                V.tensor_tensor(r, y, tab[:, b, 0, :], ALU.subtract).then_inc(n_ys, 1)
                dve.wait_ge(n_ys, b + 1)
                V.tensor_copy(tab[:, b, 1, :], r).then_inc(n_v, 1)
                dve.wait_ge(n_v, k + 2)
                V.tensor_tensor(tab[:, b, 2, :], r, tab[:, b, 1, :], ALU.subtract)
                k += 2
    clear(nc, used)


MEETS = (0, 1, 2, 0, 1, 0)


def cut_weights(dve, V, chain, whole, parts, at=0):
    steps = (lambda: V.tensor_copy(parts[:, 0, :], whole), lambda: V.tensor_tensor(whole, whole, parts[:, 0, :], ALU.subtract),
             lambda: V.tensor_copy(parts[:, 1, :], whole), lambda: V.tensor_tensor(parts[:, 2, :], whole, parts[:, 1, :], ALU.subtract))
    for k, step in enumerate(steps):
        step().then_inc(chain, 1)
        dve.wait_ge(chain, at + k + 1)


def layer0_edges_phase(nc, io, dram, keep):
    used = []
    ctx = ExitStack()
    with ctx:
        def sb(name, shape, dt):
            return ctx.enter_context(nc.sbuf_tensor("e_" + name, shape, dt))

        def ps(name, shape, dt=F32):
            return ctx.enter_context(nc.psum_tensor("e_" + name, shape, dt))

        def sem(name):
            used.append(ctx.enter_context(nc.semaphore("e_" + name)))
            return used[-1]

        def counter(name):
            primed.append(Counter(sem(name)))
            return primed[-1]

        LATER = U // 2
        primed = []
        tab, agg, ident = keep["tab"], keep["agg"], keep["ident"]
        slots = range(U)
        table = sb("table", [1, BODIES, TAB], I32)
        turns = sb("turns", [1, BODIES + LATER, TAB], I32)
        starts = sb("starts", [1, S], I32)
        iota = sb("iota", [P, P], F32)
        iotab = sb("iotab", [P, P], BF16)
        identb = sb("identb", [P, P], BF16)
        w1e = sb("w1e", [6 * 16, 2, H1], F32)
        w1_parts = sb("w1_parts", [6 * 16, 3, 2 * H1], BF16)
        w1s = sb("w1s", [6 * 16, 2 * H1], BF16)
        b1 = sb("b1", [P, 1], F32)
        w2 = sb("w2", [P, 2, D], F32)
        b2 = sb("b2", [1, G, 2, D], F32)
        ones = sb("ones", [1, P], F32)
        zeros = sb("zeros", [P, 2 * P], F32)
        strip = sb("strip", [P, 3, 2, NP], F32)
        spare = sb("spare", [1, 16], F32)
        rec = in_turn(lambda s: sb(f"rec{s}", [P, G, REC], F32), U)
        wmid = in_turn(lambda s: sb(f"wmid{s}", [P, G], BF16), 4)
        wlow = in_turn(lambda s: sb(f"wlow{s}", [P, G], F32), 4)
        oh = in_turn(lambda s: sb(f"oh{s}", [P, 2, G, P], BF16), U)
        ohw = in_turn(lambda s: sb(f"ohw{s}", [P, G, 3, P], BF16), 4)
        attr = in_turn(lambda s: sb(f"attr{s}", [P, G, 6, 16], BF16), 4)
        arest = in_turn(lambda s: sb(f"arest{s}", [P, G, 16], F32), 4)
        recT = in_turn(lambda s: sb(f"recT{s}", [6 * 16, G * P], BF16), 2)
        ohT = in_turn(lambda s: sb(f"ohT{s}", [P, 2, G, P], BF16), 2)
        hid = in_turn(lambda s: sb(f"hid{s}", [P, G, P], F32), 2)
        flow = in_turn(lambda s: sb(f"flow{s}", [P, G, 2 * D], F32), 2)
        rest = in_turn(lambda s: sb(f"rest{s}", [P, G, 2 * D], F32), 2)
        part = in_turn(lambda s: sb(f"part{s}", [P, G, 3, 2 * D + 2], BF16), 4)
        p_rec = ps("p_rec", [6 * 16, G, P], BF16)
        p_oh = ps("p_oh", [P, 2, G, P], BF16)
        p_hid = ps("p_hid", [P, G * P])
        p_flow = ps("p_flow", [P, G, 2 * D])
        p_sum = ps("p_sum", [P, G + 1, 2 * D])
        p_aw = [ps(f"p_aw{i}", [P, 2, 2 * P]) for i in range(2)]

        loaded = [sem(f"loaded{s}") for s in slots]
        w_chain = sem("w_chain")
        d_const, d_w, d_b, d_start, d_flush, d_zero = sem("d_const"), sem("d_w"), sem("d_b"), sem("d_start"), sem("d_flush"), sem("d_zero")
        prime = sem("prime")
        setup = sem("setup")
        onehots, turned = counter("onehots"), counter("turned")
        recT_copied, ohT_copied = counter("recT_copied"), counter("ohT_copied")
        hid_done, hid_relued = counter("hid_done"), counter("hid_relued")
        aw_done, aw_added = ([counter(f"{name}{u}") for u in range(2)] for name in ("aw_done", "aw_added"))
        flow_cut, hi_cut = counter("flow_cut"), counter("hi_cut")
        flow_done = counter("flow_done")
        split, sum_done, sum_added = counter("split"), counter("sum_done"), counter("sum_added")
        weighted = counter("weighted")
        attr_hi, attr_rest, attr_mid, attr_cut = counter("attr_hi"), counter("attr_rest"), counter("attr_mid"), counter("attr_cut")
        rest_cut, mid_cut = counter("rest_cut"), counter("mid_cut")
        pool_chain = [sem(f"pool_chain{i}") for i in range(2)]
        dve_chain = [sem(f"dve_chain{i}") for i in range(6)]
        block = ctx.enter_context(nc.Block())
        ev = edges_of(dram)

        @block.sync
        def _(sp):
            for f in primed:
                sp.sem_inc(f.semaphore, U)
            sp.dma_start(table[:, :, :], dram["table"].unsqueeze(0)).then_inc(d_start, 16)
            sp.dma_start(turns[:, LATER:BODIES + LATER, :], dram["table"].unsqueeze(0)).then_inc(d_start, 16)
            sp.dma_start(turns[:, 0:LATER, :], dram["table"][0:1, :].unsqueeze(0).to_broadcast([1, LATER, TAB])).then_inc(d_start, 16)
            sp.dma_start(starts[:, :], dram["starts"].unsqueeze(0)).then_inc(d_start, 16)
            sp.dma_start(iota[:, :], io["sort_consts"][:, 1, :]).then_inc(d_const, 16)
            sp.dma_start(spare[:, :], io["sort_consts"][0:1, 1, 0:16]).then_inc(d_flush, 16)
            sp.wait_ge(setup, 1)
            for k, (wn, name) in enumerate(((1, "f"), (0, "b"))):
                for i in range(6):
                    sp.dma_start(w1e[16 * i:16 * i + 16, k, :], io["L0_gnn_W1" + name][2 * D:2 * D + 16, :]).then_inc(d_b, 16)
                sp.dma_start(b1[k * H1:(k + 1) * H1, :], io["L0_gnn_b1" + name].unsqueeze(1)).then_inc(d_b, 16)
                sp.dma_start(w2[k * H1:(k + 1) * H1, wn, :], io["L0_gnn_W2" + name]).then_inc(d_b, 16)
                sp.dma_start(b2[:, :, wn, :], io["L0_gnn_b2" + name].unsqueeze(0).unsqueeze(0).to_broadcast([1, G, D])).then_inc(d_b, 16)
            sp.wait_ge(w_chain, 4)
            for i, k in enumerate(MEETS):
                sp.dma_start(w1s[16 * i:16 * i + 16, :], w1_parts[16 * i:16 * i + 16, k, :]).then_inc(d_w, 16)
            zs = zeros[:, :].unsqueeze(1).to_broadcast([P, NB, 2 * P])

            def flat(at):
                return at.rearrange("p a k x -> p (a k x)")

            for k in range(2):
                sp.dma_start(flat(strip[:, k:k + 1, :, :]).rearrange("p (b c) -> p b c", c=2 * P), zs).then_inc(d_zero, 16)
                sp.wait_ge(d_zero, 16 * (k + 1))
            sp.wait_ge(d_start, 64)
            last = sp.value_load(starts[0:1, NB:NB + 1], min_val=NB, max_val=BODIES - U)

            def one_strip(k):
                return strip[:, bass.ds(k % 3, 1), :, :]

            with sp.Fori(1, round_end(last) + U, U) as n:
                for s in slots:
                    onehots.before(sp, n, s, U)
                    weighted.before(sp, n, s, U)
                    attr_rest.before(sp, n, s, U)
                    body = body_of(nc, n, s)
                    sp.dma_start(rec[s][:, :, :].rearrange("p t c -> p (t c)"),
                                 ev[bass.ds(body, 1), :, (s % 2) * G * REC:(s % 2 + 1) * G * REC].rearrange("b p c -> p (b c)")).then_inc(loaded[s], 16)
                    if s % 2 == 0:
                        continue
                    new = sp.value_load(turns[0:1, bass.ds(body, 1), TNEW], min_val=0, max_val=1)
                    with sp.If(new):
                        src = sp.value_load(turns[0:1, bass.ds(body, 1), TSRC], min_val=1, max_val=NB - 1)
                        aw_added[1].before(sp, n, s - 1 - 2 * LATER, 1)
                        sp.sem_inc(prime, 1)
                        sp.wait_ge(d_flush, src * 16)
                        sp.sem_inc(prime, 1)
                        sp.dma_start(dram["strips"][bass.ds(src - 1, 1), :, :, :].rearrange("a p k x -> p (a k x)"),
                                     flat(one_strip(src - 1))).then_inc(d_flush, 16)
                        sp.wait_ge(d_zero, src * 16 + 16)
                        sp.sem_inc(prime, 1)
                        sp.dma_start(flat(one_strip(src + 1)).rearrange("p (b c) -> p b c", c=2 * P), zs).then_inc(d_zero, 16)
            for s in slots:
                sp.wait_ge(loaded[s], round_end(last) * 2 + 14)
                sp.sem_inc(prime, 1)
            aw_added[1].after(sp, round_end(last), 0)
            sp.sem_inc(prime, 1)
            sp.wait_ge(d_flush, NB * 16)
            sp.dma_start(dram["strips"][NB - 1, :, :, :].rearrange("p k x -> p (k x)"),
                         strip[:, (NB - 1) % 3, :, :].rearrange("p k x -> p (k x)")).then_inc(d_flush, 16)
            sp.wait_ge(d_flush, NB * 16 + 16)
            sp.wait_ge(d_zero, NB * 16 + 16)

        @block.gpsimd
        def _(pool):
            g = nc.gpsimd
            pool.wait_ge(d_start, 64)
            last = pool.value_load(starts[0:1, NB:NB + 1], min_val=NB, max_val=BODIES - U)

            def weigh(n, s):
                onehots.after(pool, n, s)
                aw_done[1].before(pool, n, s, 4)
                pool.sem_inc(prime, 1)
                g.tensor_copy(wmid[s][:, :], rec[s][:, :, CR]).then_inc(pool_chain[0], 1)
                pool.wait_ge(pool_chain[0], n + s)
                g.tensor_tensor(wlow[s][:, :], rec[s][:, :, CR], wmid[s][:, :], ALU.subtract).then_inc(pool_chain[1], 1)
                pool.wait_ge(pool_chain[1], n + s)
                for k, w in enumerate((rec[s][:, :, CW], rec[s][:, :, CR], wlow[s][:, :])):
                    i = g.tensor_tensor(ohw[s][:, :, k, :], oh[s][:, 0, :, :], w.unsqueeze(2).to_broadcast([P, G, P]), ALU.mult)
                weighted.set_by(i)

            def attributes_rest(n, s):
                attr_hi.after(pool, n, s)
                pool.sem_inc(prime, 1)
                attr_rest.set_by(g.tensor_tensor(arest[s][:, :, :], rec[s][:, :, C16:C16 + 16], attr[s][:, :, 0, :], ALU.subtract))

            def attributes_low(n, s):
                attr_mid.after(pool, n, s)
                pool.sem_inc(prime, 1)
                attr_cut.set_by(g.tensor_tensor(attr[s][:, :, 5, :], arest[s][:, :, :], attr[s][:, :, 3, :], ALU.subtract))

            def flow_rest(n, s):
                hi_cut.after(pool, n, s)
                pool.sem_inc(prime, 1)
                rest_cut.set_by(g.tensor_tensor(rest[s][:, :, :], flow[s][:, :, :], part[s][:, :, 0, 1:2 * D + 1], ALU.subtract))

            def flow_low(n, s):
                mid_cut.after(pool, n, s)
                pool.sem_inc(prime, 1)
                split.set_by(g.tensor_tensor(part[s][:, :, 2, 1:2 * D + 1], rest[s][:, :, :], part[s][:, :, 1, 1:2 * D + 1], ALU.subtract))

            pool.wait_ge(setup, 2)
            for s in range(4):
                attributes_rest(1, s); attributes_low(1, s)
            weigh(1, 0); weigh(1, 1); weigh(1, 2); flow_rest(1, 0); flow_low(1, 0)
            with pool.Fori(1, round_end(last), U) as n:
                for j in slots:
                    flow_rest(*group(n, j + 1))
                    attributes_rest(*group(n, j + 4))
                    flow_low(*group(n, j + 1))
                    attributes_low(*group(n, j + 4))
                    weigh(*group(n, j + 3))

        @block.scalar
        def _(act):
            act.wait_ge(d_start, 64)
            last = act.value_load(starts[0:1, NB:NB + 1], min_val=NB, max_val=BODIES - U)
            act.wait_ge(d_b, 288)

            def copies(n, s):
                turned.after(act, n, s)
                hid_done.before(act, n, s, 2)
                recT_copied.set_by(nc.scalar.copy(recT[s][:, :], p_rec[:, :, :].rearrange("p t e -> p (t e)")))
                ohT_copied.set_by(nc.scalar.copy(ohT[s][:, :, :, :], p_oh[:, :, :, :]))

            def attributes(n, s):
                act.wait_ge(loaded[s], n * 2 + 14)
                turned.before(act, n, s, 4)
                act.sem_inc(prime, 1)
                wide = [P, G, 3, 16]
                attr_hi.set_by(nc.scalar.copy(attr[s][:, :, 0:3, :], rec[s][:, :, C16:C16 + 16].unsqueeze(2).to_broadcast(wide)))

            def attributes_mid(n, s):
                attr_rest.after(act, n, s)
                attr_mid.set_by(nc.scalar.copy(attr[s][:, :, 3:5, :], arest[s][:, :, :].unsqueeze(2).to_broadcast([P, G, 2, 16])))

            def middle(n, s):
                rest_cut.after(act, n, s)
                mid_cut.set_by(nc.scalar.copy(part[s][:, :, 1, 1:2 * D + 1], rest[s][:, :, :]))

            def relu1(n, s):
                hid_done.after(act, n, s)
                flow_done.before(act, n, s, 2)
                hid_relued.set_by(nc.scalar.activation(hid[s][:, :, :].rearrange("p t e -> p (t e)"), p_hid[:, :], ACT.Relu, bias=b1[:, :]))

            def relu2(n, s):
                flow_done.after(act, n, s)
                rest_cut.before(act, n, s, 2)
                sum_done.before(act, n, s, 4)
                flow_cut.set_by(nc.scalar.activation(flow[s][:, :, :], p_flow[:, :, :], ACT.Relu))
                hi_cut.set_by(nc.scalar.activation(part[s][:, :, 0, 1:2 * D + 1], p_flow[:, :, :], ACT.Relu))

            act.wait_ge(setup, 2)
            for s in range(4):
                attributes(1, s); attributes_mid(1, s)
            copies(1, 0)
            copies(1, 1); relu1(1, 0)
            copies(1, 2); relu1(1, 1); relu2(1, 0); middle(1, 0)
            with act.Fori(1, round_end(last), U) as n:
                for j in slots:
                    relu1(*group(n, j + 2))
                    copies(*group(n, j + 3))
                    relu2(*group(n, j + 1))
                    attributes(*group(n, j + 4))
                    middle(*group(n, j + 1))
                    attributes_mid(*group(n, j + 4))

        @block.tensor
        def _(pe):
            mm = nc.tensor.matmul
            pe.wait_ge(d_start, 64)
            last = pe.value_load(starts[0:1, NB:NB + 1], min_val=NB, max_val=BODIES - U)
            pe.wait_ge(d_b, 288)
            pe.wait_ge(d_w, 96)
            pe.wait_ge(setup, 2)

            def turn(n, s):
                attr_cut.after(pe, n, s)
                recT_copied.before(pe, n, s, 1)
                for t in range(G):
                    nc.tensor.transpose(p_rec[:, t, :], attr[s][:, t, :, :].rearrange("p k f -> p (k f)"), identb[:, :])
                onehots.after(pe, n, s)
                ohT_copied.before(pe, n, s, 1)
                for k in range(2):
                    for t in range(G):
                        i = nc.tensor.transpose(p_oh[:, k, t, :], oh[s][:, k, t, :], identb[:, :])
                turned.set_by(i)

            def hidden(n, s, blocks):
                src, dsts = blocks
                hid_relued.before(pe, n, s, 1)
                recT_copied.after(pe, n, s)
                mm(p_hid[:, :], w1s[:, :], recT[s][:, :], start=True, stop=False, skip_group_check=True)
                ohT_copied.after(pe, n, s)
                for k in range(3):
                    mm(p_hid[:, :], tab[:, bass.ds(src, 1), k, 0:P], ohT[s][:, 0, :, :], start=False, stop=False, skip_group_check=True)
                for t in range(G):
                    for k in range(3):
                        i = mm(p_hid[:, t * P:(t + 1) * P], tab[:, bass.ds(dsts[t], 1), k, P:2 * P], ohT[s][:, 1, t, :],
                               start=False, stop=(t == G - 1 and k == 2), skip_group_check=True)
                hid_done.set_by(i)

            def dense(n, s):
                weighted.after(pe, n, s)
                for u in range(2):
                    aw_added[u].before(pe, n, s, 1)
                    for v in range(2):
                        t = 2 * u + v
                        mm(p_aw[u][:, v, 0:P], oh[s][:, 0, t, :], oh[s][:, 1, t, :], start=True, stop=True, skip_group_check=True)
                        for k in range(3):
                            i = mm(p_aw[u][:, v, P:2 * P], oh[s][:, 1, t, :], ohw[s][:, t, k, :], start=(k == 0), stop=(k == 2),
                                   skip_group_check=True)
                    aw_done[u].set_by(i)

            def second(n, s):
                hi_cut.before(pe, n, s, 1)
                mm(p_flow[:, :, :], ones[:, :], b2[:, :, :, :], start=True, stop=False, skip_group_check=True)
                hid_relued.after(pe, n, s)
                for t in range(G):
                    i = mm(p_flow[:, t, :], hid[s][:, t, :], w2[:, :, :], start=False, stop=(t == G - 1), skip_group_check=True)
                flow_done.set_by(i)

            def sums(n, s):
                sum_added.before(pe, n, s, 1)
                split.after(pe, n, s)
                for t in range(G):
                    for k in range(3):
                        mm(p_sum[:, G, 0:D + 1], oh[s][:, 0, t, :], part[s][:, t, k, 0:D + 1], start=(t == 0 and k == 0),
                           stop=(t == G - 1 and k == 2), skip_group_check=True)
                for t in range(G):
                    for k in range(3):
                        i = mm(p_sum[:, t, 0:D + 1], oh[s][:, 1, t, :], part[s][:, t, k, D + 1:2 * D + 2], start=(k == 0), stop=(k == 2),
                               skip_group_check=True)
                sum_done.set_by(i)

            turn(1, 0)
            turn(1, 1); hidden(1, 0, blocks_of(nc, pe, table, 1, 0)); dense(1, 0)
            turn(1, 2); hidden(1, 1, blocks_of(nc, pe, table, 1, 1)); second(1, 0)
            with pe.Fori(1, round_end(last), U) as n:
                for j in slots:
                    blocks = blocks_of(nc, pe, table, *group(n, j + 2))
                    dense(*group(n, j + 1))
                    hidden(*group(n, j + 2), blocks)
                    turn(*group(n, j + 3))
                    second(*group(n, j + 1))
                    sums(*group(n, j))

        @block.vector
        def _(dve):
            V = nc.vector
            V.memset(w2[:, :, :], 0.0)
            V.memset(ones[:, :], 1.0)
            V.memset(zeros[:, :], 0.0).then_inc(setup, 1)
            V.memset(agg[:, :, :], 0.0)
            for s in range(4):
                V.memset(part[s][:, :, :, :], 0.0).then_inc(dve_chain[s], 1)
                dve.wait_ge(dve_chain[s], 1)
                dve.sem_clear(dve_chain[s])
                for c in (OUT_DEGREE, IN_DEGREE):
                    V.memset(part[s][:, :, 0, c:c + 1], 1.0)
            dve.wait_ge(d_const, 16)
            V.tensor_copy(iotab[:, :], iota[:, :])
            V.tensor_copy(identb[:, :], ident[:, :]).then_inc(setup, 1)
            dve.wait_ge(d_b, 288)
            cut_weights(dve, V, w_chain, w1e[:, :, :].rearrange("p k h -> p (k h)"), w1_parts)
            dve.wait_ge(setup, 2)
            dve.wait_ge(d_start, 64)
            last = dve.value_load(starts[0:1, NB:NB + 1], min_val=NB, max_val=BODIES - U)

            def one_hots(n, s):
                dve.wait_ge(loaded[s], n * 2 + 14)
                sum_done.before(dve, n, s, U)
                for t in range(G):
                    for k, c in enumerate((CSRC, CDST)):
                        i = V.tensor_scalar(oh[s][:, k, t, :], iotab[:, :], rec[s][:, t, c:c + 1], None, ALU.is_equal)
                onehots.set_by(i)

            def add_dense(n, s, blocks):
                src, dsts = blocks
                turn = src % 3
                dve.wait_ge(d_zero, (src + 1) * 16)
                for u in range(2):
                    aw_done[u].after(dve, n, s)
                    for v in range(2):
                        at = strip[:, bass.ds(turn, 1), :, bass.ds(dsts[2 * u + v] * P, P)].rearrange("p a k c -> p (a k) c")
                        i = V.tensor_tensor(at, p_aw[u][:, v, :].rearrange("p (k c) -> p k c", k=2), at, ALU.add)
                        if v:
                            aw_added[u].set_by(i)
                            aw_added[u].after(dve, n, s)
                        else:
                            i.then_inc(dve_chain[u], 1)
                            dve.wait_ge(dve_chain[u], n + s)

            def add_sums(n, s, blocks):
                src, dsts = blocks
                sum_done.after(dve, n, s)
                at = agg[:, bass.ds(src, 1), 0:D + 1].rearrange("p a c -> p (a c)")
                V.tensor_tensor(at, p_sum[:, G, 0:D + 1], at, ALU.add).then_inc(dve_chain[2], 1)
                for t in range(G):
                    at = agg[:, bass.ds(dsts[t], 1), D + 1:2 * D + 2].rearrange("p a c -> p (a c)")
                    i = V.tensor_tensor(at, p_sum[:, t, 0:D + 1], at, ALU.add)
                    if t < G - 1:
                        i.then_inc(dve_chain[3 + t], 1)
                        dve.wait_ge(dve_chain[3 + t], n + s)
                    else:
                        sum_added.set_by(i)
                        sum_added.after(dve, n, s)

            for s in range(4):
                one_hots(1, s)
            add_dense(1, 0, blocks_of(nc, dve, table, 1, 0))
            with dve.Fori(1, round_end(last), U) as n:
                for j in slots:
                    one_hots(*group(n, j + 4))
                    now = ahead if j else blocks_of(nc, dve, table, n, 0)
                    ahead = blocks_of(nc, dve, table, *group(n, j + 1))
                    add_dense(*group(n, j + 1), ahead)
                    add_sums(*group(n, j), now)
    clear(nc, used)


EPS = 1e-5
RT3, ALPHA_MSG, ALPHA_SELF = 3.0 ** -0.5, 16.0 ** -0.5 / 16.0 ** 0.5, 8.0 ** -0.5
MUL = 8
H2 = 64
NTP = 4 * MUL * MUL
STEPS2, ALPHA2 = 10, 0.1
STEPS3 = 3
EXACT = 256.0


def layernorm(dve, V, link, x, r, tmp, std, std_ready, rooted):
    wide = [P, NB, D]
    link(V.tensor_reduce(std[:, 0, :], r[:, :, :], AX.X, ALU.add))
    link(V.tensor_scalar(std[:, 0, :], std[:, 0, :], 1.0 / D, None, ALU.mult))
    link(V.tensor_tensor(r[:, :, :], r[:, :, :], std[:, 0, :].unsqueeze(2).to_broadcast(wide), ALU.subtract))
    link(V.tensor_tensor(tmp[:, :, :], r[:, :, :], r[:, :, :], ALU.mult))
    link(V.tensor_reduce(std[:, 1, :], tmp[:, :, :], AX.X, ALU.add))
    V.tensor_scalar(std[:, 1, :], std[:, 1, :], 1.0 / D, EPS, ALU.mult, ALU.add).then_inc(std_ready, 1)
    dve.wait_ge(rooted, 1)
    link(V.reciprocal(std[:, 3, :], std[:, 2, :]))
    link(V.tensor_tensor(x[:, :, :], r[:, :, :], std[:, 3, :].unsqueeze(2).to_broadcast(wide), ALU.mult))


def nodes_phase(nc, io, keep, layer):
    used = []
    ctx = ExitStack()
    with ctx:
        def sb(name, shape, dt=F32):
            return ctx.enter_context(nc.sbuf_tensor(f"n{layer}_{name}", shape, dt))

        def sem(name):
            used.append(ctx.enter_context(nc.semaphore(f"n{layer}_{name}")))
            return used[-1]

        x, agg, ident, xp = keep["x"], keep["agg"], keep["ident"], keep["xp"]
        K = 2 * D if layer == 0 else D
        turned = sb("turned", [K, NP])
        w1 = sb("w1", [K, 2 * D])
        b1 = sb("b1", [2 * D, 1])
        z = sb("z", [2 * D + 1, NP])
        w2 = sb("w2", [2 * D + 1, D])
        r = sb("r", [P, NB, D])
        tmp = sb("tmp", [P, NB, D])
        std = sb("std", [P, 4, NB])
        p_t = [ctx.enter_context(nc.psum_tensor(f"n{layer}_p_t{i}", [K, 4, P], F32)) for i in range(2)]
        p_z = [ctx.enter_context(nc.psum_tensor(f"n{layer}_p_z{i}", [2 * D, 512], F32)) for i in range(2)]
        p_o = [ctx.enter_context(nc.psum_tensor(f"n{layer}_p_o{i}", [P, 16, D], F32)) for i in range(2)]
        s_w, s_t, s_tc, s_z, s_zc, s_o, s_v = sem("w"), sem("t"), sem("tc"), sem("z"), sem("zc"), sem("o"), sem("v")
        s_std, s_root, s_zero = sem("std"), sem("root"), sem("zero")
        groups = [(b, min(4, NB - b)) for b in range(0, NB, 4)]
        halves = [(0, 16), (16, NB - 16)]
        loads = 5 if layer == 0 else 4
        block = ctx.enter_context(nc.Block())

        @block.sync
        def _(sp):
            if layer == 0:
                sp.dma_start(w1[0:D, :], io["L0_gnn_W1n"][D:2 * D, :]).then_inc(s_w, 16)
                sp.dma_start(w1[D:2 * D, :], io["L0_gnn_W1n"][0:D, :]).then_inc(s_w, 16)
                sp.dma_start(b1[:, :], io["L0_gnn_b1n"].unsqueeze(1)).then_inc(s_w, 16)
                sp.dma_start(w2[0:2 * D, :], io["L0_gnn_W2n"]).then_inc(s_w, 16)
                sp.dma_start(w2[2 * D:2 * D + 1, :], io["L0_gnn_b2n"].unsqueeze(0)).then_inc(s_w, 16)
            else:
                sp.wait_ge(s_zero, 1)
                sp.dma_start(w1[0:MUL, 0:MUL], io["L1_gnn_Ws"]).then_inc(s_w, 16)
                for i in range(3):
                    sp.dma_start(w1[MUL + i:D:3, MUL + i:D:3], io["L1_gnn_Wv"], allow_slow_non_contiguous=True).then_inc(s_w, 16)

        @block.tensor
        def _(pe):
            what = agg[:, :, 1:K + 1] if layer == 0 else x[:, :, 0:K]
            for g, (b0, nb) in enumerate(groups):
                if g >= 2:
                    pe.wait_ge(s_tc, g - 1)
                for k in range(nb):
                    i = nc.tensor.transpose(p_t[g % 2][:, k, :], what[:, b0 + k, :], ident[:, :])
                i.then_inc(s_t, 1)
            pe.wait_ge(s_w, 16 * loads)
            pe.wait_ge(s_tc, len(groups))
            if layer == 0:
                for g, (b0, nb) in enumerate(groups):
                    if g >= 2:
                        pe.wait_ge(s_zc, g - 1)
                    nc.tensor.matmul(p_z[g % 2][:, 0:nb * P], w1[:, :], turned[:, b0 * P:(b0 + nb) * P], start=True, stop=True).then_inc(s_z, 1)
                pe.wait_ge(s_zc, len(groups))
                pe.wait_ge(s_zero, 1)
            for h, (b0, nb) in enumerate(halves):
                for k in range(nb):
                    at = slice((b0 + k) * P, (b0 + k + 1) * P)
                    if layer == 0:
                        i = nc.tensor.matmul(p_o[h][:, k, :], z[:, at], w2[:, :], start=True, stop=True, skip_group_check=True)
                    else:
                        i = nc.tensor.matmul(p_o[h][:, k, :], turned[:, at], w1[:, 0:D], start=True, stop=True, skip_group_check=True)
                i.then_inc(s_o, 1)

        @block.scalar
        def _(act):
            for g, (b0, nb) in enumerate(groups):
                act.wait_ge(s_t, g + 1)
                nc.scalar.copy(turned[:, b0 * P:(b0 + nb) * P], p_t[g % 2][:, 0:nb, :].rearrange("p k n -> p (k n)")).then_inc(s_tc, 1)
            if layer == 0:
                act.wait_ge(s_w, 16 * loads)
                for g, (b0, nb) in enumerate(groups):
                    act.wait_ge(s_z, g + 1)
                    nc.scalar.activation(z[0:2 * D, b0 * P:(b0 + nb) * P], p_z[g % 2][:, 0:nb * P], ACT.Relu, bias=b1[:, :]).then_inc(s_zc, 1)
            act.wait_ge(s_std, 1)
            nc.scalar.sqrt(std[:, 2, :], std[:, 1, :]).then_inc(s_root, 1)

        @block.vector
        def _(dve):
            V = nc.vector
            at = [0]

            def link(i):
                at[0] += 1
                i.then_inc(s_v, 1)
                dve.wait_ge(s_v, at[0])

            if layer == 0:
                V.memset(z[2 * D:2 * D + 1, :], 1.0).then_inc(s_zero, 1)
            else:
                V.memset(w1[:, :], 0.0).then_inc(s_zero, 1)
            for h, (b0, nb) in enumerate(halves):
                dve.wait_ge(s_o, h + 1)
                b = slice(b0, b0 + nb)
                if layer == 0:
                    link(V.scalar_tensor_tensor(r[:, b, :], p_o[h][:, 0:nb, :], 0.0, x[:, b, :], ALU.max, ALU.add))
                else:
                    link(V.scalar_tensor_tensor(r[:, b, :], p_o[h][:, 0:nb, :], ALPHA_SELF, x[:, b, :], ALU.mult, ALU.add))
                    link(V.scalar_tensor_tensor(r[:, b, :], agg[:, b, 1:D + 1], ALPHA_MSG, r[:, b, :], ALU.mult, ALU.add))
            layernorm(dve, V, link, x, r, tmp, std, s_std, s_root)
            if layer == 0:
                link(V.tensor_copy(xp[:, :, 0, :], x[:, :, :]))
                link(V.tensor_tensor(r[:, :, :], x[:, :, :], xp[:, :, 0, :], ALU.subtract))
                link(V.tensor_copy(xp[:, :, 1, :], r[:, :, :]))
                link(V.tensor_tensor(xp[:, :, 2, :], r[:, :, :], xp[:, :, 1, :], ALU.subtract))
    clear(nc, used)


def layer1_edges_phase(nc, io, dram, keep):
    used = []
    ctx = ExitStack()
    with ctx:
        def sb(name, shape, dt=F32):
            return ctx.enter_context(nc.sbuf_tensor("m_" + name, shape, dt))

        def ps(name, shape, dt=F32):
            return ctx.enter_context(nc.psum_tensor("m_" + name, shape, dt))

        def sem(name):
            used.append(ctx.enter_context(nc.semaphore("m_" + name)))
            return used[-1]

        def counter(name):
            primed.append(Counter(sem(name)))
            return primed[-1]

        primed = []
        xp, agg, ident = keep["xp"], keep["agg"], keep["ident"]
        slots = range(U)
        table = sb("table", [1, BODIES, TAB], I32)
        starts = sb("starts", [1, S], I32)
        iota = sb("iota", [P, P])
        iotab = sb("iotab", [P, P], BF16)
        rt3 = sb("rt3", [P, G, 3])
        identb = sb("identb", [P, P], BF16)
        w1 = sb("w1", [6 * MUL, 2, H2])
        b1 = sb("b1", [2 * H2, 1])
        w2 = sb("w2", [H2, 2, H2])
        b2 = sb("b2", [2 * H2, 1])
        w3 = sb("w3", [H2, NTP])
        b3 = sb("b3", [3, NTP])
        w1_parts = sb("w1_parts", [6 * MUL, 3, 2 * H2], BF16)
        w2_parts = sb("w2_parts", [H2, 3, 2 * H2], BF16)
        w3_parts = sb("w3_parts", [H2, 3, NTP], BF16)
        b3_parts = sb("b3_parts", [3, 3, NTP], BF16)
        w1s = sb("w1s", [6 * MUL, 2 * H2], BF16)
        w2s = sb("w2s", [2 * H2, 2 * H2], BF16)
        w3s = sb("w3s", [2 * H2, NTP], BF16)
        b3s = sb("b3s", [3, NTP], BF16)
        ones3 = sb("ones3", [3, P], BF16)
        rec = in_turn(lambda s: sb(f"rec{s}", [P, G, REC]), U)
        oh = in_turn(lambda s: sb(f"oh{s}", [P, 2, G, P], BF16), U)
        attr = in_turn(lambda s: sb(f"attr{s}", [P, G, 6, MUL], BF16), 2)
        arest = in_turn(lambda s: sb(f"arest{s}", [P, G, MUL]), 2)
        recT = in_turn(lambda s: sb(f"recT{s}", [6 * MUL, G * P], BF16), 2)
        ohT = in_turn(lambda s: sb(f"ohT{s}", [P, G, P], BF16), 2)
        node = in_turn(lambda s: sb(f"node{s}", [P, G, D]), 4)
        h = [in_turn(lambda s: sb(f"h{k}_{s}", [2 * H2, G * P]), 2) for k in range(2)]
        hrest = [in_turn(lambda s: sb(f"hrest{k}_{s}", [2 * H2, G * P]), 2) for k in range(2)]
        hpart = [in_turn(lambda s: sb(f"hpart{k}_{s}", [2 * H2, 3, G * P], BF16), 2 + 2 * k) for k in range(2)]
        coef = in_turn(lambda s: sb(f"coef{s}", [P, G, 2 * MUL]), 4)
        sh3 = in_turn(lambda s: sb(f"sh3{s}", [P, G, 3]), 4)
        dots = in_turn(lambda s: sb(f"dots{s}", [P, G, MUL, 3]), 4)
        vec0 = in_turn(lambda s: sb(f"vec0{s}", [P, G, MUL, 3]), 4)
        prod0 = sb("prod0", [P, G, 2 * MUL, MUL])
        prod1 = sb("prod1", [P, 4, G, MUL, MUL])
        sum1 = sb("sum1", [P, 4, G, MUL])
        outer = sb("outer", [P, G, MUL, 3])
        msg = in_turn(lambda s: sb(f"msg{s}", [P, G, D]), 2)
        rest = in_turn(lambda s: sb(f"rest{s}", [P, G, D]), 2)
        part = in_turn(lambda s: sb(f"part{s}", [P, G, 3, D], BF16), 2)
        p_rec = ps("p_rec", [6 * MUL, G, P], BF16)
        p_oh = ps("p_oh", [P, G, P], BF16)
        p_node = ps("p_node", [P, G, D])
        p_h = [ps(f"p_h{k}", [2 * H2, G * P]) for k in range(2)]
        p_w = ps("p_w", [P, G, NTP])
        p_sum = ps("p_sum", [P, G, D])

        loaded = [sem(f"loaded{s}") for s in slots]
        d_start, d_const, setup, prime = sem("d_start"), sem("d_const"), sem("setup"), sem("prime")
        onehots, turned = counter("onehots"), counter("turned")
        recT_copied, ohT_copied = counter("recT_copied"), counter("ohT_copied")
        node_done, node_copied, made_coef = counter("node_done"), counter("node_copied"), counter("made_coef")
        attr_hi, attr_rest, attr_mid, attr_cut = counter("attr_hi"), counter("attr_rest"), counter("attr_mid"), counter("attr_cut")
        h_done, h_hi, h_rest, h_mid, h_cut = ([counter(f"{name}{k}") for k in range(2)] for name in ("h_done", "h_hi", "h_rest", "h_mid", "h_cut"))
        made_msg, msg_hi, msg_rest, msg_mid = counter("made_msg"), counter("msg_hi"), counter("msg_rest"), counter("msg_mid")
        w_done, w_read = counter("w_done"), counter("w_read")
        split, sum_done, sum_added = counter("split"), counter("sum_done"), counter("sum_added")
        dve_chain = [sem(f"dve_chain{i}") for i in range(12)]
        pool_chain = sem("pool_chain")
        w_chain, d_w = sem("w_chain"), sem("d_w")
        D_CONST = 16 * 21
        AHEAD = 6
        block = ctx.enter_context(nc.Block())
        ev = edges_of(dram)

        @block.sync
        def _(sp):
            for f in primed:
                sp.sem_inc(f.semaphore, U)
            sp.dma_start(table[:, :, :], dram["table"].unsqueeze(0)).then_inc(d_start, 16)
            sp.dma_start(starts[:, :], dram["starts"].unsqueeze(0)).then_inc(d_start, 16)
            sp.dma_start(iota[:, :], io["sort_consts"][:, 1, :]).then_inc(d_const, 16)
            for k in range(2):
                for i in range(6):
                    sp.dma_start(w1[MUL * i:MUL * i + MUL, k, :], io["L1_gnn_W1"]).then_inc(d_const, 16)
                sp.dma_start(b1[H2 * k:H2 * k + H2, :], io["L1_gnn_b1"].unsqueeze(1)).then_inc(d_const, 16)
                sp.dma_start(w2[:, k, :], io["L1_gnn_W2"]).then_inc(d_const, 16)
                sp.dma_start(b2[H2 * k:H2 * k + H2, :], io["L1_gnn_b2"].unsqueeze(1)).then_inc(d_const, 16)
            sp.dma_start(w3[:, :], io["L1_gnn_W3"]).then_inc(d_const, 16)
            sp.dma_start(b3[:, :], io["L1_gnn_b3"].unsqueeze(0).to_broadcast([3, NTP])).then_inc(d_const, 16)
            sp.wait_ge(w_chain, 16)
            for i, k in enumerate(MEETS):
                sp.dma_start(w1s[MUL * i:MUL * i + MUL, :], w1_parts[MUL * i:MUL * i + MUL, k, :]).then_inc(d_w, 16)
            for k in range(2):
                sp.dma_start(w2s[H2 * k:H2 * k + H2, :], w2_parts[:, k, :]).then_inc(d_w, 16)
                sp.dma_start(w3s[H2 * k:H2 * k + H2, :], w3_parts[:, k, :]).then_inc(d_w, 16)
            for k in range(3):
                sp.dma_start(b3s[k:k + 1, :], b3_parts[k:k + 1, k, :]).then_inc(d_w, 16)
            sp.wait_ge(d_start, 32)
            last = sp.value_load(starts[0:1, NB:NB + 1], min_val=NB, max_val=BODIES - U)
            with sp.Fori(1, round_end(last) + U, U) as n:
                for s in slots:
                    onehots.before(sp, n, s, U)
                    attr_rest.before(sp, n, s, U)
                    split.before(sp, n, s, U)
                    sp.dma_start(rec[s][:, :, :].rearrange("p t c -> p (t c)"),
                                 ev[bass.ds(body_of(nc, n, s), 1), :, (s % 2) * G * REC:(s % 2 + 1) * G * REC].rearrange("b p c -> p (b c)")
                                 ).then_inc(loaded[s], 16)
            for s in slots:
                sp.wait_ge(loaded[s], round_end(last) * 2 + 14)
                sp.sem_inc(prime, 1)

        @block.gpsimd
        def _(pool):
            g = nc.gpsimd
            pool.wait_ge(d_start, 32)
            pool.wait_ge(setup, 2)
            last = pool.value_load(starts[0:1, NB:NB + 1], min_val=NB, max_val=BODIES - U)

            def coefficients(n, s):
                node_copied.after(pool, n, s)
                pool.wait_ge(loaded[s], n * 2 + 14)
                w_read.before(pool, n, s, 4)
                pool.sem_inc(prime, 1)
                sh0, sh1 = rec[s][:, :, C4:C4 + 1], rec[s][:, :, C4 + 1:C4 + 4]
                vec = node[s][:, :, MUL:D].rearrange("p t (u i) -> p t u i", i=3)
                g.tensor_tensor(coef[s][:, :, 0:MUL], node[s][:, :, 0:MUL], sh0.to_broadcast([P, G, MUL]), ALU.mult)
                g.tensor_tensor(vec0[s][:, :, :, :].rearrange("p t u i -> p t (u i)"), node[s][:, :, MUL:D],
                                sh0.to_broadcast([P, G, 3 * MUL]), ALU.mult)
                g.tensor_tensor(sh3[s][:, :, :], sh1, rt3[:, :, :], ALU.mult).then_inc(pool_chain, 1)
                pool.wait_ge(pool_chain, n + s)
                made_coef.set_by(g.tensor_tensor(dots[s][:, :, :, :], vec, sh3[s][:, :, :].unsqueeze(2).to_broadcast([P, G, MUL, 3]), ALU.mult))

            def attributes_rest(n, s):
                attr_hi.after(pool, n, s)
                pool.sem_inc(prime, 1)
                attr_rest.set_by(g.tensor_tensor(arest[s][:, :, :], rec[s][:, :, C8:C8 + MUL], attr[s][:, :, 0, :], ALU.subtract))

            def attributes_low(n, s):
                attr_mid.after(pool, n, s)
                pool.sem_inc(prime, 1)
                attr_cut.set_by(g.tensor_tensor(attr[s][:, :, 5, :], arest[s][:, :, :], attr[s][:, :, 3, :], ALU.subtract))

            def hidden_rest_of(k, n, s):
                h_hi[k].after(pool, n, s)
                pool.sem_inc(prime, 1)
                h_rest[k].set_by(g.tensor_tensor(hrest[k][s][:, :], h[k][s][:, :], hpart[k][s][:, 0, :], ALU.subtract))

            hidden_rest = [lambda n, s, k=k: hidden_rest_of(k, n, s) for k in range(2)]

            def message_rest(n, s):
                msg_hi.after(pool, n, s)
                pool.sem_inc(prime, 1)
                msg_rest.set_by(g.tensor_tensor(rest[s][:, :, :], msg[s][:, :, :], part[s][:, :, 0, :], ALU.subtract))

            def message_low(n, s):
                msg_mid.after(pool, n, s)
                pool.sem_inc(prime, 1)
                split.set_by(g.tensor_tensor(part[s][:, :, 2, :], rest[s][:, :, :], part[s][:, :, 1, :], ALU.subtract))

            def hidden_low_of(k, n, s):
                h_mid[k].after(pool, n, s)
                pool.sem_inc(prime, 1)
                h_cut[k].set_by(g.tensor_tensor(hpart[k][s][0:H2, 2, :], hrest[k][s][0:H2, :], hpart[k][s][0:H2, 1, :], ALU.subtract))

            hidden_low = [lambda n, s, k=k: hidden_low_of(k, n, s) for k in range(2)]

            def work(n, j):
                staged(n, j, (message_rest, 0), (attributes_rest, 6), (message_low, 0), (attributes_low, 6), (coefficients, 2),
                       (hidden_rest[0], 4), (hidden_rest[1], 3), (hidden_low[0], 4), (hidden_low[1], 3))

            for j in range(-AHEAD, 0):
                work(1, j)
            with pool.Fori(1, round_end(last), U) as n:
                for j in slots:
                    work(n, j)

        @block.scalar
        def _(act):
            act.wait_ge(d_start, 32)
            last = act.value_load(starts[0:1, NB:NB + 1], min_val=NB, max_val=BODIES - U)
            act.wait_ge(d_const, D_CONST)

            def copies(n, s):
                turned.after(act, n, s)
                h_done[0].before(act, n, s, 2)
                node_done.before(act, n, s, 2)
                recT_copied.set_by(nc.scalar.copy(recT[s][:, :], p_rec[:, :, :].rearrange("p t e -> p (t e)")))
                ohT_copied.set_by(nc.scalar.copy(ohT[s][:, :, :], p_oh[:, :, :]))

            def attributes(n, s):
                act.wait_ge(loaded[s], n * 2 + 14)
                turned.before(act, n, s, 2)
                act.sem_inc(prime, 1)
                attr_hi.set_by(nc.scalar.copy(attr[s][:, :, 0:3, :], rec[s][:, :, C8:C8 + MUL].unsqueeze(2).to_broadcast([P, G, 3, MUL])))

            def attributes_mid(n, s):
                attr_rest.after(act, n, s)
                attr_mid.set_by(nc.scalar.copy(attr[s][:, :, 3:5, :], arest[s][:, :, :].unsqueeze(2).to_broadcast([P, G, 2, MUL])))

            def node_copy(n, s):
                node_done.after(act, n, s)
                w_read.before(act, n, s, 4)
                node_copied.set_by(nc.scalar.copy(node[s][:, :, :], p_node[:, :, :]))

            def silu_of(k, n, s):
                h_done[k].after(act, n, s)
                h_rest[k].before(act, n, s, 2)
                (h_done[1], w_done)[k].before(act, n, s, 2 + 2 * k)
                nc.scalar.activation(h[k][s][:, :], p_h[k][:, :], ACT.Silu, bias=(b1, b2)[k][:, :])
                h_hi[k].set_by(nc.scalar.activation(hpart[k][s][:, 0, :], p_h[k][:, :], ACT.Silu, bias=(b1, b2)[k][:, :]))

            silu = [lambda n, s, k=k: silu_of(k, n, s) for k in range(2)]

            def message_hi(n, s):
                made_msg.after(act, n, s)
                sum_done.before(act, n, s, 2)
                msg_hi.set_by(nc.scalar.copy(part[s][:, :, 0, :], msg[s][:, :, :]))

            def message_mid(n, s):
                msg_rest.after(act, n, s)
                msg_mid.set_by(nc.scalar.copy(part[s][:, :, 1, :], rest[s][:, :, :]))

            def silu_mid_of(k, n, s):
                h_rest[k].after(act, n, s)
                h_mid[k].set_by(nc.scalar.copy(hpart[k][s][:, 1, :], hrest[k][s][:, :]))

            silu_mid = [lambda n, s, k=k: silu_mid_of(k, n, s) for k in range(2)]

            def work(n, j):
                staged(n, j, (message_hi, 0), (attributes, 6), (message_mid, 0), (attributes_mid, 6),
                       (silu[0], 4), (silu[1], 3), (silu_mid[0], 4), (copies, 5), (silu_mid[1], 3), (node_copy, 3))

            act.wait_ge(setup, 2)
            for j in range(-AHEAD, 0):
                work(1, j)
            with act.Fori(1, round_end(last), U) as n:
                for j in slots:
                    work(n, j)

        @block.tensor
        def _(pe):
            mm = nc.tensor.matmul
            pe.wait_ge(d_start, 32)
            last = pe.value_load(starts[0:1, NB:NB + 1], min_val=NB, max_val=BODIES - U)
            pe.wait_ge(d_const, D_CONST)
            pe.wait_ge(d_w, 16 * 13)
            pe.wait_ge(setup, 2)

            def turn(n, s):
                attr_cut.after(pe, n, s)
                recT_copied.before(pe, n, s, 1)
                pe.sem_inc(prime, 1)
                for t in range(G):
                    nc.tensor.transpose(p_rec[:, t, :], attr[s][:, t, :, :].rearrange("p k f -> p (k f)"), identb[:, :])
                onehots.after(pe, n, s)
                ohT_copied.before(pe, n, s, 1)
                for t in range(G):
                    i = nc.tensor.transpose(p_oh[:, t, :], oh[s][:, 0, t, :], identb[:, :])
                turned.set_by(i)

            def gather(n, s):
                src, _ = blocks_of(nc, pe, table, n, s, targets=False)
                ohT_copied.after(pe, n, s)
                node_copied.before(pe, n, s, 1)
                for t in range(G):
                    for k in range(3):
                        i = mm(p_node[:, t, :], ohT[s][:, t, :], xp[:, bass.ds(src, 1), k, :], start=(k == 0), stop=(k == 2), skip_group_check=True)
                node_done.set_by(i)

            def first(n, s):
                recT_copied.after(pe, n, s)
                h_hi[0].before(pe, n, s, 1)
                pe.sem_inc(prime, 1)
                h_done[0].set_by(mm(p_h[0][:, :], w1s[:, :], recT[s][:, :], start=True, stop=True))

            def second(n, s):
                h_cut[0].after(pe, n, s)
                h_hi[1].before(pe, n, s, 1)
                pe.sem_inc(prime, 1)
                part = hpart[0][s]
                mm(p_h[1][:, :], w2s[:, :], part[:, 0, :], start=True, stop=False)
                mm(p_h[1][:, :], w2s[:, :], part[:, 1, :], start=False, stop=False)
                mm(p_h[1][:, :], w2_parts[:, 2, :], part[0:H2, 0, :], start=False, stop=False)
                h_done[1].set_by(mm(p_h[1][:, :], w2_parts[:, 0, :], part[0:H2, 2, :], start=False, stop=True))

            def third(n, s):
                h_cut[1].after(pe, n, s)
                w_read.before(pe, n, s, 1)
                part = hpart[1][s]
                pe.sem_inc(prime, 1)
                for t in range(0, G, 2):
                    mm(p_w[:, t:t + 2, :], ones3[:, :], b3s[:, :].unsqueeze(1).to_broadcast([3, 2, NTP]), start=True, stop=False, skip_group_check=True)
                for t in range(G):
                    e = slice(t * P, (t + 1) * P)
                    for k, (a, b) in enumerate(((part[:, 0, e], w3s[:, :]), (part[:, 1, e], w3s[:, :]),
                                 (part[0:H2, 0, e], w3_parts[:, 2, :]), (part[0:H2, 2, e], w3_parts[:, 0, :]))):
                        i = mm(p_w[:, t, :], a, b, start=False, stop=(t % 2 == 1 and k == 3), skip_group_check=True)
                w_done.set_by(i)

            def sums(n, s):
                split.after(pe, n, s)
                sum_added.before(pe, n, s, 1)
                for t in range(G):
                    for k in range(3):
                        i = mm(p_sum[:, t, :], oh[s][:, 1, t, :], part[s][:, t, k, :], start=(k == 0), stop=(k == 2), skip_group_check=True)
                sum_done.set_by(i)

            def work(n, j):
                staged(n, j, (third, 1), (first, 4), (second, 3), (gather, 3), (turn, 5), (sums, 0))

            for j in range(-AHEAD, 0):
                work(1, j)
            with pe.Fori(1, round_end(last), U) as n:
                for j in slots:
                    work(n, j)

        @block.vector
        def _(dve):
            V = nc.vector
            V.memset(ones3[:, :], 1.0).then_inc(setup, 1)
            V.memset(agg[:, :, 1:D + 1], 0.0)
            V.memset(rt3[:, :, :], RT3)
            dve.wait_ge(d_const, D_CONST)
            V.tensor_copy(iotab[:, :], iota[:, :])
            V.tensor_copy(identb[:, :], ident[:, :]).then_inc(setup, 1)
            for at, (whole, parts) in enumerate(((w1[:, :, :].rearrange("p k h -> p (k h)"), w1_parts), (w2[:, :, :].rearrange("p k h -> p (k h)"), w2_parts),
                                                 (w3[:, :], w3_parts), (b3[:, :], b3_parts))):
                cut_weights(dve, V, w_chain, whole, parts, 4 * at)
            dve.wait_ge(setup, 2)
            dve.wait_ge(d_start, 32)
            last = dve.value_load(starts[0:1, NB:NB + 1], min_val=NB, max_val=BODIES - U)
            MM = MUL * MUL

            def one_hots(n, s):
                dve.wait_ge(loaded[s], n * 2 + 14)
                sum_done.before(dve, n, s, U)
                for t in range(G):
                    for k, c in enumerate((CSRC, CDST)):
                        i = V.tensor_scalar(oh[s][:, k, t, :], iotab[:, :], rec[s][:, t, c:c + 1], None, ALU.is_equal)
                onehots.set_by(i)

            def products(n, s):
                link = Chain(dve, dve_chain, n, s).link
                made_coef.after(dve, n, s)
                link(V.tensor_reduce(coef[s][:, :, MUL:2 * MUL], dots[s][:, :, :, :], AX.X, ALU.add))
                w_done.after(dve, n, s)
                V.tensor_tensor(prod0[:, :, :, :], p_w[:, :, 0:2 * MM].rearrange("p t (u w) -> p t u w", w=MUL),
                                coef[s][:, :, :].unsqueeze(3).to_broadcast([P, G, 2 * MUL, MUL]), ALU.mult)
                V.tensor_tensor(prod1[:, 0, :, :, :], p_w[:, :, 2 * MM:3 * MM].rearrange("p t (u w) -> p t u w", w=MUL),
                                node[s][:, :, 0:MUL].unsqueeze(3).to_broadcast([P, G, MUL, MUL]), ALU.mult)
                for i in range(3):
                    last_op = V.tensor_tensor(prod1[:, 1 + i, :, :, :], p_w[:, :, 3 * MM:4 * MM].rearrange("p t (u w) -> p t u w", w=MUL),
                                              vec0[s][:, :, :, i].unsqueeze(3).to_broadcast([P, G, MUL, MUL]), ALU.mult)
                w_read.set_by(last_op)

            def messages(n, s):
                link = Chain(dve, dve_chain[1:], n, s).link
                w_read.after(dve, n, s)
                msg_rest.before(dve, n, s, 2)
                V.tensor_reduce(msg[s][:, :, 0:MUL], prod0[:, :, :, :].rearrange("p t u w -> p t w u"), AX.X, ALU.add)
                link(V.tensor_reduce(sum1[:, :, :, :].rearrange("p i t w -> p (i t) w"),
                                     prod1[:, :, :, :, :].rearrange("p i t u w -> p (i t) w u"), AX.X, ALU.add))
                link(V.tensor_tensor(outer[:, :, :, :], sum1[:, 0, :, :].unsqueeze(3).to_broadcast([P, G, MUL, 3]),
                                     rec[s][:, :, C4 + 1:C4 + 4].unsqueeze(2).to_broadcast([P, G, MUL, 3]), ALU.mult))
                made_msg.set_by(V.tensor_tensor(msg[s][:, :, MUL:D].rearrange("p t (w i) -> p t w i", i=3), outer[:, :, :, :],
                                                sum1[:, 1:4, :, :].rearrange("p i t w -> p t w i"), ALU.add))

            def add_sums(n, s, dsts):
                sum_done.after(dve, n, s)
                for t in range(G):
                    at = agg[:, bass.ds(dsts[t], 1), 1:D + 1].rearrange("p a c -> p (a c)")
                    i = V.tensor_tensor(at, p_sum[:, t, :], at, ALU.add)
                    if t < G - 1:
                        i.then_inc(dve_chain[9 + t], 1)
                        dve.wait_ge(dve_chain[9 + t], n + s)
                    else:
                        sum_added.set_by(i)
                        sum_added.after(dve, n, s)

            def work(n, j):
                staged(n, j, (products, 1), (one_hots, 6))
                if j >= 0:
                    _, dsts = blocks_of(nc, dve, table, *group(n, j), source=False)
                staged(n, j, (messages, 1))
                if j >= 0:
                    add_sums(*group(n, j), dsts)

            for j in range(-AHEAD, 0):
                work(1, j)
            with dve.Fori(1, round_end(last), U) as n:
                for j in slots:
                    work(n, j)
    clear(nc, used)


def degree_phase(nc, keep):
    used = []
    with ExitStack() as ctx:
        done = ctx.enter_context(nc.semaphore("d_done"))
        used.append(done)
        most = ctx.enter_context(nc.sbuf_tensor("d_most", [P, 2], F32))
        flag = ctx.enter_context(nc.sbuf_tensor("d_flag", [1, 5], F32))
        p_row = ctx.enter_context(nc.psum_tensor("d_p_row", [1, 2, P], F32))
        block = ctx.enter_context(nc.Block())

        @block.tensor
        def _(pe):
            pe.wait_ge(done, 1)
            for k in range(2):
                i = nc.tensor.matmul(p_row[:, k, :], most[:, k:k + 1], keep["ident"][:, :], start=True, stop=True)
            i.then_inc(done, 1)

        @block.vector
        def _(dve):
            V = nc.vector
            for k, c in enumerate((OUT_DEGREE, IN_DEGREE)):
                i = V.tensor_reduce(most[:, k:k + 1], keep["agg"][:, :, c], AX.X, ALU.max)
            i.then_inc(done, 1)
            dve.wait_ge(done, 2)
            V.tensor_reduce(flag[:, 0:2], p_row[:, :, :], AX.X, ALU.max).then_inc(done, 1)
            dve.wait_ge(done, 3)
            V.tensor_tensor(flag[:, 2:3], flag[:, 0:1], flag[:, 1:2], ALU.min).then_inc(done, 1)
            dve.wait_ge(done, 4)
            V.tensor_scalar(flag[:, 3:4], flag[:, 2:3], EXACT, None, ALU.is_gt)
            V.tensor_scalar(flag[:, 4:5], flag[:, 2:3], EXACT, None, ALU.is_le).then_inc(done, 1)
            dve.wait_ge(done, 5)
            V.tensor_copy(keep["large"][:, :], flag[:, 3:5])
    clear(nc, used)


def layer2_phase(nc, io, dram, keep):
    used = []
    ctx = ExitStack()
    with ctx:
        def sb(name, shape, dt=F32):
            return ctx.enter_context(nc.sbuf_tensor("q_" + name, shape, dt))

        def sem(name):
            used.append(ctx.enter_context(nc.semaphore("q_" + name)))
            return used[-1]

        def flags(name, n):
            made = [Flag(sem(f"{name}{i}")) for i in range(n)]
            primed.extend(made)
            return made

        primed = []
        x, agg, ident = keep["x"], keep["agg"], keep["ident"]
        CH = -(-NB // 4)
        width = [min(4, NB - 4 * c) for c in range(CH)]
        A = sb("A", [P, NB, NP], BF16)
        g3 = [sb(f"g3{k}", [P, NB, 3, D], BF16) for k in range(2)]
        sT = [sb(f"sT{k}", [3 * D, 4 * P]) for k in range(2)]
        s_ = sb("s_", [P, 4, D])
        gf = sb("gf", [P, 4, D])
        rest = sb("rest", [P, 4, D])
        h = sb("h", [P, NB, D])
        base = sb("base", [P, NB, D])
        norm = sb("norm", [P, 4, NB])
        std = sb("std", [P, 4, NB])
        p_s = [ctx.enter_context(nc.psum_tensor(f"q_p_s{k}", [3 * D, 512], F32)) for k in range(4)]
        p_t = [ctx.enter_context(nc.psum_tensor(f"q_p_t{k}", [P, 4, 3 * D], F32)) for k in range(2)]
        a_loaded = dram["a_loaded"]
        d_ready, rooted, s_v, started, s_std, s_root, s_credit = (sem("d_ready"), sem("rooted"), sem("v"), sem("started"),
                                                                  sem("std"), sem("root"), sem("credit"))
        U = 2
        summed, copied, turned, gathered = flags("summed", U * CH), flags("copied", U * CH), flags("turned", U * CH), flags("gathered", U * CH)
        dve_chain = [sem(f"chain{i}") for i in range(7)]
        block = ctx.enter_context(nc.Block())

        @block.gpsimd
        def _(pool):
            fits = pool.value_load(keep["large"][0:1, 1:2], min_val=0, max_val=1)
            with pool.If(fits):
                for b in range(NB):
                    pool.dma_start(A[:, b, :], dram["strips"][b, :, 0, :]).then_inc(a_loaded, 16)

        @block.sync
        def _(sp):
            fits = sp.value_load(keep["large"][0:1, 1:2], min_val=0, max_val=1)
            with sp.If(fits):
                for f in primed:
                    sp.sem_inc(f.semaphore, 1)

        @block.scalar
        def _(act):
            fits = act.value_load(keep["large"][0:1, 1:2], min_val=0, max_val=1)
            with act.If(fits):
                act.wait_ge(d_ready, 1)
                nc.scalar.sqrt(norm[:, 1, :], norm[:, 0, :]).then_inc(rooted, 1)
                with act.Fori(1, STEPS2 // U + 1) as n:
                    for u in range(U):
                        for c in range(CH):
                            i = u * CH + c
                            summed[i].after(act, n)
                            if i >= 2:
                                turned[i - 2].after(act, n)
                            else:
                                turned[U * CH - 2 + i].before(act, n)
                            copied[i].set_by(nc.scalar.copy(sT[i % 2][:, 0:width[c] * P], p_s[i % 4][:, 0:width[c] * P]))
                act.wait_ge(s_std, 1)
                nc.scalar.sqrt(std[:, 2, :], std[:, 1, :]).then_inc(s_root, 1)

        @block.tensor
        def _(pe):
            fits = pe.value_load(keep["large"][0:1, 1:2], min_val=0, max_val=1)
            with pe.If(fits):
                pe.wait_ge(started, 1)
                pe.wait_ge(a_loaded, 16 * NB)
                total = U * CH
                with pe.Fori(1, STEPS2 // U + 1) as n:
                    def turn(i):
                        c = i % CH
                        copied[i].after(pe, n)
                        if i >= 2:
                            gathered[i - 2].after(pe, n)
                        else:
                            gathered[total - 2 + i].before(pe, n)
                        for k in range(width[c]):
                            m = nc.tensor.transpose(p_t[i % 2][:, k, :], sT[i % 2][:, k * P:(k + 1) * P], ident[0:3 * D, 0:3 * D])
                        turned[i].set_by(m)

                    for u in range(U):
                        for c in range(CH):
                            i = u * CH + c
                            if i >= 4:
                                copied[i - 4].after(pe, n)
                            else:
                                last_use = [j for j in range(total) if j % 4 == i % 4][-1]
                                copied[last_use].before(pe, n)
                            for b in range(NB):
                                if c == 0 and b % 4 == 0:
                                    if u:
                                        gathered[b // 4].after(pe, n)
                                    else:
                                        gathered[CH + b // 4].before(pe, n)
                                m = nc.tensor.matmul(p_s[i % 4][:, 0:width[c] * P], g3[u][:, b, :, :], A[:, b, 4 * c * P:(4 * c + width[c]) * P],
                                                     start=(b == 0), stop=(b == NB - 1))
                            summed[i].set_by(m)
                            if c:
                                turn(i - 1)
                        turn(u * CH + CH - 1)

        @block.vector
        def _(dve):
            fits = dve.value_load(keep["large"][0:1, 1:2], min_val=0, max_val=1)
            with dve.If(fits):
                V = nc.vector
                at = [0]

                def link(i):
                    at[0] += 1
                    i.then_inc(s_v, 1)
                    dve.wait_ge(s_v, at[0])

                deg = agg[:, :, IN_DEGREE]
                wide = [P, NB, D]
                V.tensor_scalar(norm[:, 0, :], deg, 1.0, None, ALU.max).then_inc(d_ready, 1)
                link(V.tensor_scalar(norm[:, 3, :], deg, 0.0, None, ALU.is_gt))
                dve.wait_ge(rooted, 1)
                link(V.reciprocal(norm[:, 2, :], norm[:, 1, :]))
                link(V.tensor_tensor(norm[:, 1, :], norm[:, 2, :], norm[:, 3, :], ALU.mult))
                link(V.tensor_scalar(norm[:, 2, :], norm[:, 1, :], 1.0 - ALPHA2, None, ALU.mult))
                link(V.tensor_scalar(base[:, :, :], x[:, :, :], ALPHA2, None, ALU.mult))
                link(V.tensor_tensor(h[:, :, :], x[:, :, :], norm[:, 1, :].unsqueeze(2).to_broadcast(wide), ALU.mult))
                link(V.tensor_copy(g3[0][:, :, 0, :], h[:, :, :]))
                link(V.tensor_tensor(h[:, :, :], h[:, :, :], g3[0][:, :, 0, :], ALU.subtract))
                link(V.tensor_copy(g3[0][:, :, 1, :], h[:, :, :]))
                link(V.tensor_tensor(g3[0][:, :, 2, :], h[:, :, :], g3[0][:, :, 1, :], ALU.subtract))
                dve.sem_inc(started, 1)
                with dve.Fori(1, STEPS2 // U + 1) as n:
                    for u in range(U):
                        to = g3[1 - u]
                        for c in range(CH):
                            i = u * CH + c
                            w = width[c]
                            b = slice(4 * c, 4 * c + w)
                            wd = [P, w, D]

                            def chained(k, ins):
                                ins.then_inc(dve_chain[k], 1)
                                dve.wait_ge(dve_chain[k], (n - 1) * total + (i + 1))

                            total = U * CH
                            turned[i].after(dve, n)
                            chained(0, V.tensor_reduce(s_[:, 0:w, :], p_t[i % 2][:, 0:w, :].rearrange("p b (k f) -> p b f k", k=3), AX.X, ALU.add))
                            chained(1, V.tensor_tensor(gf[:, 0:w, :], s_[:, 0:w, :], norm[:, 2, b].unsqueeze(2).to_broadcast(wd), ALU.mult))
                            chained(2, V.tensor_tensor(h[:, b, :], gf[:, 0:w, :], base[:, b, :], ALU.add))
                            chained(3, V.tensor_tensor(gf[:, 0:w, :], h[:, b, :], norm[:, 1, b].unsqueeze(2).to_broadcast(wd), ALU.mult))
                            chained(4, V.tensor_copy(to[:, b, 0, :], gf[:, 0:w, :]))
                            chained(5, V.tensor_tensor(rest[:, 0:w, :], gf[:, 0:w, :], to[:, b, 0, :], ALU.subtract))
                            chained(6, V.tensor_copy(to[:, b, 1, :], rest[:, 0:w, :]))
                            gathered[i].set_by(V.tensor_tensor(to[:, b, 2, :], rest[:, 0:w, :], to[:, b, 1, :], ALU.subtract))
                gathered[U * CH - 1].after(dve, STEPS2 // U)
                link(V.tensor_tensor(h[:, :, :], x[:, :, :], h[:, :, :], ALU.add))
                layernorm(dve, V, link, x, h, base, std, s_std, s_root)
    clear(nc, used)


def layer2_large_phase(nc, io, dram, keep):
    used = []
    ctx = ExitStack()
    with ctx:
        def sb(name, shape, dt=F32):
            return ctx.enter_context(nc.sbuf_tensor("l_" + name, shape, dt))

        def sem(name):
            used.append(ctx.enter_context(nc.semaphore("l_" + name)))
            return used[-1]

        def flags(name, n):
            made = [Flag(sem(f"{name}{i}")) for i in range(n)]
            primed.extend(made)
            return made

        primed = []
        x, agg, ident = keep["x"], keep["agg"], keep["ident"]
        CH, SL = -(-NB // 4), 5
        width = [min(4, NB - 4 * c) for c in range(CH)]
        halves = ((0, 13), (13, NB - 13))
        A = [sb(f"A{k}", [P, NP]) for k in range(SL)]
        g = sb("g", [P, NB, D])
        sumT = sb("sumT", [D, NP])
        gf = sb("gf", [P, NB, D])
        h = sb("h", [P, NB, D])
        base = sb("base", [P, NB, D])
        norm = sb("norm", [P, 4, NB])
        std = sb("std", [P, 4, NB])
        p_s = [ctx.enter_context(nc.psum_tensor(f"l_p_s{c}", [D, 512], F32)) for c in range(CH)]
        p_t = ctx.enter_context(nc.psum_tensor("l_p_t", [P, 13, D], F32))
        arrived = [sem(f"arrived{k}") for k in range(SL)]
        passed = sem("passed")
        d_ready, rooted, s_v, started, s_std, s_root = sem("d_ready"), sem("rooted"), sem("v"), sem("started"), sem("std"), sem("root")
        used_up, copied, turned, gathered = flags("used_up", NB), flags("copied", 1), flags("turned", 2), flags("gathered", 2)
        dve_chain = [sem(f"chain{i}") for i in range(4)]
        block = ctx.enter_context(nc.Block())

        @block.sync
        def _(sp):
            large = sp.value_load(keep["large"][0:1, 0:1], min_val=0, max_val=1)
            with sp.If(large):
                for f in primed:
                    sp.sem_inc(f.semaphore, 1)
                with sp.Fori(1, STEPS2 + 1) as n:
                    for b in range(NB):
                        if b >= SL:
                            used_up[b - SL].after(sp, n)
                        else:
                            used_up[NB - SL + b].before(sp, n)
                        sp.dma_start(A[b % SL][:, :], dram["strips"][b, :, 0, :]).then_inc(arrived[b % SL], 16)

        @block.tensor
        def _(pe):
            large = pe.value_load(keep["large"][0:1, 0:1], min_val=0, max_val=1)
            with pe.If(large):
                pe.wait_ge(started, 1)
                with pe.Fori(1, STEPS2 + 1) as n:
                    gathered[1].before(pe, n)
                    copied[0].before(pe, n)
                    for b in range(NB):
                        pe.wait_ge(arrived[b % SL], (n - 1) * (16 * NB // SL) + 16 * (b // SL + 1))
                        for c in range(CH):
                            i = nc.tensor.matmul(p_s[c][:, 0:width[c] * P], g[:, b, :], A[b % SL][:, 4 * c * P:(4 * c + width[c]) * P],
                                                 start=(b == 0), stop=(b == NB - 1))
                        used_up[b].set_by(i)
                    copied[0].after(pe, n)
                    for k, (b0, nb) in enumerate(halves):
                        if k:
                            gathered[0].after(pe, n)
                        pe.sem_inc(passed, 1)
                        for b in range(nb):
                            i = nc.tensor.transpose(p_t[:, b, :], sumT[:, (b0 + b) * P:(b0 + b + 1) * P], ident[0:D, 0:D])
                        turned[k].set_by(i)

        @block.scalar
        def _(act):
            large = act.value_load(keep["large"][0:1, 0:1], min_val=0, max_val=1)
            with act.If(large):
                act.wait_ge(d_ready, 1)
                nc.scalar.sqrt(norm[:, 1, :], norm[:, 0, :]).then_inc(rooted, 1)
                with act.Fori(1, STEPS2 + 1) as n:
                    used_up[NB - 1].after(act, n)
                    for c in range(CH):
                        i = nc.scalar.copy(sumT[:, 4 * c * P:(4 * c + width[c]) * P], p_s[c][:, 0:width[c] * P])
                    copied[0].set_by(i)
                act.wait_ge(s_std, 1)
                nc.scalar.sqrt(std[:, 2, :], std[:, 1, :]).then_inc(s_root, 1)

        @block.vector
        def _(dve):
            large = dve.value_load(keep["large"][0:1, 0:1], min_val=0, max_val=1)
            with dve.If(large):
                V = nc.vector
                at = [0]

                def link(i):
                    at[0] += 1
                    i.then_inc(s_v, 1)
                    dve.wait_ge(s_v, at[0])

                deg = agg[:, :, IN_DEGREE]
                wide = [P, NB, D]
                V.tensor_scalar(norm[:, 0, :], deg, 1.0, None, ALU.max).then_inc(d_ready, 1)
                link(V.tensor_scalar(norm[:, 3, :], deg, 0.0, None, ALU.is_gt))
                dve.wait_ge(rooted, 1)
                link(V.reciprocal(norm[:, 2, :], norm[:, 1, :]))
                link(V.tensor_tensor(norm[:, 1, :], norm[:, 2, :], norm[:, 3, :], ALU.mult))
                link(V.tensor_scalar(norm[:, 2, :], norm[:, 1, :], 1.0 - ALPHA2, None, ALU.mult))
                link(V.tensor_scalar(base[:, :, :], x[:, :, :], ALPHA2, None, ALU.mult))
                link(V.tensor_tensor(g[:, :, :], x[:, :, :], norm[:, 1, :].unsqueeze(2).to_broadcast(wide), ALU.mult))
                dve.sem_inc(started, 1)
                with dve.Fori(1, STEPS2 + 1) as n:
                    for k, (b0, nb) in enumerate(halves):
                        b = slice(b0, b0 + nb)
                        wd = [P, nb, D]
                        turned[k].after(dve, n)
                        i = V.tensor_tensor(gf[:, b, :], p_t[:, 0:nb, :], norm[:, 2, b].unsqueeze(2).to_broadcast(wd), ALU.mult)
                        i.then_inc(dve_chain[2 * k], 1)
                        dve.wait_ge(dve_chain[2 * k], n)
                        V.tensor_tensor(h[:, b, :], gf[:, b, :], base[:, b, :], ALU.add).then_inc(dve_chain[2 * k + 1], 1)
                        dve.wait_ge(dve_chain[2 * k + 1], n)
                        gathered[k].set_by(V.tensor_tensor(g[:, b, :], h[:, b, :], norm[:, 1, b].unsqueeze(2).to_broadcast(wd), ALU.mult))
                gathered[1].after(dve, STEPS2)
                link(V.tensor_tensor(h[:, :, :], x[:, :, :], h[:, :, :], ALU.add))
                layernorm(dve, V, link, x, h, base, std, s_std, s_root)
    clear(nc, used)


def layer3_phase(nc, io, dram, keep, out):
    used = []
    ctx = ExitStack()
    with ctx:
        def sb(name, shape, dt=F32):
            return ctx.enter_context(nc.sbuf_tensor("r_" + name, shape, dt))

        def sem(name):
            used.append(ctx.enter_context(nc.semaphore("r_" + name)))
            return used[-1]

        def flags(name, n):
            made = [Flag(sem(f"{name}{i}")) for i in range(n)]
            primed.extend(made)
            return made

        primed = []
        x, ident = keep["x"], keep["ident"]
        CH = -(-NB // 4)
        width = [min(4, NB - 4 * c) for c in range(CH)]
        SL = 3
        W = [sb(f"W{k}", [P, 4, NB, P]) for k in range(SL)] + [sb(f"W{SL}", [P, width[-1], NB, P])]
        slot = [c % SL for c in range(CH - 1)] + [SL]
        loads = [slot.count(k) for k in range(SL + 1)]
        X = sb("X", [P, NB, D])
        Y = sb("Y", [P, NB, D])
        sT = [sb(f"sT{k}", [D, 4 * P]) for k in range(2)]
        std = sb("std", [P, 4, NB])
        p_o = [ctx.enter_context(nc.psum_tensor(f"r_p_o{k}", [D, 512], F32)) for k in range(3)]
        p_t = [ctx.enter_context(nc.psum_tensor(f"r_p_t{k}", [P, 4, D], F32)) for k in range(2)]
        arrived = [sem(f"arrived{k}") for k in range(SL + 1)]
        started, s_v, s_std, s_root, final, stored = sem("started"), sem("v"), sem("std"), sem("root"), sem("final"), sem("stored")
        summed, copied, turned, gathered = flags("summed", CH), flags("copied", CH), flags("turned", CH), flags("gathered", CH)
        renewed, passed = flags("renewed", 1)[0], sem("passed")
        block = ctx.enter_context(nc.Block())

        def last_user(engine, flag, turns, c, n):
            earlier = [j for j in range(CH) if turns[j] == turns[c] and j < c]
            if earlier:
                flag[earlier[-1]].after(engine, n)
            else:
                flag[[j for j in range(CH) if turns[j] == turns[c]][-1]].before(engine, n)

        two, three = [c % 2 for c in range(CH)], [c % 3 for c in range(CH)]

        @block.sync
        def _(sp):
            for f in primed:
                sp.sem_inc(f.semaphore, 1)
            with sp.Fori(1, STEPS3 + 1) as n:
                for c in range(CH):
                    last_user(sp, summed, slot, c, n)
                    sp.dma_start(W[slot[c]][:, :, :, :].rearrange("p b d k -> p b (d k)"),
                                 dram["strips"][4 * c:4 * c + width[c], :, 1, :].rearrange("b p x -> p b x")
                                 ).then_inc(arrived[slot[c]], 16)
            sp.wait_ge(final, 1)
            sp.dma_start(out[0:(NB - 1) * P, :].rearrange("(b p) f -> p b f", p=P), x[:, 0:NB - 1, :]).then_inc(stored, 16)
            sp.dma_start(out[(NB - 1) * P:N, :], x[0:LAST, NB - 1, :]).then_inc(stored, 16)
            sp.wait_ge(stored, 32)

        @block.tensor
        def _(pe):
            pe.wait_ge(started, 1)
            with pe.Fori(1, STEPS3 + 1) as n:
                def turn(c):
                    copied[c].after(pe, n)
                    last_user(pe, gathered, two, c, n)
                    pe.sem_inc(passed, 1)
                    for k in range(width[c]):
                        m = nc.tensor.transpose(p_t[c % 2][:, k, :], sT[c % 2][:, k * P:(k + 1) * P], ident[0:D, 0:D])
                    turned[c].set_by(m)

                renewed.before(pe, n)
                for c in range(CH):
                    pe.wait_ge(arrived[slot[c]], (n - 1) * (16 * loads[slot[c]]) + 16 * (slot[:c].count(slot[c]) + 1))
                    last_user(pe, copied, three, c, n)
                    for d in range(NB):
                        m = nc.tensor.matmul(p_o[c % 3][:, 0:width[c] * P], X[:, d, :],
                                             W[slot[c]][:, :, d, :], start=(d == 0), stop=(d == NB - 1))
                    summed[c].set_by(m)
                    if c:
                        turn(c - 1)
                turn(CH - 1)

        @block.scalar
        def _(act):
            with act.Fori(1, STEPS3 + 1) as n:
                for c in range(CH):
                    summed[c].after(act, n)
                    last_user(act, turned, two, c, n)
                    copied[c].set_by(nc.scalar.copy(sT[c % 2][:, 0:width[c] * P], p_o[c % 3][:, 0:width[c] * P]))
            act.wait_ge(s_std, 1)
            nc.scalar.sqrt(std[:, 2, :], std[:, 1, :]).then_inc(s_root, 1)

        @block.vector
        def _(dve):
            V = nc.vector
            at = [0]

            def link(i):
                at[0] += 1
                i.then_inc(s_v, 1)
                dve.wait_ge(s_v, at[0])

            V.tensor_copy(X[:, :, :], x[:, :, :]).then_inc(started, 1)
            with dve.Fori(1, STEPS3 + 1) as n:
                for c in range(CH):
                    turned[c].after(dve, n)
                    gathered[c].set_by(V.tensor_copy(Y[:, 4 * c:4 * c + width[c], :], p_t[c % 2][:, 0:width[c], :]))
                gathered[CH - 1].after(dve, n)
                renewed.set_by(V.tensor_copy(X[:, :, :], Y[:, :, :]))
            renewed.after(dve, STEPS3)
            link(V.tensor_tensor(Y[:, :, :], Y[:, :, :], x[:, :, :], ALU.add))
            layernorm(dve, V, link, x, Y, X, std, s_std, s_root)
            dve.sem_inc(final, 1)
    clear(nc, used)


def sort_constants(np):
    r = np.arange(P)
    j, s = r // S, r % S
    same = s[:, None] == s[None, :]
    before = (s[:, None] < s[None, :]) & (j[:, None] == 0)
    mats = [r[:, None] == r[None, :], np.broadcast_to(r, (P, P)), r[:, None] > r[None, :],
            same, same & (j[:, None] < j[None, :]), before]
    return np.ascontiguousarray(np.stack(mats, 1).astype(np.float32))


_INS = ["x", "src", "dst", "edge_attr_16", "edge_attr_4", "edge_attr_8", "edge_weight",
        "L0_gnn_W1f", "L0_gnn_b1f", "L0_gnn_W2f", "L0_gnn_b2f", "L0_gnn_W1b", "L0_gnn_b1b", "L0_gnn_W2b", "L0_gnn_b2b",
        "L0_gnn_W1n", "L0_gnn_b1n", "L0_gnn_W2n", "L0_gnn_b2n",
        "L1_gnn_W1", "L1_gnn_b1", "L1_gnn_W2", "L1_gnn_b2", "L1_gnn_W3", "L1_gnn_b3", "L1_gnn_Ws", "L1_gnn_Wv"]


def build(nc, io, out):
    dram = {
        "edges": nc.dram_tensor("sorted_edges", (ROWS, REC), F32, kind="Internal").ap(),
        "table": nc.dram_tensor("body_table", (BODIES, TAB), I32, kind="Internal").ap(),
        "starts": nc.dram_tensor("block_starts", (S,), I32, kind="Internal").ap(),
        "strips": nc.dram_tensor("dense_strips", (NB, P, 2, NP), F32, kind="Internal").ap(),
    }
    with ExitStack() as ctx:
        dram["sent"] = [ctx.enter_context(nc.semaphore(f"sent{k}")) for k in range(2)]
        dram["a_loaded"] = ctx.enter_context(nc.semaphore("a_loaded"))
        sort_phase(nc, io, dram, io["sort_consts"])
        with ExitStack() as inner:
            def sb(name, shape, dt=F32):
                return inner.enter_context(nc.sbuf_tensor(name, shape, dt))

            keep = {"x": sb("x", [P, NB, D]), "agg": sb("agg", [P, NB, 2 * D + 2]), "ident": sb("ident", [P, P])}
            with nc.sbuf_tensor("tab", [P, NB, 3, 4 * H1], BF16) as tab:
                keep["tab"] = tab
                load_nodes_phase(nc, io, keep)
                layer0_edges_phase(nc, io, dram, keep)
            with nc.sbuf_tensor("xp", [P, NB, 3, D], BF16) as xp:
                keep["xp"] = xp
                nodes_phase(nc, io, keep, 0)
                layer1_edges_phase(nc, io, dram, keep)
                nodes_phase(nc, io, keep, 1)
            keep["large"] = sb("large", [1, 2], I32)
            degree_phase(nc, keep)
            layer2_phase(nc, io, dram, keep)
            layer2_large_phase(nc, io, dram, keep)
            layer3_phase(nc, io, dram, keep, out)


def kernel(**inputs):
    import numpy as np
    import concourse.bacc as bacc
    from concourse.bass_utils import run_bass_kernel_spmd

    nc = bacc.Bacc("TRN2", target_bir_lowering=False, num_devices=1)
    arrays = {name: np.ascontiguousarray(inputs[name]) for name in _INS}
    arrays["sort_consts"] = sort_constants(np)
    arrays["iota_t"] = np.ascontiguousarray(np.broadcast_to(np.arange(BODIES * TB, dtype=np.float32), (P, BODIES * TB)))
    io = {name: nc.dram_tensor(f"in_{name}", a.shape, mybir.dt.from_np(a.dtype), kind="ExternalInput").ap()
          for name, a in arrays.items()}
    out = nc.dram_tensor("out", (N, D), F32, kind="ExternalOutput").ap()
    build(nc, io, out)
    r = run_bass_kernel_spmd(nc, [{f"in_{name}": a for name, a in arrays.items()}], core_ids=[0])
    return r.results[0]["out"]
```
